# Optimizing a Trainium2 kernel written in Bass

```python
import numpy as np
import jax
import jax.numpy as jnp

def _softmax(x, axis=-1):
    return jax.nn.softmax(x, axis=axis)

def _gelu(x):
    return jax.nn.gelu(x, approximate=True)

def _silu(x):
    return jax.nn.silu(x)

def _sigmoid(x):
    return jax.nn.sigmoid(x)

def _layernorm(x, axis=-1, eps=1e-05):
    m = jnp.mean(x, axis=axis, keepdims=True)
    v = jnp.var(x, axis=axis, keepdims=True)
    return (x - m) / jnp.sqrt(v + eps)

def _scatter_add(tgt, idx, src, axis=0):
    return tgt.at[idx].add(src)

def _segment_sum(src, seg, n):
    return jax.ops.segment_sum(src, seg, n)
kernel_name = 'mk_adj_ffn_d4_adj_r2_d42708'

def setup_inputs(seed: int=0):
    np.random.seed(seed)
    _w = jnp.asarray

    def _rec_inputs():
        import jax
        import jax.numpy as jnp
        _gk = jax.random.key(seed)
        x = -0.0002928 + 1 * jax.random.normal(jax.random.fold_in(_gk, 1), (1354, 256), jnp.float32)
        _w = (1.0 + jnp.arange(1354, dtype=jnp.float32)) ** (-0.5)
        _w = _w / _w.mean()
        _pij = jnp.clip(0.00295421 * _w[:, None] * _w[None, :], 0.0, 1.0)
        _a = jax.random.uniform(jax.random.fold_in(_gk, 2), (1354, 1354)) < _pij
        _a = jnp.logical_or(_a, jnp.eye(1354, dtype=bool))
        _af = _a.astype(jnp.float32)
        adj = _af
        return (x, adj)
    x, adj = _rec_inputs()

    def _L0_gnn_setup():
        import jax, jax.numpy as jnp
        import numpy as np
        N = 4096
        F_IN = 256
        F_OUT = 256
        DENSITY = 0.01
        key = jax.random.key(seed)
        k_x, k_adj, k_w, k_b = jax.random.split(key, 4)
        input_features = jax.random.normal(k_x, (N, F_IN), dtype=jnp.float32)
        adj = (jax.random.uniform(k_adj, (N, N)) < DENSITY).astype(jnp.float32)
        idx = jnp.arange(N)
        adj = adj.at[idx, idx].set(1.0)
        W = jax.random.normal(k_w, (F_IN, F_OUT), dtype=jnp.float32) / np.sqrt(F_IN)
        b = jax.random.normal(k_b, (F_OUT,), dtype=jnp.float32) * 0.01
        return {'input_features': input_features, 'adj': adj, 'W': W, 'b': b}
    _L0_gnn_all = _L0_gnn_setup()
    _L0_gnn_in = {k: v for k, v in _L0_gnn_all.items() if k in ('W', 'b')}
    del _L0_gnn_all

    def _L0_ffn_setup():
        import jax, jax.numpy as jnp
        import numpy as np
        MARK_AX = 0
        OP_AND = 1
        OP_OR = 2
        OP_XOR = 3
        ALU_LO = 16
        ALU_HI = 32
        AX_CARRY_LO = 48
        AX_CARRY_HI = 64
        OUTPUT_LO = 80
        OUTPUT_HI = 96
        NIB_A = 0
        NIB_B = 1
        OP_START = 16
        RESULT = 64
        GE_DIM = 160
        N_ROWS = 8
        B, S, D = (8, 2048, 256)

        def _decode_nibble(x_bd, start):
            bits = x_bd[..., start:start + 16] > 0.5
            return jnp.argmax(bits, axis=-1).astype(x_bd.dtype)

        def _mlp2(x, w1, b1, w2, b2):
            h = jax.nn.relu(jnp.einsum('bsrd,de->bsre', x, w1) + b1)
            return jnp.einsum('bsrd,de->bsre', h, w2) + b2

        def _forward(x_bd, and_w1, and_b1, and_w2, and_b2, or_w1, or_b1, or_w2, or_b2, xor_w1, xor_b1, xor_w2, xor_b2):
            a_lo = _decode_nibble(x_bd, ALU_LO)
            a_hi = _decode_nibble(x_bd, ALU_HI)
            b_lo = _decode_nibble(x_bd, AX_CARRY_LO)
            b_hi = _decode_nibble(x_bd, AX_CARRY_HI)
            Bsz, Ssz, _ = x_bd.shape
            x_ge = jnp.zeros((Bsz, Ssz, N_ROWS, GE_DIM), x_bd.dtype)
            x_ge = x_ge.at[..., 0, NIB_A].set(a_lo).at[..., 1, NIB_A].set(a_hi)
            x_ge = x_ge.at[..., 0, NIB_B].set(b_lo).at[..., 1, NIB_B].set(b_hi)
            x_ge = x_ge.at[..., :, OP_START + 28].set(x_bd[..., OP_OR, None])
            x_ge = x_ge.at[..., :, OP_START + 29].set(x_bd[..., OP_XOR, None])
            x_ge = x_ge.at[..., :, OP_START + 30].set(x_bd[..., OP_AND, None])
            y_and = _mlp2(x_ge, and_w1, and_b1, and_w2, and_b2)
            y_or = _mlp2(x_ge, or_w1, or_b1, or_w2, or_b2)
            y_xor = _mlp2(x_ge, xor_w1, xor_b1, xor_w2, xor_b2)
            is_and = x_bd[..., OP_AND] > 0.5
            is_or = x_bd[..., OP_OR] > 0.5
            is_xor = x_bd[..., OP_XOR] > 0.5
            sel = jnp.where(is_and[..., None, None], y_and, jnp.where(is_or[..., None, None], y_or, y_xor))
            active = (x_bd[..., MARK_AX] >= 0.5) & (is_and | is_or | is_xor)
            res_lo = jnp.clip(jnp.round(sel[..., 0, RESULT]), 0, 15).astype(jnp.int32)
            res_hi = jnp.clip(jnp.round(sel[..., 1, RESULT]), 0, 15).astype(jnp.int32)
            amask = active.astype(x_bd.dtype)[..., None]
            add_lo = 2.0 * jax.nn.one_hot(res_lo, 16, dtype=x_bd.dtype) * amask
            add_hi = 2.0 * jax.nn.one_hot(res_hi, 16, dtype=x_bd.dtype) * amask
            out = x_bd.at[..., OUTPUT_LO:OUTPUT_LO + 16].add(add_lo)
            out = out.at[..., OUTPUT_HI:OUTPUT_HI + 16].add(add_hi)
            return out
        key = jax.random.key(seed)
        ks = jax.random.split(key, 7)
        inp = {'x_bd': jax.random.uniform(ks[0], (B, S, D), dtype=jnp.float32)}
        for i, op in enumerate(['and', 'or', 'xor']):
            inp[op + '_w1'] = jax.random.normal(ks[1 + 2 * i], (GE_DIM, GE_DIM), jnp.float32) * 0.08
            inp[op + '_b1'] = jnp.zeros((GE_DIM,), jnp.float32)
            inp[op + '_w2'] = jax.random.normal(ks[2 + 2 * i], (GE_DIM, GE_DIM), jnp.float32) * 0.08
            inp[op + '_b2'] = jnp.zeros((GE_DIM,), jnp.float32)
        return inp
    _L0_ffn_all = _L0_ffn_setup()
    _L0_ffn_in = {k: v for k, v in _L0_ffn_all.items() if k in ('and_w1', 'and_b1', 'and_w2', 'and_b2', 'or_w1', 'or_b1', 'or_w2', 'or_b2', 'xor_w1', 'xor_b1', 'xor_w2', 'xor_b2')}
    del _L0_ffn_all

    def _L1_gnn_setup():
        import jax, jax.numpy as jnp
        import numpy as np
        N = 4096
        D_IN = 256
        D_OUT = 256
        NEG_BIG = -9000000000000000.0
        key = jax.random.key(seed)
        kx, ka, kw, kb, kn, ke = jax.random.split(key, 6)
        x = jax.random.normal(kx, (N, D_IN), dtype=jnp.float32)
        adj = (jax.random.uniform(ka, (N, N)) > 0.9).astype(jnp.float32)
        stdv = 1.0 / np.sqrt(D_OUT)
        weight = jax.random.uniform(kw, (D_IN, D_OUT), minval=-stdv, maxval=stdv, dtype=jnp.float32)
        bias = jax.random.uniform(kb, (D_OUT,), minval=-stdv, maxval=stdv, dtype=jnp.float32)
        node_w = jax.random.uniform(kn, (D_IN, 1), minval=-1.0, maxval=1.0, dtype=jnp.float32)
        stdv_e = 1.0 / np.sqrt(D_IN)
        edge_w = jax.random.uniform(ke, (D_IN, D_IN), minval=-stdv_e, maxval=stdv_e, dtype=jnp.float32)
        return {'x': x, 'adj': adj, 'weight': weight, 'bias': bias, 'node_w': node_w, 'edge_w': edge_w}
    _L1_gnn_all = _L1_gnn_setup()
    _L1_gnn_in = {k: v for k, v in _L1_gnn_all.items() if k in ('weight', 'bias', 'node_w', 'edge_w')}
    del _L1_gnn_all

    def _L1_ffn_setup():
        import jax, jax.numpy as jnp
        import numpy as np
        B, S, D, F, E, K = (64, 256, 256, 1024, 8, 2)
        key = jax.random.key(seed)
        k0, k1, k2, k3 = jax.random.split(key, 4)
        x = jax.random.normal(k0, (B, S, D), dtype=jnp.float32)
        Wr = jax.random.normal(k1, (D, E), dtype=jnp.float32) * D ** (-0.5)
        br = jnp.zeros((E,), dtype=jnp.float32)
        W1 = jax.random.normal(k2, (E, D, F), dtype=jnp.float32) * D ** (-0.5)
        b1 = jnp.zeros((E, F), dtype=jnp.float32)
        W2 = jax.random.normal(k3, (E, F, D), dtype=jnp.float32) * F ** (-0.5)
        b2 = jnp.zeros((E, D), dtype=jnp.float32)
        return {'x': x, 'Wr': Wr, 'br': br, 'W1': W1, 'b1': b1, 'W2': W2, 'b2': b2}
    _L1_ffn_all = _L1_ffn_setup()
    _L1_ffn_in = {k: v for k, v in _L1_ffn_all.items() if k in ('Wr', 'br', 'W1', 'b1', 'W2', 'b2')}
    del _L1_ffn_all

    def _L2_gnn_setup():
        import jax, jax.numpy as jnp
        import numpy as np
        IN_C, HID_C = (256, 256)
        ALPHA = 0.2
        N = 4096
        NEG_BIG = -9000000000000000.0
        key = jax.random.key(seed)
        k1, k2, k3, k4, k5, k6, k7 = jax.random.split(key, 7)
        h = jax.random.normal(k1, (N, IN_C), dtype=jnp.float32)
        adj = jax.random.randint(k2, (N, N), 0, 2).astype(jnp.float32)
        gain = np.sqrt(2.0 / (1.0 + ALPHA ** 2))
        lim_W = gain * np.sqrt(6.0 / (2 * IN_C + HID_C))
        W = jax.random.uniform(k3, (2 * IN_C, HID_C), jnp.float32, -lim_W, lim_W)
        lim_a = np.sqrt(1.0 / HID_C)
        a_w = jax.random.uniform(k4, (HID_C,), jnp.float32, -lim_a, lim_a)
        a_b = jax.random.uniform(k5, (), jnp.float32, -lim_a, lim_a)
        lim_fc = np.sqrt(1.0 / IN_C)
        fc_w = jax.random.uniform(k6, (IN_C, HID_C), jnp.float32, -lim_fc, lim_fc)
        fc_b = jax.random.uniform(k7, (HID_C,), jnp.float32, -lim_fc, lim_fc)
        return {'h': h, 'adj': adj, 'W': W, 'a_w': a_w, 'a_b': a_b, 'fc_w': fc_w, 'fc_b': fc_b}
    _L2_gnn_all = _L2_gnn_setup()
    _L2_gnn_in = {k: v for k, v in _L2_gnn_all.items() if k in ('W', 'a_w', 'a_b', 'fc_w', 'fc_b')}
    del _L2_gnn_all

    def _L2_ffn_setup():
        import jax, jax.numpy as jnp
        import numpy as np
        N_EXPERT = 8
        D_MODEL = 256
        D_HIDDEN = 512
        TOP_K = 2
        key = jax.random.key(seed)
        k_x, k_g, k_gu, k_d = jax.random.split(key, 4)
        b, t = (2, 512)
        s = 0.02
        x = jax.random.normal(k_x, (b, t, D_MODEL), dtype=jnp.float32)
        Wg = jax.random.normal(k_g, (D_MODEL, N_EXPERT), dtype=jnp.float32) * s
        Wgu = jax.random.normal(k_gu, (N_EXPERT, D_MODEL, 2 * D_HIDDEN), dtype=jnp.float32) * s
        bgu = jnp.zeros((N_EXPERT, 2 * D_HIDDEN), dtype=jnp.float32)
        Wd = jax.random.normal(k_d, (N_EXPERT, D_HIDDEN, D_MODEL), dtype=jnp.float32) * s
        bd = jnp.zeros((N_EXPERT, D_MODEL), dtype=jnp.float32)
        return {'x': x, 'Wg': Wg, 'Wgu': Wgu, 'bgu': bgu, 'Wd': Wd, 'bd': bd}
    _L2_ffn_all = _L2_ffn_setup()
    _L2_ffn_in = {k: v for k, v in _L2_ffn_all.items() if k in ('Wg', 'Wgu', 'bgu', 'Wd', 'bd')}
    del _L2_ffn_all

    def _L3_gnn_setup():
        import jax, jax.numpy as jnp
        import numpy as np
        N = 4096
        D = 256
        L = 2
        NEG_SLOPE = 0.01

        def _gat_layer(x, W, adj):
            proj = x @ W
            Wh, Ws = jnp.split(proj, 2, axis=-1)
            scores = Wh @ Ws.T
            a = jax.nn.softmax(scores, axis=-1) * adj
            out = a @ Wh
            out = out + x
            return jax.nn.leaky_relu(out, NEG_SLOPE)
        key = jax.random.key(seed)
        k1, k2, k3 = jax.random.split(key, 3)
        inputs = jax.random.normal(k1, (N, D), dtype=jnp.float32)
        adj = jax.random.randint(k2, (N, N), 0, 2).astype(jnp.float32)
        W_stack = jax.random.normal(k3, (L, D, 2 * D), dtype=jnp.float32) * (1.0 / np.sqrt(D))
        return {'inputs': inputs, 'adj': adj, 'W_stack': W_stack}
    _L3_gnn_all = _L3_gnn_setup()
    _L3_gnn_in = {k: v for k, v in _L3_gnn_all.items() if k in ('W_stack',)}
    del _L3_gnn_all

    def _L3_ffn_setup():
        import jax, jax.numpy as jnp
        import numpy as np
        B, T, C = (8, 512, 256)
        H = 512
        G, EG = (2, 4)
        E = G * EG
        K = 2
        LN_EPS = 1e-05

        def _swiglu(x):
            a, b = jnp.split(x, 2, axis=-1)
            return jax.nn.silu(a) * b
        key = jax.random.key(seed)
        ks = jax.random.split(key, 8)
        n = lambda k, shape, s: jax.random.normal(k, shape, dtype=jnp.float32) * s
        return {'x': n(ks[0], (B, T, C), 1.0), 'ln_scale': jnp.ones((C,), jnp.float32), 'ln_bias': jnp.zeros((C,), jnp.float32), 'shared_in_w': n(ks[1], (2 * H, C), 0.02), 'shared_out_w': n(ks[2], (C, H), 0.02), 'shared_out_b': jnp.zeros((C,), jnp.float32), 'expert_in_w': n(ks[3], (2 * H, C), 0.02), 'expert_out_weight': n(ks[4], (E, C, H), 0.02), 'expert_out_bias': jnp.zeros((E, C), jnp.float32), 'group_gate_w': n(ks[5], (G, C), 0.02), 'expert_gate_w': n(ks[6], (E, C), 0.02), 'group_bias': jnp.zeros((G,), jnp.float32), 'expert_bias': jnp.zeros((E,), jnp.float32)}
    _L3_ffn_all = _L3_ffn_setup()
    _L3_ffn_in = {k: v for k, v in _L3_ffn_all.items() if k in ('ln_scale', 'ln_bias', 'shared_in_w', 'shared_out_w', 'shared_out_b', 'expert_in_w', 'expert_out_weight', 'expert_out_bias', 'group_gate_w', 'expert_gate_w', 'group_bias', 'expert_bias')}
    del _L3_ffn_all
    return {'x': x, 'adj': adj, 'L0_gnn_W': _L0_gnn_in['W'], 'L0_gnn_b': _L0_gnn_in['b'], 'L0_ffn_and_w1': _L0_ffn_in['and_w1'], 'L0_ffn_and_b1': _L0_ffn_in['and_b1'], 'L0_ffn_and_w2': _L0_ffn_in['and_w2'], 'L0_ffn_and_b2': _L0_ffn_in['and_b2'], 'L0_ffn_or_w1': _L0_ffn_in['or_w1'], 'L0_ffn_or_b1': _L0_ffn_in['or_b1'], 'L0_ffn_or_w2': _L0_ffn_in['or_w2'], 'L0_ffn_or_b2': _L0_ffn_in['or_b2'], 'L0_ffn_xor_w1': _L0_ffn_in['xor_w1'], 'L0_ffn_xor_b1': _L0_ffn_in['xor_b1'], 'L0_ffn_xor_w2': _L0_ffn_in['xor_w2'], 'L0_ffn_xor_b2': _L0_ffn_in['xor_b2'], 'L1_gnn_weight': _L1_gnn_in['weight'], 'L1_gnn_bias': _L1_gnn_in['bias'], 'L1_gnn_node_w': _L1_gnn_in['node_w'], 'L1_gnn_edge_w': _L1_gnn_in['edge_w'], 'L1_ffn_Wr': _L1_ffn_in['Wr'], 'L1_ffn_br': _L1_ffn_in['br'], 'L1_ffn_W1': _L1_ffn_in['W1'], 'L1_ffn_b1': _L1_ffn_in['b1'], 'L1_ffn_W2': _L1_ffn_in['W2'], 'L1_ffn_b2': _L1_ffn_in['b2'], 'L2_gnn_W': _L2_gnn_in['W'], 'L2_gnn_a_w': _L2_gnn_in['a_w'], 'L2_gnn_a_b': _L2_gnn_in['a_b'], 'L2_gnn_fc_w': _L2_gnn_in['fc_w'], 'L2_gnn_fc_b': _L2_gnn_in['fc_b'], 'L2_ffn_Wg': _L2_ffn_in['Wg'], 'L2_ffn_Wgu': _L2_ffn_in['Wgu'], 'L2_ffn_bgu': _L2_ffn_in['bgu'], 'L2_ffn_Wd': _L2_ffn_in['Wd'], 'L2_ffn_bd': _L2_ffn_in['bd'], 'L3_gnn_W_stack': _L3_gnn_in['W_stack'], 'L3_ffn_ln_scale': _L3_ffn_in['ln_scale'], 'L3_ffn_ln_bias': _L3_ffn_in['ln_bias'], 'L3_ffn_shared_in_w': _L3_ffn_in['shared_in_w'], 'L3_ffn_shared_out_w': _L3_ffn_in['shared_out_w'], 'L3_ffn_shared_out_b': _L3_ffn_in['shared_out_b'], 'L3_ffn_expert_in_w': _L3_ffn_in['expert_in_w'], 'L3_ffn_expert_out_weight': _L3_ffn_in['expert_out_weight'], 'L3_ffn_expert_out_bias': _L3_ffn_in['expert_out_bias'], 'L3_ffn_group_gate_w': _L3_ffn_in['group_gate_w'], 'L3_ffn_expert_gate_w': _L3_ffn_in['expert_gate_w'], 'L3_ffn_group_bias': _L3_ffn_in['group_bias'], 'L3_ffn_expert_bias': _L3_ffn_in['expert_bias']}

def reference(x, adj, L0_gnn_W, L0_gnn_b, L0_ffn_and_w1, L0_ffn_and_b1, L0_ffn_and_w2, L0_ffn_and_b2, L0_ffn_or_w1, L0_ffn_or_b1, L0_ffn_or_w2, L0_ffn_or_b2, L0_ffn_xor_w1, L0_ffn_xor_b1, L0_ffn_xor_w2, L0_ffn_xor_b2, L1_gnn_weight, L1_gnn_bias, L1_gnn_node_w, L1_gnn_edge_w, L1_ffn_Wr, L1_ffn_br, L1_ffn_W1, L1_ffn_b1, L1_ffn_W2, L1_ffn_b2, L2_gnn_W, L2_gnn_a_w, L2_gnn_a_b, L2_gnn_fc_w, L2_gnn_fc_b, L2_ffn_Wg, L2_ffn_Wgu, L2_ffn_bgu, L2_ffn_Wd, L2_ffn_bd, L3_gnn_W_stack, L3_ffn_ln_scale, L3_ffn_ln_bias, L3_ffn_shared_in_w, L3_ffn_shared_out_w, L3_ffn_shared_out_b, L3_ffn_expert_in_w, L3_ffn_expert_out_weight, L3_ffn_expert_out_bias, L3_ffn_group_gate_w, L3_ffn_expert_gate_w, L3_ffn_group_bias, L3_ffn_expert_bias):
    import jax
    import jax.numpy as jnp

    def _L0_gnn_ref(input_features, adj, W, b):
        import jax, jax.numpy as jnp
        import numpy as np
        N = 4096
        F_IN = 256
        F_OUT = 256
        DENSITY = 0.01
        A = (adj != 0).astype(input_features.dtype)
        hidden = input_features @ W + b
        deg = jnp.sum(A, axis=0)
        return A @ hidden / deg[:, None]

    def _L0_ffn_ref(x_bd, and_w1, and_b1, and_w2, and_b2, or_w1, or_b1, or_w2, or_b2, xor_w1, xor_b1, xor_w2, xor_b2):
        import jax, jax.numpy as jnp
        import numpy as np
        MARK_AX = 0
        OP_AND = 1
        OP_OR = 2
        OP_XOR = 3
        ALU_LO = 16
        ALU_HI = 32
        AX_CARRY_LO = 48
        AX_CARRY_HI = 64
        OUTPUT_LO = 80
        OUTPUT_HI = 96
        NIB_A = 0
        NIB_B = 1
        OP_START = 16
        RESULT = 64
        GE_DIM = 160
        N_ROWS = 8
        B, S, D = (8, 2048, 256)

        def _decode_nibble(x_bd, start):
            bits = x_bd[..., start:start + 16] > 0.5
            return jnp.argmax(bits, axis=-1).astype(x_bd.dtype)

        def _mlp2(x, w1, b1, w2, b2):
            h = jax.nn.relu(jnp.einsum('bsrd,de->bsre', x, w1) + b1)
            return jnp.einsum('bsrd,de->bsre', h, w2) + b2

        def _forward(x_bd, and_w1, and_b1, and_w2, and_b2, or_w1, or_b1, or_w2, or_b2, xor_w1, xor_b1, xor_w2, xor_b2):
            a_lo = _decode_nibble(x_bd, ALU_LO)
            a_hi = _decode_nibble(x_bd, ALU_HI)
            b_lo = _decode_nibble(x_bd, AX_CARRY_LO)
            b_hi = _decode_nibble(x_bd, AX_CARRY_HI)
            Bsz, Ssz, _ = x_bd.shape
            x_ge = jnp.zeros((Bsz, Ssz, N_ROWS, GE_DIM), x_bd.dtype)
            x_ge = x_ge.at[..., 0, NIB_A].set(a_lo).at[..., 1, NIB_A].set(a_hi)
            x_ge = x_ge.at[..., 0, NIB_B].set(b_lo).at[..., 1, NIB_B].set(b_hi)
            x_ge = x_ge.at[..., :, OP_START + 28].set(x_bd[..., OP_OR, None])
            x_ge = x_ge.at[..., :, OP_START + 29].set(x_bd[..., OP_XOR, None])
            x_ge = x_ge.at[..., :, OP_START + 30].set(x_bd[..., OP_AND, None])
            y_and = _mlp2(x_ge, and_w1, and_b1, and_w2, and_b2)
            y_or = _mlp2(x_ge, or_w1, or_b1, or_w2, or_b2)
            y_xor = _mlp2(x_ge, xor_w1, xor_b1, xor_w2, xor_b2)
            is_and = x_bd[..., OP_AND] > 0.5
            is_or = x_bd[..., OP_OR] > 0.5
            is_xor = x_bd[..., OP_XOR] > 0.5
            sel = jnp.where(is_and[..., None, None], y_and, jnp.where(is_or[..., None, None], y_or, y_xor))
            active = (x_bd[..., MARK_AX] >= 0.5) & (is_and | is_or | is_xor)
            res_lo = jnp.clip(jnp.round(sel[..., 0, RESULT]), 0, 15).astype(jnp.int32)
            res_hi = jnp.clip(jnp.round(sel[..., 1, RESULT]), 0, 15).astype(jnp.int32)
            amask = active.astype(x_bd.dtype)[..., None]
            add_lo = 2.0 * jax.nn.one_hot(res_lo, 16, dtype=x_bd.dtype) * amask
            add_hi = 2.0 * jax.nn.one_hot(res_hi, 16, dtype=x_bd.dtype) * amask
            out = x_bd.at[..., OUTPUT_LO:OUTPUT_LO + 16].add(add_lo)
            out = out.at[..., OUTPUT_HI:OUTPUT_HI + 16].add(add_hi)
            return out
        return _forward(x_bd, and_w1, and_b1, and_w2, and_b2, or_w1, or_b1, or_w2, or_b2, xor_w1, xor_b1, xor_w2, xor_b2)

    def _L1_gnn_ref(x, adj, weight, bias, node_w, edge_w):
        import jax, jax.numpy as jnp
        import numpy as np
        N = 4096
        D_IN = 256
        D_OUT = 256
        NEG_BIG = -9000000000000000.0
        node_att = jax.nn.softmax(x @ node_w, axis=0)
        h = x @ edge_w
        e = h @ h.T
        e = jnp.where(adj > 0, e, NEG_BIG)
        edge_att = jax.nn.softmax(e, axis=1)
        combined_att = node_att * edge_att
        support = x @ weight
        output = adj * combined_att @ support
        return output + bias

    def _L1_ffn_ref(x, Wr, br, W1, b1, W2, b2):
        import jax, jax.numpy as jnp
        import numpy as np
        B, S, D, F, E, K = (64, 256, 256, 1024, 8, 2)
        orig_shape = x.shape
        t = x.reshape(-1, orig_shape[-1])
        logits = t @ Wr + br
        gates = jax.nn.softmax(logits, axis=-1)
        top_vals, top_idx = jax.lax.top_k(gates, K)
        top_vals = top_vals / top_vals.sum(axis=-1, keepdims=True)
        onehot = jax.nn.one_hot(top_idx, E, dtype=t.dtype)
        combine = jnp.einsum('tk,tke->te', top_vals, onehot)
        out = jnp.zeros_like(t)
        for e in range(E):
            h = jax.nn.relu(t @ W1[e] + b1[e])
            y = h @ W2[e] + b2[e]
            out = out + combine[:, e:e + 1] * y
        return out.reshape(orig_shape)

    def _L2_gnn_ref(h, adj, W, a_w, a_b, fc_w, fc_b):
        import jax, jax.numpy as jnp
        import numpy as np
        IN_C, HID_C = (256, 256)
        ALPHA = 0.2
        N = 4096
        NEG_BIG = -9000000000000000.0
        Wh1 = h @ W[:IN_C]
        Wh2 = h @ W[IN_C:]
        s1 = Wh1 @ a_w
        s2 = Wh2 @ a_w
        e = s1[:, None] + s2[None, :] + a_b
        e = jnp.where(e >= 0, e, ALPHA * e)
        e = jnp.where(adj > 0, e, NEG_BIG)
        att = jax.nn.softmax(e, axis=1)
        return att @ (h @ fc_w + fc_b)

    def _L2_ffn_ref(x, Wg, Wgu, bgu, Wd, bd):
        import jax, jax.numpy as jnp
        import numpy as np
        N_EXPERT = 8
        D_MODEL = 256
        D_HIDDEN = 512
        TOP_K = 2
        b, t, d = x.shape
        xf = x.reshape(-1, d)
        N = xf.shape[0]
        logits = xf @ Wg
        topw, topi = jax.lax.top_k(logits, TOP_K)
        topw = jax.nn.softmax(topw, axis=-1)
        comb = jnp.zeros((N, N_EXPERT), dtype=xf.dtype)
        comb = comb.at[jnp.arange(N)[:, None], topi].add(topw)
        gu = jnp.einsum('nd,edh->enh', xf, Wgu) + bgu[:, None, :]
        g, u = jnp.split(gu, 2, axis=-1)
        h = jax.nn.silu(g) * u
        eo = jnp.einsum('enh,ehd->end', h, Wd) + bd[:, None, :]
        out = jnp.einsum('end,ne->nd', eo, comb)
        return out.reshape(b, t, d)

    def _L3_gnn_ref(inputs, adj, W_stack):
        import jax, jax.numpy as jnp
        import numpy as np
        N = 4096
        D = 256
        L = 2
        NEG_SLOPE = 0.01

        def _gat_layer(x, W, adj):
            proj = x @ W
            Wh, Ws = jnp.split(proj, 2, axis=-1)
            scores = Wh @ Ws.T
            a = jax.nn.softmax(scores, axis=-1) * adj
            out = a @ Wh
            out = out + x
            return jax.nn.leaky_relu(out, NEG_SLOPE)
        x = inputs
        for l in range(W_stack.shape[0]):
            x = _gat_layer(x, W_stack[l], adj)
        return x

    def _L3_ffn_ref(x, ln_scale, ln_bias, shared_in_w, shared_out_w, shared_out_b, expert_in_w, expert_out_weight, expert_out_bias, group_gate_w, expert_gate_w, group_bias, expert_bias):
        import jax, jax.numpy as jnp
        import numpy as np
        B, T, C = (8, 512, 256)
        H = 512
        G, EG = (2, 4)
        E = G * EG
        K = 2
        LN_EPS = 1e-05

        def _swiglu(x):
            a, b = jnp.split(x, 2, axis=-1)
            return jax.nn.silu(a) * b
        Bx, Tx, Cx = x.shape
        S = Bx * Tx
        flat = x.reshape(S, Cx)
        mu = flat.mean(-1, keepdims=True)
        var = ((flat - mu) ** 2).mean(-1, keepdims=True)
        flat = (flat - mu) * jax.lax.rsqrt(var + LN_EPS) * ln_scale + ln_bias
        h_shared = _swiglu(flat @ shared_in_w.T)
        out_shared = h_shared @ shared_out_w.T + shared_out_b
        g_logits = flat @ group_gate_w.T + group_bias
        g_idx = jnp.argmax(g_logits, axis=-1)
        e_logits = (flat @ expert_gate_w.T).reshape(S, G, EG)
        e_sel = jnp.take_along_axis(e_logits, g_idx[:, None, None], axis=1)[:, 0, :]
        e_sel = e_sel + expert_bias.reshape(G, EG)[g_idx]
        e_probs = jax.nn.softmax(e_sel, axis=-1)
        topv, topi = jax.lax.top_k(e_probs, K)
        topv = topv / (topv.sum(-1, keepdims=True) + 1e-08)
        disp = g_idx[:, None] * EG + topi
        h_expert = _swiglu(flat @ expert_in_w.T)
        rows = jnp.arange(S)[:, None]
        comb = jnp.zeros((S, E), flat.dtype).at[rows, disp].add(topv)
        cnt = jnp.zeros((S, E), flat.dtype).at[rows, disp].add(1.0)
        routed = cnt @ expert_out_bias
        for e in range(E):
            routed = routed + comb[:, e:e + 1] * (h_expert @ expert_out_weight[e].T)
        return (out_shared + routed).reshape(Bx, Tx, Cx)
    x = x + _L0_gnn_ref(_layernorm(x, axis=-1), adj, L0_gnn_W, L0_gnn_b)
    x = x + _L0_ffn_ref(_layernorm(x, axis=-1)[None], L0_ffn_and_w1, L0_ffn_and_b1, L0_ffn_and_w2, L0_ffn_and_b2, L0_ffn_or_w1, L0_ffn_or_b1, L0_ffn_or_w2, L0_ffn_or_b2, L0_ffn_xor_w1, L0_ffn_xor_b1, L0_ffn_xor_w2, L0_ffn_xor_b2)[0]
    x = x + _L1_gnn_ref(_layernorm(x, axis=-1), adj, L1_gnn_weight, L1_gnn_bias, L1_gnn_node_w, L1_gnn_edge_w)
    x = x + _L1_ffn_ref(_layernorm(x, axis=-1)[None], L1_ffn_Wr, L1_ffn_br, L1_ffn_W1, L1_ffn_b1, L1_ffn_W2, L1_ffn_b2)[0]
    x = x + _L2_gnn_ref(_layernorm(x, axis=-1), adj, L2_gnn_W, L2_gnn_a_w, L2_gnn_a_b, L2_gnn_fc_w, L2_gnn_fc_b)
    x = x + _L2_ffn_ref(_layernorm(x, axis=-1)[None], L2_ffn_Wg, L2_ffn_Wgu, L2_ffn_bgu, L2_ffn_Wd, L2_ffn_bd)[0]
    x = x + _L3_gnn_ref(_layernorm(x, axis=-1), adj, L3_gnn_W_stack)
    x = x + _L3_ffn_ref(_layernorm(x, axis=-1)[None], L3_ffn_ln_scale, L3_ffn_ln_bias, L3_ffn_shared_in_w, L3_ffn_shared_out_w, L3_ffn_shared_out_b, L3_ffn_expert_in_w, L3_ffn_expert_out_weight, L3_ffn_expert_out_bias, L3_ffn_group_gate_w, L3_ffn_expert_gate_w, L3_ffn_group_bias, L3_ffn_expert_bias)[0]
    return x

_drawn_inputs = setup_inputs


def setup_inputs(seed=0):
    import zlib

    import numpy as np

    out = dict(_drawn_inputs(seed))
    spreads = {'L0_ffn_and_b1': (0.0, 0.8),
     'L0_ffn_and_b2': (0.0, 0.8),
     'L0_ffn_or_b1': (0.0, 0.8),
     'L0_ffn_or_b2': (0.0, 0.607),
     'L0_ffn_xor_b1': (0.0, 0.1),
     'L0_ffn_xor_b2': (0.0, 0.1),
     'L1_ffn_br': (0.0, 0.1),
     'L1_ffn_b1': (0.0, 0.315),
     'L1_ffn_b2': (0.0, 0.1),
     'L2_ffn_bgu': (0.0, 0.8),
     'L2_ffn_bd': (0.0, 0.1),
     'L3_ffn_ln_scale': (1.0, 0.6),
     'L3_ffn_ln_bias': (0.0, 0.596),
     'L3_ffn_shared_out_b': (0.0, 2.0),
     'L3_ffn_expert_out_bias': (0.0, 0.8),
     'L3_ffn_group_bias': (0.0, 0.439),
     'L3_ffn_expert_bias': (0.0, 0.331)}
    factors = {'L0_gnn_b': 3.663,
     'L0_ffn_and_w1': 7.035,
     'L0_ffn_and_w2': 7.183,
     'L0_ffn_or_w1': 3.648,
     'L0_ffn_or_w2': 6.462,
     'L0_ffn_xor_w2': 8.0,
     'L1_gnn_weight': 7.706,
     'L1_gnn_node_w': 8.0,
     'L2_gnn_fc_b': 2.888,
     'L2_ffn_Wgu': 6.148,
     'L2_ffn_Wd': 6.154,
     'L3_gnn_W_stack': 3.161,
     'L3_ffn_shared_in_w': 5.483,
     'L3_ffn_shared_out_w': 4.952,
     'L3_ffn_expert_in_w': 8.0,
     'L3_ffn_expert_out_weight': 8.0}
    for name, (base, spread) in spreads.items():
        noise = np.random.default_rng([zlib.crc32(name.encode()), seed]).standard_normal(out[name].shape)
        drawn = base * np.exp(spread * noise) if base else spread * noise
        out[name] = jnp.asarray(drawn.astype(out[name].dtype))
    for name, factor in factors.items():
        out[name] = (out[name] * factor).astype(out[name].dtype)
    return out
```

```python
from contextlib import ExitStack

import concourse.bass as bass
from concourse import mybir

F32, F32R, BF16 = mybir.dt.float32, mybir.dt.float32r, mybir.dt.bfloat16
I32, U32 = mybir.dt.int32, mybir.dt.uint32
ALU = mybir.AluOpType
ACT = mybir.ActivationFunctionType
AX = mybir.AxisListType

P = 128
N = 1354
D = 256
KD = D // P
TILES = -(-N // P)
LAST = N - (TILES - 1) * P
NP = TILES * P
BANK = 512
CHUNKS = [(a, min(BANK, N - a)) for a in range(0, N, BANK)]
PCHUNKS = [(a, min(BANK, NP - a)) for a in range(0, NP, BANK)]
GROUPS = [(a, min(4, TILES - a)) for a in range(0, TILES, 4)]
NG = len(GROUPS)
EPS = 1e-5
NEG_BIG = -9e15
LOWEST = -3e38
ROUND = 12582912.0
E = 8
SLOTS = (2 * N + E * (P - 1)) // P
LAG = 2
NPROB, NADJ, NPT, RING = 3, 3, 3, 4
GE = 160
STAGES = ("L0_gnn", "L0_ffn", "L1_gnn", "L1_ffn", "L2_gnn", "L2_ffn", "L3_gnn", "L3_ffn")


def build(nc, d, out, stages=STAGES):
    with ExitStack() as ctx:
        def sem(name):
            return ctx.enter_context(nc.semaphore(name))

        base = (nc.sbuf_base + 31) // 32 * 32
        top = nc.sbuf_usable_end

        class Area:

            def __init__(self, at):
                self.at = at

            def __call__(self, name, shape, dt=F32):
                words = 1
                for s in shape[1:]:
                    words *= s
                t = nc.alloc_sbuf_tensor_at(name, list(shape), dt, offset=self.at)
                self.at += (words * (2 if dt == BF16 else 4) + 31) // 32 * 32
                assert self.at <= top, (name, self.at, top)
                return t

        keep = Area(base)
        resid = keep("resid", [P, TILES, D])
        normed = keep("normed", [P, TILES, D])
        ident = keep("ident", [P, P])
        ones = keep("ones", [P, P])
        before = keep("before", [P, P])
        ones3 = keep("ones3", [3, P], BF16)
        valid = keep("valid", [P, TILES])
        invalid_bias = keep("invalid_bias", [P, TILES])
        stats = keep("stats", [P, TILES, 6])
        mean_var = keep("mean_var", [P, TILES, 2])
        var_eps = keep("var_eps", [P, TILES])
        std = keep("std", [P, TILES])
        rstd = keep("rstd", [P, TILES])
        chunk_max = keep("chunk_max", [P, TILES, NG])
        neg_max = keep("neg_max", [P, TILES])
        row_sum = keep("row_sum", [P, TILES])
        row_scale = keep("row_scale", [P, TILES])
        node_att = keep("node_att", [P, TILES])
        node_logit = keep("node_logit", [P, TILES])
        col = keep("col", [P, 4])
        deg_part = keep("deg_part", [P, TILES, 12])
        deg = keep("deg", [P, TILES])
        first = keep("first", [P, TILES, E])
        second = keep("second", [P, TILES, E])
        gate = keep("gate", [P, TILES, 2])
        rank_down = keep("rank_down", [P, TILES, E])
        router_sb = [keep(f"router_sb{i}", [P, TILES, E]) for i in range(3)]
        best = keep("best", [P, TILES, 4])
        pos = keep("pos", [P, 2, TILES])
        pos_u = keep("pos_u", [P, 2, TILES], U32)
        steps128 = keep("steps128", [P, E, TILES])
        step_gt = keep("step_gt", [P, E, TILES])
        expert_lt = keep("expert_lt", [P, E, E])
        lt_prod = keep("lt_prod", [P, E, E])
        per_expert = keep("per_expert", [P, 4, E])
        slot_iota = keep("slot_iota", [P, SLOTS, E])
        slot_ge = keep("slot_ge", [P, SLOTS, E])
        slot_f = keep("slot_f", [P, SLOTS])
        slot_expert = keep("slot_expert", [P, SLOTS], I32)
        nib_w = keep("nib_w", [64, 2 * GE + 2])
        slot_zero = keep("slot_zero", [P, D])
        shared_at = keep.at

        g = Area(shared_at)
        turned_hi = g("turned_hi", [P, KD, NP], F32R)
        turned_lo = g("turned_lo", [P, KD, NP], F32R)
        w_raw = g("w_raw", [P, KD, 2 * D + 2])
        w_hi = g("w_hi", [P, KD, 2 * D + 2], F32R)
        w_lo = g("w_lo", [P, KD, 2 * D + 2], F32R)
        values_hi = g("values_hi", [P, TILES, D], F32R)
        values_lo = g("values_lo", [P, TILES, D], F32R)
        q_hi = g("q_hi", [P, KD, NP], F32R)
        q_lo = g("q_lo", [P, KD, NP], F32R)
        probs = g("probs", [P, NPROB, NP])
        adj_rows = g("adj_rows", [P, NADJ, N])
        pt_hi = g("pt_hi", [P, NPT, BANK], F32R)
        pt_lo = g("pt_lo", [P, NPT, BANK], F32R)
        mask_bias = g("mask_bias", [P, 2, N], BF16)
        bias_row = g("bias_row", [P, D])
        biased = g("biased", [P, 2, D])
        k_at = g.at
        k_hi = g("k_hi", [P, KD, NP], F32R)
        k_lo = g("k_lo", [P, KD, NP], F32R)
        g2 = Area(k_at)
        unscaled = g2("unscaled", [P, TILES, D])
        g3 = Area(k_at)
        s2_row = g3("s2_row", [P, N])
        a_row = g3("a_row", [P, D])
        a_prod = g3("a_prod", [P, D])
        attn_w = g3("attn_w", [P, 2, KD])
        attn_raw = g3("attn_raw", [P, 2, KD, D])
        rep_hi = g3("rep_hi", [P, KD, P], F32R)
        rep_lo = g3("rep_lo", [P, KD, P], F32R)
        s1 = g3("s1", [P, TILES])
        s1_fifth = g3("s1_fifth", [P, TILES])
        ab = g3("ab", [P, 1])
        leaky = g3("leaky", [P, 2, N])

        n = Area(shared_at)
        bit_w = n("bit_w", [P, TILES, 64])
        bits = n("bits", [P, TILES, 64])
        nib_max = n("nib_max", [P, TILES, 4])
        nib_rev = n("nib_rev", [P, TILES, 4])
        nib = n("nib", [P, TILES, 4])
        opf = n("opf", [P, TILES, 3])
        opn = n("opn", [P, TILES, 2])
        sel = n("sel", [P, TILES, 3])
        active = n("active", [P, TILES, 3])
        feat6 = n("feat6", [P, 2, TILES, 6])
        feats = n("feats", [P, TILES, 64])
        feats_t = n("feats_t", [64, TILES, P])
        hidden = n("hidden", [P, 2, GE])
        nib_prod = n("nib_prod", [P, 2, GE])
        res_b = n("res_b", [P, TILES, 2])
        res = n("res", [P, TILES, 2])
        digit = n("digit", [P, 2 * TILES, 16])
        onehot = n("onehot", [P, 2 * TILES, 16])

        m = Area(shared_at)
        expert_w = m("expert_w", [P, E * 4096])
        bias3 = m("bias3", [3, E * 1280], BF16)
        m_at = m.at
        mturned_hi = m("mturned_hi", [P, KD, NP], F32R)
        mturned_lo = m("mturned_lo", [P, KD, NP], F32R)
        m2 = Area(m_at)
        slot_x = m2("slot_x", [P, 2, D])
        slot_xt = m2("slot_xt", [P, 2, KD, P])
        slot_h = m2("slot_h", [P, 2, 1024])
        slot_ht = m2("slot_ht", [P, 1024])
        slot_silu = m2("slot_silu", [P, BANK])
        slot_y = m2("slot_y", [P, 2, D])
        m3 = Area(max(m.at, m2.at))
        router_raw = m3("router_raw", [P, KD, E])
        router_hi = m3("router_hi", [P, KD, E], F32R)
        router_lo = m3("router_lo", [P, KD, E], F32R)
        router_b = m3("router_b", [P, E])
        split_f = m3("split_f", [80, 3, P])
        split_b = m3("split_b", [80, 3, P], BF16)
        m4 = Area(shared_at)
        gathered = m4("gathered", [P, TILES, 2, D])

        f = Area(shared_at)
        f_turned_hi = f("f_turned_hi", [P, KD, NP], F32R)
        f_turned_lo = f("f_turned_lo", [P, KD, NP], F32R)
        in_hi = f("in_hi", [P, 2, KD, 1024], F32R)
        in_lo = f("in_lo", [P, 2, KD, 1024], F32R)
        out_hi = f("out_hi", [P, 4, 9 * D], F32R)
        out_lo = f("out_lo", [P, 4, 9 * D], F32R)
        f2 = Area(f.at)
        nat_in = f2("nat_in", [P, 2, 8, D])
        f.at = f2.at
        nat_out = f("nat_out", [P, 2, KD, BANK])
        gate_nat = f("gate_nat", [E + 2, D])
        gate_hi = f("gate_hi", [P, KD, E + 2], F32R)
        gate_lo = f("gate_lo", [P, KD, E + 2], F32R)
        ln_rows = f("ln_rows", [P, 2, D])
        gate_b = f("gate_b", [P, E + 2])
        glog = f("glog", [P, TILES, E + 2])
        grp = f("grp", [P, TILES, 2])
        esel = f("esel", [P, 6, TILES, 4])
        pk = f("pk", [P, TILES, 4])
        comb = f("comb", [P, TILES, E])
        psel = f("psel", [P, 4, TILES])
        cnt = f("cnt", [P, TILES, E + 1])
        cnt_t = f("cnt_t", [E + 1, TILES, P])
        bias9 = f("bias9", [E + 1, D])
        f3 = Area(f2.at - 2 * 8 * D * 4)
        act_silu = f3("act_silu", [P, 2, BANK])
        act_h = f3("act_h", [P, 2, BANK])
        act_t_hi = f3("act_t_hi", [P, 2, BANK], F32R)
        act_t_lo = f3("act_t_lo", [P, 2, BANK], F32R)

        psum = ctx.enter_context(nc.psum_tensor("psum", [P, 8, BANK], F32))

        slots_in = nc.dram_tensor("slots_in", [SLOTS * P, D], F32).ap()
        slots_out = nc.dram_tensor("slots_out", [SLOTS * P, D], F32).ap()
        bias_scratch = nc.dram_tensor("bias_scratch", [3, E * 1280], BF16).ap()

        stage_done = sem("stage_done")
        vector_step = sem("vector_step")
        scalar_step = sem("scalar_step")
        pool_step = sem("pool_step")
        consts_ready = sem("consts_ready")
        x_loaded = sem("x_loaded")
        slots_cleared = sem("slots_cleared")
        out_stored = sem("out_stored")
        var_ready = sem("var_ready")
        std_ready = sem("std_ready")
        rows_normed = sem("rows_normed")
        block = ctx.enter_context(nc.Block())

        counts = {"v": 0, "s": 0, "p": 0, "norms": 0}

        def vstep(v, ins):
            counts["v"] += 1
            ins.then_inc(vector_step, 1)
            v.wait_ge(vector_step, counts["v"])

        def sstep(a, ins):
            counts["s"] += 1
            ins.then_inc(scalar_step, 1)
            a.wait_ge(scalar_step, counts["s"])

        def pstep(p, ins):
            counts["p"] += 1
            ins.then_inc(pool_step, 1)
            p.wait_ge(pool_step, counts["p"])

        def stage_end(eng, number):
            eng.drain().then_inc(stage_done, 1)
            eng.wait_ge(stage_done, 4 * number)

        def graph_items(layer):
            items = [("weights",)] + [("turn", i) for i in range(0, TILES, 2)]
            if layer in ("L1_gnn", "L3a", "L3b"):
                items += [("features", "q", mb, c) for c in range(3) for mb in range(KD)]
            if layer in ("L3a", "L3b"):
                items += [("features", "k", mb, c) for c in range(3) for mb in range(KD)]
            items += [("values", t) for t in range(TILES)]
            if layer == "L2_gnn":
                items += [("s2", c) for c in range(3)] + [("s1", 0)]
            return items

        graph_layers = [s for s in stages if s.endswith("gnn")]
        graph_layers = [x for s in graph_layers for x in (("L3a", "L3b") if s == "L3_gnn" else (s,))]
        moe_layers = [s for s in stages if s in ("L1_ffn", "L2_ffn")]
        w_cols = {"L0_gnn": D, "L1_gnn": 2 * D + 2, "L2_gnn": D, "L3a": 2 * D, "L3b": 2 * D}
        v_col = {"L0_gnn": 0, "L1_gnn": D, "L2_gnn": 0, "L3a": 0, "L3b": 0}

        class gs:
            w_loaded = sem("w_loaded")
            adj_loaded = [sem(f"adj_loaded{i}") for i in range(NADJ)]
            cleared = sem("cleared")
            item_ready = sem("item_ready")
            item_hi = sem("item_hi")
            item_done = sem("item_done")
            scores_ready = sem("scores_ready")
            scores_free = sem("scores_free")
            max_ready = sem("max_ready")
            exp_done = sem("exp_done")
            probs_ready = sem("probs_ready")
            adj_used = sem("adj_used")
            turned = sem("turned")
            pt_hi_ready = sem("pt_hi_ready")
            pt_ready = sem("pt_ready")
            pt_used = sem("pt_used")
            mixed_taken = sem("mixed_taken")
            node_max = sem("node_max")
            node_exp = sem("node_exp")
            node_sum = sem("node_sum")
            attn_split = sem("attn_split")
            biased_ready = sem("biased_ready")
            leaky_used = sem("leaky_used")
        w_dmas = {"L0_gnn": 2, "L1_gnn": 4, "L2_gnn": 5, "L3a": 1, "L3b": 1}

        def graph_counts(x):
            scored, items = x in ("L1_gnn", "L3a", "L3b"), len(graph_items(x))
            return dict(
                w_loaded=16 * w_dmas[x], cleared=1, item_ready=items - 1, item_hi=items, item_done=items,
                scores_ready=NG * TILES if scored else TILES if x == "L2_gnn" else 0,
                scores_free=NG * TILES if scored else 0, max_ready=TILES if x != "L0_gnn" else 0,
                exp_done=TILES if scored else 0, probs_ready=TILES, adj_used=TILES if x == "L2_gnn" else 0,
                turned=NG * TILES, pt_hi_ready=NG * TILES, pt_ready=NG * TILES, pt_used=NG * TILES,
                mixed_taken=TILES, node_max=2 if x == "L1_gnn" else 0, node_exp=1 if x == "L1_gnn" else 0,
                node_sum=1 if x == "L1_gnn" else 0, attn_split=KD if x == "L2_gnn" else 0,
                biased_ready=TILES if x in ("L0_gnn", "L2_gnn") else 0, leaky_used=TILES if x == "L2_gnn" else 0)

        gb = {}
        so_far, adj_so_far = {name: 0 for name in graph_counts("L0_gnn")}, [0] * NADJ
        for x in graph_layers:
            gb[x] = dict(adj_loaded=list(adj_so_far), **so_far)
            so_far = {name: so_far[name] + n_ for name, n_ in graph_counts(x).items()}
            adj_so_far = [adj_so_far[i] + 16 * len(range(i, TILES, NADJ)) for i in range(NADJ)]
        ml = {}
        for x in moe_layers:
            class sems:
                w_loaded = sem(f"{x}_w_loaded")
                r_loaded = sem(f"{x}_r_loaded")
                b_loaded = sem(f"{x}_b_loaded")
                b_split = sem(f"{x}_b_split")
                b_placed = sem(f"{x}_b_placed")
                b_spread = sem(f"{x}_b_spread")
                item_ready = sem(f"{x}_item_ready")
                item_hi = sem(f"{x}_item_hi")
                item_done = sem(f"{x}_item_done")
                logits = sem(f"{x}_logits")
                gap = sem(f"{x}_gap")
                gap_exp = sem(f"{x}_gap_exp")
                chosen = sem(f"{x}_chosen")
                counted = sem(f"{x}_counted")
                placed = sem(f"{x}_placed")
                sent = sem(f"{x}_sent")
                x_loaded = [sem(f"{x}_x_loaded{i}") for i in range(2)]
                x_turned = sem(f"{x}_x_turned")
                xt_ready = sem(f"{x}_xt_ready")
                h_ready = sem(f"{x}_h_ready")
                silu_ready = sem(f"{x}_silu_ready")
                silu_used = sem(f"{x}_silu_used")
                h_kept_s = sem(f"{x}_h_kept_s")
                h_kept_v = sem(f"{x}_h_kept_v")
                h_turned = sem(f"{x}_h_turned")
                ht_ready_s = sem(f"{x}_ht_ready_s")
                ht_ready_v = sem(f"{x}_ht_ready_v")
                y_ready = sem(f"{x}_y_ready")
                y_kept = sem(f"{x}_y_kept")
                y_stored = [sem(f"{x}_y_stored{i}") for i in range(2)]
            ml[x] = sems
        if moe_layers:
            gathered_ready = [sem(f"gathered_ready{t}") for t in range(TILES)]

        class ns:
            w_zeroed = sem("nib_w_zeroed")
            w_loaded = sem("nib_w_loaded")
            feats_ready = sem("nib_feats_ready")
            turned = sem("nib_turned")
            turned_kept = sem("nib_turned_kept")
            hidden = sem("nib_hidden")
            relu = sem("nib_relu")
            used = sem("nib_used")
            iota = sem("nib_iota")
        class fs:
            loaded = sem("f_loaded")
            in_loaded = [sem(f"f_in_loaded{i}") for i in range(2)]
            out_loaded = [sem(f"f_out_loaded{i}") for i in range(2)]
            item_ready = sem("f_item_ready")
            item_hi = sem("f_item_hi")
            item_done = sem("f_item_done")
            logits = sem("f_logits")
            exp_in = sem("f_exp_in")
            exp_out = sem("f_exp_out")
            cnt_ready = sem("f_cnt_ready")
            cnt_turned = sem("f_cnt_turned")
            cnt_kept = sem("f_cnt_kept")
            h_ready = sem("f_h_ready")
            silu = sem("f_silu")
            h_kept = sem("f_h_kept")
            h_turned = sem("f_h_turned")
            ht_hi = sem("f_ht_hi")
            ht_done = sem("f_ht_done")
            ht_used = sem("f_ht_used")
            y_ready = sem("f_y_ready")
            y_used = sem("f_y_used")

        def pairs(hi, lo):
            return lambda *ix: (hi[ix], lo[ix])

        def product(eng, o, lhs, rhs, start, stop):
            eng.matmul(o, lhs[0], rhs[0], start=start, stop=False)
            eng.matmul(o, lhs[0], rhs[1], start=False, stop=False)
            return eng.matmul(o, lhs[1], rhs[0], start=False, stop=stop)

        def norm_vector(v, src, index):
            for t in range(TILES):
                ins = v.bn_stats(stats[:, t, :], src[:, t, :])
            vstep(v, ins)
            for t in range(TILES):
                ins = v.bn_aggr(mean_var[:, t, :], stats[:, t, :])
            vstep(v, ins)
            v.tensor_scalar(var_eps[:], mean_var[:, :, 1], EPS, None, ALU.add).then_inc(var_ready, 1)
            v.wait_ge(std_ready, index + 1)
            vstep(v, v.reciprocal(rstd[:], std[:]))
            for t in range(TILES):
                v.tensor_scalar(normed[:, t, :], src[:, t, :], mean_var[:, t, 0:1], rstd[:, t:t + 1],
                                ALU.subtract, ALU.mult).then_inc(rows_normed, 1)

        def norm_scalar(a, index):
            a.wait_ge(var_ready, index + 1)
            a.activation(std[:], var_eps[:], ACT.Sqrt).then_inc(std_ready, 1)

        def ring_free(eng, done, k, start=0):
            if k >= RING:
                eng.wait_ge(done, start + k - RING + 1)

        def turn_tensor(pe, i, k, wait_rows):
            for j in range(min(2, TILES - i)):
                pe.wait_ge(rows_normed, wait_rows + i + j + 1)
                for kb in range(KD):
                    ins = pe.transpose(psum[:, k % RING, kb * 256 + j * P:kb * 256 + (j + 1) * P],
                                       normed[:, i + j, kb * P:(kb + 1) * P], ident[:])
            return ins

        def turn_source(i, k):
            w = min(2, TILES - i) * P
            return psum[:, k % RING, :].rearrange("p (k n) -> p k n", k=KD)[:, :, 0:w], slice(i * P, i * P + w)

        def graph_tensor(pe, x, rows_base):
            s, b, items = gs, gb[x], graph_items(x)
            where = {it: k for k, it in enumerate(items)}
            turned, w = pairs(turned_hi, turned_lo), pairs(w_hi, w_lo)
            for k, it in enumerate(items):
                if it[0] == "weights":
                    continue
                ring_free(pe, s.item_done, k, b["item_done"])
                if it[0] == "turn":
                    ins = turn_tensor(pe, it[1], k, rows_base)
                elif it[0] == "features":
                    _, dst, mb, c = it
                    a, width = PCHUNKS[c]
                    pe.wait_ge(s.item_done, b["item_done"] + where[("turn", min(4 * c + 2, (TILES - 1) // 2 * 2))] + 1)
                    off = (D if dst == "k" else 0) + mb * P
                    for kb in range(KD):
                        ins = product(pe, psum[:, k % RING, 0:width], w(slice(None), kb, slice(off, off + P)),
                                      turned(slice(None), kb, slice(a, a + width)), kb == 0, kb == KD - 1)
                elif it[0] == "values":
                    t = it[1]
                    pe.wait_ge(s.item_done, b["item_done"] + where[("turn", t // 2 * 2)] + 1)
                    width = D + 2 if x == "L1_gnn" else D
                    for kb in range(KD):
                        ins = product(pe, psum[:, k % RING, 0:width], turned(slice(None), kb, slice(t * P, t * P + P)),
                                      w(slice(None), kb, slice(v_col[x], v_col[x] + width)), kb == 0, kb == KD - 1)
                elif it[0] == "s2":
                    a, width = CHUNKS[it[1]]
                    pe.wait_ge(s.attn_split, b["attn_split"] + KD)
                    for kb in range(KD):
                        ins = product(pe, psum[:, k % RING, 0:width], pairs(rep_hi, rep_lo)(slice(None), kb, slice(None)),
                                      turned(slice(None), kb, slice(a, a + width)), kb == 0, kb == KD - 1)
                else:
                    for t in range(TILES):
                        for kb in range(KD):
                            for part in (turned_hi, turned_lo):
                                ins = pe.matmul(psum[:, k % RING, t:t + 1], part[:, kb, t * P:(t + 1) * P].bitcast(F32),
                                                attn_w[:, 0, kb:kb + 1],
                                                start=(kb == 0 and part is turned_hi), stop=(kb == 1 and part is turned_lo))
                ins.then_inc(s.item_ready, 1)
            pe.wait_ge(s.item_done, b["item_done"] + len(items))

            q = pairs(q_hi, q_lo)
            keys = pairs(k_hi, k_lo) if x in ("L3a", "L3b") else q
            scored = x in ("L1_gnn", "L3a", "L3b")
            pt, vals = pairs(pt_hi, pt_lo), pairs(values_hi, values_lo)

            def scores(r):
                for c, (a, width) in enumerate(CHUNKS):
                    n_ = r * NG + c
                    if n_ >= RING:
                        pe.wait_ge(s.scores_free, b["scores_free"] + n_ - RING + 1)
                    for kb in range(KD):
                        ins = product(pe, psum[:, n_ % RING, 0:width], q(slice(None), kb, slice(r * P, r * P + P)),
                                      keys(slice(None), kb, slice(a, a + width)), kb == 0, kb == KD - 1)
                    ins.then_inc(s.scores_ready, 1)

            def turn(r, c):
                n_ = r * NG + c
                if n_ >= 2:
                    pe.wait_ge(s.pt_ready, b["pt_ready"] + n_ - 1)
                a, w_ = GROUPS[c]
                for j in range(w_):
                    ins = pe.transpose(psum[:, 4 + n_ % 2, j * P:(j + 1) * P],
                                       probs[:, r % NPROB, (a + j) * P:(a + j + 1) * P], ident[:])
                ins.then_inc(s.turned, 1)

            def mix(r, c):
                n_ = r * NG + c
                pe.wait_ge(s.pt_ready, b["pt_ready"] + n_ + 1)
                a, w_ = GROUPS[c]
                o = psum[:, 6 + r % 2, 0:D]
                for j in range(w_):
                    l = pt(slice(None), n_ % NPT, slice(j * P, (j + 1) * P))
                    rr = vals(slice(None), a + j, slice(None))
                    st, sp = c == 0 and j == 0, c == NG - 1 and j == w_ - 1
                    if x == "L0_gnn":
                        pe.matmul(o, l[0], rr[0], start=st, stop=False)
                        ins = pe.matmul(o, l[0], rr[1], start=False, stop=sp)
                    else:
                        ins = product(pe, o, l, rr, st, sp)
                ins.then_inc(s.pt_used, 1)

            pe.wait_ge(s.cleared, b["cleared"] + 1)
            for i in range(TILES + LAG):
                r = i - LAG
                if r >= 0:
                    pe.wait_ge(s.probs_ready, b["probs_ready"] + r + 1)
                    turn(r, 0)
                    turn(r, 1)
                if i < TILES and scored:
                    scores(i)
                if r >= 0:
                    if r >= 2:
                        pe.wait_ge(s.mixed_taken, b["mixed_taken"] + r - 1)
                    mix(r, 0)
                    turn(r, 2)
                    mix(r, 1)
                    mix(r, 2)

        def graph_scalar(a, x):
            s, b, items = gs, gb[x], graph_items(x)
            n_pe = 0
            for k, it in enumerate(items):
                if it[0] == "weights":
                    a.wait_ge(s.w_loaded, b["w_loaded"] + 16 * w_dmas[x])
                    a.wait_ge(s.cleared, b["cleared"] + 1)
                    a.copy(w_hi[:, :, 0:w_cols[x]], w_raw[:, :, 0:w_cols[x]]).then_inc(s.item_hi, 1)
                    continue
                n_pe += 1
                a.wait_ge(s.item_ready, b["item_ready"] + n_pe)
                bank = psum[:, k % RING, :]
                if it[0] == "turn":
                    src, cols = turn_source(it[1], k)
                    ins = a.copy(turned_hi[:, :, cols], src)
                elif it[0] == "features":
                    _, dst, mb, c = it
                    at, width = PCHUNKS[c]
                    ins = a.copy((q_hi if dst == "q" else k_hi)[:, mb, at:at + width], bank[:, 0:width])
                elif it[0] == "values":
                    if x in ("L0_gnn", "L2_gnn"):
                        a.wait_ge(s.biased_ready, b["biased_ready"] + it[1] + 1)
                        ins = a.copy(values_hi[:, it[1], :], biased[:, it[1] % 2, :])
                    else:
                        ins = a.copy(values_hi[:, it[1], :], bank[:, 0:D])
                elif it[0] == "s2":
                    at, width = CHUNKS[it[1]]
                    ins = a.copy(s2_row[:, at:at + width], bank[:, 0:width])
                else:
                    ins = a.activation(s1[:], bank[:, 0:TILES], ACT.Identity, bias=ab[:, 0:1])
                ins.then_inc(s.item_hi, 1)
            if x == "L1_gnn":
                a.wait_ge(s.node_max, b["node_max"] + 2)
                a.activation(node_att[:], node_logit[:], ACT.Exp, bias=col[:, 1:2],
                             accum_out=col[:, 2:3]).then_inc(s.node_exp, 1)
            if x == "L2_gnn":
                a.wait_ge(s.item_done, b["item_done"] + len(items))

            def slope(r):
                if r >= 2:
                    a.wait_ge(s.leaky_used, b["leaky_used"] + r - 1)
                a.activation(leaky[:, r % 2, :], s2_row[:], ACT.Identity, bias=s1_fifth[:, r:r + 1],
                             scale=0.2).then_inc(s.scores_ready, 1)

            def exp(r):
                a.wait_ge(s.max_ready, b["max_ready"] + r + 1)
                a.activation(probs[:, r % NPROB, 0:N], probs[:, r % NPROB, 0:N], ACT.Exp, bias=neg_max[:, r:r + 1],
                             accum_out=row_sum[:, r:r + 1]).then_inc(s.exp_done if x != "L2_gnn" else s.probs_ready, 1)

            def hi(r, c):
                n_ = r * NG + c
                a.wait_ge(s.turned, b["turned"] + n_ + 1)
                if n_ >= NPT:
                    a.wait_ge(s.pt_used, b["pt_used"] + n_ - NPT + 1)
                w_ = GROUPS[c][1] * P
                a.copy(pt_hi[:, n_ % NPT, 0:w_], psum[:, 4 + n_ % 2, 0:w_]).then_inc(s.pt_hi_ready, 1)

            for i in range(TILES + LAG):
                if x == "L2_gnn" and i < TILES:
                    slope(i)
                if i >= LAG:
                    for c in range(NG):
                        hi(i - LAG, c)
                if x != "L0_gnn" and i < TILES:
                    exp(i)

        def graph_vector(v, x):
            s, b, items = gs, gb[x], graph_items(x)
            masked = x in ("L1_gnn", "L2_gnn")
            if x == "L2_gnn":
                v.wait_ge(s.w_loaded, b["w_loaded"] + 16 * w_dmas[x])
                for half in range(2):
                    for kb in range(KD):
                        vstep(v, v.tensor_tensor_reduce(a_prod[:], attn_raw[:, half, kb, :], a_row[:], 1.0, 0.0,
                                                        ALU.mult, ALU.add, attn_w[:, half, kb:kb + 1]))
                for kb in range(KD):
                    vstep(v, v.tensor_scalar(rep_hi[:, kb, :], ones[:], attn_w[:, 1, kb:kb + 1], None, ALU.mult))
                    v.scalar_tensor_tensor(rep_lo[:, kb, :], ones[:], attn_w[:, 1, kb:kb + 1],
                                           rep_hi[:, kb, :].bitcast(F32), ALU.mult, ALU.subtract).then_inc(s.attn_split, 1)
            n_pe = 0
            for k, it in enumerate(items):
                bank = psum[:, k % RING, :]
                n_pe += it[0] != "weights"
                if it[0] == "values" and x in ("L0_gnn", "L2_gnn"):
                    t = it[1]
                    v.wait_ge(s.w_loaded, b["w_loaded"] + 16 * w_dmas[x])
                    v.wait_ge(s.item_ready, b["item_ready"] + n_pe)
                    ins = v.tensor_tensor(biased[:, t % 2, :], bank[:, 0:D], bias_row[:], ALU.add)
                    ins.then_inc(s.biased_ready, 1)
                    v.wait_ge(s.item_hi, b["item_hi"] + k + 1)
                    v.tensor_tensor(values_lo[:, t, :], biased[:, t % 2, :], values_hi[:, t, :].bitcast(F32),
                                    ALU.subtract).then_inc(s.item_done, 1)
                    continue
                v.wait_ge(s.item_hi, b["item_hi"] + k + 1)
                if it[0] == "weights":
                    ins = v.tensor_tensor(w_lo[:, :, 0:w_cols[x]], w_raw[:, :, 0:w_cols[x]],
                                          w_hi[:, :, 0:w_cols[x]].bitcast(F32), ALU.subtract)
                elif it[0] == "turn":
                    src, cols = turn_source(it[1], k)
                    ins = v.tensor_tensor(turned_lo[:, :, cols], src, turned_hi[:, :, cols].bitcast(F32), ALU.subtract)
                elif it[0] == "features":
                    _, dst, mb, c = it
                    at, width = PCHUNKS[c]
                    h_, l_ = (q_hi, q_lo) if dst == "q" else (k_hi, k_lo)
                    ins = v.tensor_tensor(l_[:, mb, at:at + width], bank[:, 0:width],
                                          h_[:, mb, at:at + width].bitcast(F32), ALU.subtract)
                elif it[0] == "values":
                    t = it[1]
                    if x == "L1_gnn":
                        v.tensor_copy(node_logit[:, t:t + 1], bank[:, D:D + 1])
                    ins = v.tensor_tensor(values_lo[:, t, :], bank[:, 0:D], values_hi[:, t, :].bitcast(F32), ALU.subtract)
                elif it[0] == "s2":
                    ins = v.engine_nop()
                else:
                    ins = v.tensor_scalar(s1_fifth[:], s1[:], 0.2, None, ALU.mult)
                ins.then_inc(s.item_done, 1)
            v.wait_ge(s.item_done, b["item_done"] + len(items))
            if x == "L1_gnn":
                vstep(v, v.tensor_tensor(node_logit[:], node_logit[:], valid[:], ALU.mult))
                vstep(v, v.tensor_tensor(node_logit[:], node_logit[:], invalid_bias[:], ALU.add))
                v.tensor_reduce(col[:, 0:1], node_logit[:], AX.X, ALU.max).then_inc(s.node_max, 1)

            def front(r):
                pr, ad = probs[:, r % NPROB, 0:N], adj_rows[:, r % NADJ, :]
                if r >= NPROB:
                    v.wait_ge(s.turned, b["turned"] + (r - NPROB + 1) * NG)
                if x == "L0_gnn":
                    v.wait_ge(s.adj_loaded[r % NADJ], b["adj_loaded"][r % NADJ] + 16 * (r // NADJ + 1))
                    v.tensor_scalar(pr, ad, 0.0, None, ALU.not_equal).then_inc(s.probs_ready, 1)
                    return
                if masked:
                    v.wait_ge(s.adj_loaded[r % NADJ], b["adj_loaded"][r % NADJ] + 16 * (r // NADJ + 1))
                    mb = mask_bias[:, r % 2, :]
                    ins = v.tensor_scalar(mb, ad, 0.0, NEG_BIG, ALU.is_le, ALU.mult)
                    if x == "L2_gnn":
                        ins.then_inc(s.adj_used, 1)
                        v.wait_ge(s.adj_used, b["adj_used"] + r + 1)
                    else:
                        vstep(v, ins)
                if x == "L2_gnn":
                    v.wait_ge(s.scores_ready, b["scores_ready"] + r + 1)
                    ins = v.scalar_tensor_tensor(pr, s2_row[:], s1[:, r:r + 1], leaky[:, r % 2, :], ALU.add, ALU.max)
                    ins.then_inc(s.leaky_used, 1)
                    v.wait_ge(s.leaky_used, b["leaky_used"] + r + 1)
                    vstep(v, v.tensor_tensor_reduce(pr, pr, mb, 1.0, LOWEST, ALU.add, ALU.max, chunk_max[:, r, 0:1]))
                    v.tensor_scalar(neg_max[:, r:r + 1], chunk_max[:, r, 0:1], -1.0, None, ALU.mult).then_inc(s.max_ready, 1)
                    return
                for c, (at, width) in enumerate(CHUNKS):
                    n_ = r * NG + c
                    v.wait_ge(s.scores_ready, b["scores_ready"] + n_ + 1)
                    bank = psum[:, n_ % RING, 0:width]
                    if masked:
                        ins = v.tensor_tensor_reduce(pr[:, at:at + width], bank, mb[:, at:at + width], 1.0, LOWEST,
                                                     ALU.add, ALU.max, chunk_max[:, r, c:c + 1])
                    else:
                        ins = v.tensor_scalar(pr[:, at:at + width], bank, 1.0, None, ALU.mult, ALU.max,
                                              accum_out=chunk_max[:, r, c:c + 1])
                    ins.then_inc(s.scores_free, 1)
                v.wait_ge(s.scores_free, b["scores_free"] + (r + 1) * NG)
                v.tensor_reduce(neg_max[:, r:r + 1], chunk_max[:, r, :], AX.X, ALU.max, negate=True).then_inc(s.max_ready, 1)

            def lo(r, c):
                n_ = r * NG + c
                v.wait_ge(s.pt_hi_ready, b["pt_hi_ready"] + n_ + 1)
                a_, w_ = GROUPS[c]
                if x == "L0_gnn":
                    rows = LAST if r == TILES - 1 else P
                    v.tensor_reduce(deg_part[:, r, a_:a_ + w_],
                                    psum[:, 4 + n_ % 2, 0:w_ * P].rearrange("p (b n) -> p b n", n=P)[:, :, 0:rows],
                                    AX.X, ALU.add).then_inc(s.pt_ready, 1)
                else:
                    v.tensor_tensor(pt_lo[:, n_ % NPT, 0:w_ * P], psum[:, 4 + n_ % 2, 0:w_ * P],
                                    pt_hi[:, n_ % NPT, 0:w_ * P].bitcast(F32), ALU.subtract).then_inc(s.pt_ready, 1)

            def back(r):
                v.wait_ge(s.pt_used, b["pt_used"] + (r + 1) * NG)
                o = psum[:, 6 + r % 2, 0:D]
                if x == "L0_gnn":
                    v.tensor_copy(unscaled[:, r, :], o).then_inc(s.mixed_taken, 1)
                    return
                vstep(v, v.reciprocal(row_scale[:, r:r + 1], row_sum[:, r:r + 1]))
                if x == "L1_gnn":
                    vstep(v, v.tensor_tensor(row_scale[:, r:r + 1], row_scale[:, r:r + 1], node_att[:, r:r + 1], ALU.mult))
                if x in ("L1_gnn", "L2_gnn"):
                    v.scalar_tensor_tensor(resid[:, r, :], o, row_scale[:, r:r + 1], resid[:, r, :],
                                           ALU.mult, ALU.add).then_inc(s.mixed_taken, 1)
                else:
                    ins = v.scalar_tensor_tensor(normed[:, r, :], o, row_scale[:, r:r + 1], normed[:, r, :],
                                                 ALU.mult, ALU.add)
                    ins.then_inc(s.mixed_taken, 1)
                    v.wait_ge(s.mixed_taken, b["mixed_taken"] + r + 1)
                    v.scalar_tensor_tensor(normed[:, r, :], normed[:, r, :], 0.01, normed[:, r, :],
                                           ALU.mult, ALU.max).then_inc(rows_normed, 1)

            for i in range(TILES + LAG + 1):
                if i < TILES:
                    front(i)
                if x == "L1_gnn" and i == 1:
                    v.wait_ge(s.node_sum, b["node_sum"] + 1)
                    vstep(v, v.reciprocal(col[:, 3:4], col[:, 3:4]))
                    vstep(v, v.tensor_scalar(node_att[:], node_att[:], col[:, 3:4], None, ALU.mult))
                if LAG <= i < TILES + LAG:
                    for c in range(NG):
                        lo(i - LAG, c)
                if i > LAG:
                    back(i - LAG - 1)
            if x == "L0_gnn":
                v.wait_ge(s.pt_ready, b["pt_ready"] + TILES * NG)
                vstep(v, v.tensor_reduce(deg[:], deg_part[:, :, 0:TILES].rearrange("p r b -> p b r"), AX.X, ALU.add))
                vstep(v, v.scalar_tensor_tensor(deg[:], valid[:], -1.0, deg[:], ALU.mult, ALU.add))
                vstep(v, v.tensor_scalar(deg[:], deg[:], 1.0, None, ALU.add))
                vstep(v, v.reciprocal(row_scale[:], deg[:]))
                v.wait_ge(s.mixed_taken, b["mixed_taken"] + TILES)
                for t in range(TILES):
                    v.scalar_tensor_tensor(resid[:, t, :], unscaled[:, t, :], row_scale[:, t:t + 1], resid[:, t, :],
                                           ALU.mult, ALU.add)
            if x == "L3b":
                v.wait_ge(rows_normed, counts["rows_end_" + x])
                v.tensor_tensor(resid[:].rearrange("p t n -> p (t n)"), resid[:].rearrange("p t n -> p (t n)"),
                                normed[:].rearrange("p t n -> p (t n)"), ALU.add)

        def graph_pool(p, x):
            s, b = gs, gb[x]
            p.memset(w_raw[:, :, 2 * D:2 * D + 2] if x != "L1_gnn" else w_raw[:, :, 2 * D + 1:2 * D + 2], 0.0)
            p.memset(probs[:, :, N:NP], 0.0).then_inc(s.cleared, 1)
            if x == "L1_gnn":
                p.wait_ge(s.node_max, b["node_max"] + 1)
                pstep(p, p.partition_all_reduce(col[:, 1:2], col[:, 0:1], P, bass.bass_isa.ReduceOp.max))
                p.tensor_scalar(col[:, 1:2], col[:, 1:2], -1.0, 0.0, ALU.mult, ALU.add).then_inc(s.node_max, 1)
                p.wait_ge(s.w_loaded, b["w_loaded"] + 16 * w_dmas[x])
                for t in range(TILES):
                    ins = p.tensor_tensor(resid[:, t, :], resid[:, t, :], bias_row[:], ALU.add)
                p.wait_ge(s.node_exp, b["node_exp"] + 1)
                p.partition_all_reduce(col[:, 3:4], col[:, 2:3], P, bass.bass_isa.ReduceOp.add).then_inc(s.node_sum, 1)
            if x in ("L1_gnn", "L3a", "L3b"):
                for r in range(TILES):
                    p.wait_ge(s.exp_done, b["exp_done"] + r + 1)
                    p.wait_ge(s.adj_loaded[r % NADJ], b["adj_loaded"][r % NADJ] + 16 * (r // NADJ + 1))
                    ins = p.tensor_tensor(probs[:, r % NPROB, 0:N], probs[:, r % NPROB, 0:N], adj_rows[:, r % NADJ, :],
                                          ALU.mult)
                    ins.then_inc(s.probs_ready, 1)

        def load_weights(q, x):
            s, b = gs, gb[x]

            def put(dst, src):
                q.dma_start(dst, src).then_inc(s.w_loaded, 16)

            def rows(w):
                return w.rearrange("(k p) n -> p k n", p=P)

            def every(b):
                return b.rearrange("(o n) -> o n", o=1).to_broadcast([P, D])

            if x == "L0_gnn":
                put(w_raw[:, :, 0:D], rows(d["L0_gnn_W"]))
                put(bias_row[:], every(d["L0_gnn_b"]))
            elif x == "L1_gnn":
                put(w_raw[:, :, 0:D], rows(d["L1_gnn_edge_w"]))
                put(w_raw[:, :, D:2 * D], rows(d["L1_gnn_weight"]))
                with nc.allow_non_contiguous_dma(reason="one column of 256 numbers"):
                    put(w_raw[:, :, 2 * D:2 * D + 1], rows(d["L1_gnn_node_w"]))
                put(bias_row[:], every(d["L1_gnn_bias"]))
            elif x == "L2_gnn":
                put(w_raw[:, :, 0:D], rows(d["L2_gnn_fc_w"]))
                put(attn_raw[:], d["L2_gnn_W"].rearrange("(h k p) n -> p h k n", h=2, p=P))
                put(bias_row[:], every(d["L2_gnn_fc_b"]))
                put(a_row[:], every(d["L2_gnn_a_w"]))
                put(ab[:], d["L2_gnn_a_b"].to_broadcast([P, 1]))
            else:
                put(w_raw[:, :, 0:2 * D], rows(d["L3_gnn_W_stack"][0 if x == "L3a" else 1]))

        def load_adjacency(q, x):
            s, b = gs, gb[x]
            for r in range(TILES):
                if r >= NADJ:
                    if x == "L2_gnn":
                        q.wait_ge(s.adj_used, b["adj_used"] + r - NADJ + 1)
                    else:
                        q.wait_ge(s.probs_ready, b["probs_ready"] + r - NADJ + 1)
                rows = LAST if r == TILES - 1 else P
                q.dma_start(adj_rows[0:rows, r % NADJ, :], d["adj"][r * P:r * P + rows, :]).then_inc(
                    s.adj_loaded[r % NADJ], 16)

        def load_nibble_weights(q):
            q.wait_ge(ns.w_zeroed, 1)
            for o, op in enumerate(("and", "or", "xor")):
                w1, b1 = d[f"L0_ffn_{op}_w1"], d[f"L0_ffn_{op}_b1"]
                w2, b2 = d[f"L0_ffn_{op}_w2"], d[f"L0_ffn_{op}_b2"]
                r = 6 * o
                with nc.allow_non_contiguous_dma(reason="one column of the second layer"):
                    for dst, src in ((nib_w[r:r + 2, 0:GE], w1[0:2, :]), (nib_w[r + 2:r + 5, 0:GE], w1[44:47, :]),
                                     (nib_w[r + 5:r + 6, 0:GE], b1.rearrange("(o n) -> o n", o=1)),
                                     (nib_w[r + 5:r + 6, GE:2 * GE], w2[:, 64:65].rearrange("n o -> o n")),
                                     (nib_w[r + 5:r + 6, 2 * GE:2 * GE + 1], b2.rearrange("(o n) -> o n", o=1)[:, 64:65])):
                        q.dma_start(dst, src).then_inc(ns.w_loaded, 16)
            q.wait_ge(ns.w_loaded, 16 * 15)
            q.dma_start(nib_w[32:50, :], nib_w[0:18, :]).then_inc(ns.w_loaded, 16)

        NIB_BANKS = 4

        def nibble_pool(p):
            p.iota(bit_w[:].rearrange("p t (k j) -> p t k j", j=16), pattern=[[0, TILES], [0, 4], [-1, 16]], base=16,
                   channel_multiplier=0, allow_small_or_imprecise_dtypes=True)
            p.iota(digit[:], pattern=[[0, 2 * TILES], [1, 16]], base=0, channel_multiplier=0,
                   allow_small_or_imprecise_dtypes=True)
            p.memset(feats[:], 0.0).then_inc(ns.iota, 1)

        def nibble_vector(v, rows_base):
            v.wait_ge(ns.iota, 1)
            v.wait_ge(rows_normed, rows_base + TILES)
            vstep(v, v.scalar_tensor_tensor(bits[:], normed[:, :, 16:80], 0.5, bit_w[:], ALU.is_gt, ALU.mult))
            vstep(v, v.tensor_reduce(nib_max[:].rearrange("p t k -> p (t k)"),
                                     bits[:].rearrange("p t (k j) -> p (t k) j", j=16), AX.X, ALU.max))
            vstep(v, v.tensor_scalar(nib_rev[:], nib_max[:], -1.0, 16.0, ALU.mult, ALU.add))
            v.scalar_tensor_tensor(nib[:], nib_max[:], 0.0, nib_rev[:], ALU.is_gt, ALU.mult)
            vstep(v, v.tensor_scalar(opf[:], normed[:, :, 1:4], 0.5, None, ALU.is_gt))
            vstep(v, v.tensor_scalar(opn[:], opf[:, :, 0:2], -1.0, 1.0, ALU.mult, ALU.add))
            v.tensor_copy(sel[:, :, 0:1], opf[:, :, 0:1])
            v.tensor_tensor(sel[:, :, 1:2], opf[:, :, 1:2], opn[:, :, 0:1], ALU.mult)
            v.tensor_tensor(sel[:, :, 2:3], opn[:, :, 0:1], opn[:, :, 1:2], ALU.mult)
            vstep(v, v.tensor_tensor(active[:, :, 0:1], opf[:, :, 0:1], opf[:, :, 1:2], ALU.max))
            vstep(v, v.tensor_tensor(active[:, :, 1:2], active[:, :, 0:1], opf[:, :, 2:3], ALU.max))
            vstep(v, v.scalar_tensor_tensor(active[:, :, 2:3], normed[:, :, 0:1], 0.5, active[:, :, 1:2],
                                            ALU.is_ge, ALU.mult))
            vstep(v, v.tensor_scalar(active[:, :, 0:1], active[:, :, 2:3], 2.0, None, ALU.mult))
            for row in range(2):
                v.tensor_copy(feat6[:, row, :, 0:1], nib[:, :, row:row + 1])
                v.tensor_copy(feat6[:, row, :, 1:2], nib[:, :, 2 + row:3 + row])
                v.tensor_copy(feat6[:, row, :, 2:4], normed[:, :, 2:4])
                v.tensor_copy(feat6[:, row, :, 4:5], normed[:, :, 1:2])
                ins = v.memset(feat6[:, row, :, 5:6], 1.0)
            vstep(v, ins)
            for row in range(2):
                for o in range(3):
                    at = 32 * row + 6 * o
                    ins = v.tensor_tensor(feats[:, :, at:at + 6], feat6[:, row, :, :],
                                          sel[:, :, o:o + 1].to_broadcast([P, TILES, 6]), ALU.mult)
            ins.then_inc(ns.feats_ready, 1)
            for k in range(2 * TILES):
                t, row = k // 2, k % 2
                bank = psum[:, 4 + k % NIB_BANKS, :]
                v.wait_ge(ns.relu, k + 1)
                v.tensor_tensor_reduce(nib_prod[:, k % 2, :], hidden[:, k % 2, :], bank[:, GE:2 * GE], 1.0, 0.0,
                                       ALU.mult, ALU.add, res[:, t, row:row + 1])
                v.tensor_copy(res_b[:, t, row:row + 1], bank[:, 2 * GE:2 * GE + 1]).then_inc(ns.used, 1)
            v.wait_ge(ns.used, 2 * TILES)
            vstep(v, v.tensor_tensor(res[:], res[:], res_b[:], ALU.add))
            vstep(v, v.tensor_scalar(res[:], res[:], 0.0, 15.0, ALU.max, ALU.min))
            vstep(v, v.tensor_scalar(res[:], res[:], ROUND, ROUND, ALU.add, ALU.subtract))
            vstep(v, v.tensor_tensor(onehot[:], digit[:], res[:].rearrange("p t (r o) -> p (t r) o", o=1)
                                     .to_broadcast([P, 2 * TILES, 16]), ALU.is_equal))
            both = onehot[:].rearrange("p (t r) j -> p t (r j)", r=2)
            vstep(v, v.tensor_tensor(both, both, active[:, :, 0:1].to_broadcast([P, TILES, 32]), ALU.mult))
            vstep(v, v.tensor_tensor(resid[:], resid[:], normed[:], ALU.add))
            v.tensor_tensor(resid[:, :, 80:112], resid[:, :, 80:112], both, ALU.add)

        def nibble_scalar(a):
            for c, (t0, w_) in enumerate(GROUPS):
                a.wait_ge(ns.turned, c + 1)
                a.copy(feats_t[:, t0:t0 + w_, :], psum[0:64, c, 0:w_ * P].rearrange("p (t n) -> p t n", n=P)).then_inc(
                    ns.turned_kept, 1)
            for k in range(2 * TILES):
                a.wait_ge(ns.hidden, k + 1)
                if k >= 2:
                    a.wait_ge(ns.used, k - 1)
                a.activation(hidden[:, k % 2, :], psum[:, 4 + k % NIB_BANKS, 0:GE], ACT.Relu).then_inc(ns.relu, 1)

        def nibble_tensor(pe):
            pe.wait_ge(ns.feats_ready, 1)
            for c, (t0, w_) in enumerate(GROUPS):
                for j in range(w_):
                    ins = pe.transpose(psum[0:64, c, j * P:(j + 1) * P], feats[:, t0 + j, :], ident[:])
                ins.then_inc(ns.turned, 1)
            pe.wait_ge(ns.w_loaded, 16 * 16)
            for k in range(2 * TILES):
                t, row = k // 2, k % 2
                pe.wait_ge(ns.turned_kept, t // 4 + 1)
                if k >= NIB_BANKS:
                    pe.wait_ge(ns.used, k - NIB_BANKS + 1)
                at = 32 * row
                pe.matmul(psum[:, 4 + k % NIB_BANKS, 0:2 * GE + 1], feats_t[at:at + 18, t, :],
                          nib_w[at:at + 18, 0:2 * GE + 1], start=True, stop=True).then_inc(ns.hidden, 1)

        MOE = {"L1_ffn": ("L1_ffn_W1", "L1_ffn_b1", "L1_ffn_W2", "L1_ffn_b2", "L1_ffn_Wr"),
               "L2_ffn": ("L2_ffn_Wgu", "L2_ffn_bgu", "L2_ffn_Wd", "L2_ffn_bd", "L2_ffn_Wg")}
        UP = KD * 1024
        up_w = expert_w[:, 0:E * UP].rearrange("p (e k n) -> p e k n", e=E, k=KD)
        down = {x: expert_w[:, E * UP:E * (UP + kh * D)].rearrange("p (e k n) -> p e k n", e=E, k=kh)
                for x, kh in (("L1_ffn", 8), ("L2_ffn", 4))}
        up_b = bias3[:, 0:E * 1024].rearrange("p (e n) -> p e n", e=E)
        down_b = bias3[:, E * 1024:E * 1280].rearrange("p (e n) -> p e n", e=E)

        def moe_items():
            return [("weights",)] + [("turn", i) for i in range(0, TILES, 2)] + [("logits",)]

        def load_router(q, x):
            s = ml[x]
            q.dma_start(router_raw[:], d[MOE[x][4]].rearrange("(k p) e -> p k e", p=P)).then_inc(s.r_loaded, 16)
            if x == "L1_ffn":
                q.dma_start(router_b[:], d["L1_ffn_br"].rearrange("(o n) -> o n", o=1).to_broadcast([P, E])).then_inc(
                    s.r_loaded, 16)
            q.dma_start(split_f[0:64, 0, :], d[MOE[x][1]].rearrange("e (j n) -> (e j) n", n=P)).then_inc(s.b_loaded, 16)
            q.dma_start(split_f[64:80, 0, :], d[MOE[x][3]].rearrange("e (j n) -> (e j) n", n=P)).then_inc(s.b_loaded, 16)

        def load_experts(q, x):
            s = ml[x]
            for e in range(E):
                q.dma_start(up_w[:, e], d[MOE[x][0]][e].rearrange("(k p) n -> p k n", p=P)).then_inc(s.w_loaded, 16)
                q.dma_start(down[x][:, e], d[MOE[x][2]][e].rearrange("(k p) n -> p k n", p=P)).then_inc(s.w_loaded, 16)

        def place_biases(q, x):
            s = ml[x]
            q.wait_ge(s.b_split, 1)
            for i in range(3):
                q.dma_start(bias_scratch[i].rearrange("(a n) -> a n", n=P), split_b[:, i, :]).then_inc(s.b_placed, 16)
            q.wait_ge(s.b_placed, 48)
            q.dma_start(bias3[:], bias_scratch).then_inc(s.b_spread, 16)

        def load_slots(q, x):
            s = ml[x]
            q.wait_ge(s.sent, 16 * 2 * TILES)

            def load(k, parity):
                q.dma_start(slot_x[:, parity, :], slots_in[bass.ds(k * P, P), :]).then_inc(s.x_loaded[parity], 16)

            q.wait_ge(s.logits, 1)
            load(0, 0)
            load(1, 1)
            q.wait_ge(s.x_turned, 1)
            load(2, 0)
            with q.Fori(0, (SLOTS - 3) // 2) as j:
                for parity in (1, 0):
                    k = j * 2 + (3 if parity else 4)
                    q.wait_ge(s.x_turned, k - 1)
                    load(k, parity)

        def moe_tensor(pe, x, rows_base):
            s = ml[x]
            turned, w = pairs(mturned_hi, mturned_lo), pairs(router_hi, router_lo)
            for k, it in enumerate(moe_items()):
                if it[0] == "weights":
                    continue
                ring_free(pe, s.item_done, k)
                if it[0] == "turn":
                    ins = turn_tensor(pe, it[1], k, rows_base)
                else:
                    pe.wait_ge(s.item_done, k)
                    for t in range(TILES):
                        for kb in range(KD):
                            ins = product(pe, psum[:, k % RING, t * E:(t + 1) * E],
                                          turned(slice(None), kb, slice(t * P, (t + 1) * P)),
                                          w(slice(None), kb, slice(None)), kb == 0, kb == KD - 1)
                ins.then_inc(s.item_ready, 1)
            pe.wait_ge(s.chosen, 1)
            both = router_sb[0]
            flat = psum[:, 4, 0:TILES * E]
            pe.matmul(flat, before[:], both[:].rearrange("p t e -> p (t e)"), start=True, stop=False)
            for t in range(TILES - 1):
                rest = TILES - 1 - t
                pe.matmul(psum[:, 4, (t + 1) * E:TILES * E].rearrange("p (t e) -> p t e", e=E), ones[:],
                          both[:, t:t + 1, :].to_broadcast([P, rest, E]), start=False, stop=t == TILES - 2)
            for t in range(TILES):
                ins = pe.matmul(psum[:, 5, 0:E], ones[:], both[:, t, :], start=t == 0, stop=t == TILES - 1)
            ins.then_inc(s.counted, 1)

            HB = 8 if x == "L1_ffn" else 4
            pe.wait_ge(s.placed, 1)

            def expert(k):
                return bass.ds(pe.value_load(slot_expert[0:1, bass.ds(k, 1)], min_val=0, max_val=E - 1), 1)

            def one(ap):
                return ap.rearrange("p o n -> p (o n)")

            def turn_x(k, parity, half):
                pe.wait_ge(s.x_loaded[parity], (half + 1) * 16)
                for kb in range(KD):
                    ins = pe.transpose(psum[:, 6, kb * P:(kb + 1) * P], slot_x[:, parity, kb * P:(kb + 1) * P], ident[:])
                ins.then_inc(s.x_turned, 1)

            def up(k, parity, early=False):
                e = expert(k)
                pe.wait_ge(s.xt_ready, k + 1)
                if not early:
                    pe.wait_ge(s.h_kept_s, k - 1)
                    pe.wait_ge(s.h_kept_v, k - 1)
                for c in range(2):
                    o = psum[:, 2 * parity + c, :]
                    pe.matmul(o, ones3[:], one(up_b[:, e, c * BANK:(c + 1) * BANK]), start=True, stop=False)
                    for kb in range(KD):
                        ins = pe.matmul(o, slot_xt[:, parity, kb, :], one(up_w[:, e, kb, c * BANK:(c + 1) * BANK]),
                                        start=False, stop=kb == KD - 1)
                    ins.then_inc(s.h_ready, 1)

            def turn_h(k, parity):
                pe.wait_ge(s.h_kept_s, k + 1)
                if x == "L2_ffn":
                    pe.wait_ge(s.h_kept_v, k + 1)
                if not isinstance(k, int) or k > 0:
                    pe.wait_ge(s.ht_ready_s, k)
                for b in range(HB):
                    if b == 4:
                        pe.wait_ge(s.h_kept_v, k + 1)
                        if not isinstance(k, int) or k > 0:
                            pe.wait_ge(s.ht_ready_v, k)
                    ins = pe.transpose(psum[:, 4 + b // 4, b % 4 * P:(b % 4 + 1) * P],
                                       slot_h[:, parity, b * P:(b + 1) * P], ident[:])
                    if b % 4 == 3:
                        ins.then_inc(s.h_turned, 1)

            def down_(k):
                e = expert(k)
                if not isinstance(k, int) or k > 0:
                    pe.wait_ge(s.y_kept, k)
                o = psum[:, 7, 0:D]
                pe.matmul(o, ones3[:], one(down_b[:, e, :]), start=True, stop=False)
                pe.wait_ge(s.ht_ready_s, k + 1)
                for b in range(HB):
                    if b == 4:
                        pe.wait_ge(s.ht_ready_v, k + 1)
                    ins = pe.matmul(o, slot_ht[:, b * P:(b + 1) * P], one(down[x][:, e, b, :]),
                                    start=False, stop=b == HB - 1)
                ins.then_inc(s.y_ready, 1)

            def step(k, parity, half, early=False, last=False):
                turn_h(k - 1, 1 - parity)
                up(k, parity, early)
                if not last:
                    turn_x(k + 1, 1 - parity, half + parity)
                down_(k - 1)

            pe.wait_ge(s.w_loaded, 16 * 2 * E)
            pe.wait_ge(s.b_spread, 16)
            turn_x(0, 0, 0)
            up(0, 0, early=True)
            turn_x(1, 1, 0)
            step(1, 1, 0, early=True)
            step(2, 0, 1)
            with pe.Fori(0, (SLOTS - 5) // 2) as j:
                step(j * 2 + 3, 1, j + 1)
                step(j * 2 + 4, 0, j + 2)
            step(SLOTS - 2, 1, (SLOTS - 2) // 2)
            step(SLOTS - 1, 0, (SLOTS - 1) // 2, last=True)
            turn_h(SLOTS - 1, 0)
            down_(SLOTS - 1)

        def moe_scalar(a, x):
            s = ml[x]
            n_pe = 0
            for k, it in enumerate(moe_items()):
                if it[0] == "weights":
                    a.wait_ge(s.r_loaded, 32 if x == "L1_ffn" else 16)
                    a.copy(router_hi[:], router_raw[:]).then_inc(s.item_hi, 1)
                elif it[0] == "turn":
                    n_pe += 1
                    a.wait_ge(s.item_ready, n_pe)
                    src, cols = turn_source(it[1], k)
                    a.copy(mturned_hi[:, :, cols], src).then_inc(s.item_hi, 1)
            a.wait_ge(s.gap, 1)
            a.activation(best[:, :, 3], best[:, :, 2], ACT.Exp).then_inc(s.gap_exp, 1)

            def keep_xt(k, parity, early=False):
                a.wait_ge(s.x_turned, k + 1)
                if not early:
                    a.wait_ge(s.h_ready, k * 2 - 2)
                a.copy(slot_xt[:, parity, :, :], psum[:, 6, 0:D].rearrange("p (k n) -> p k n", k=KD)).then_inc(
                    s.xt_ready, 1)

            def keep_h(k, parity, early=False):
                a.wait_ge(s.h_ready, k * 2 + 1)
                if x == "L1_ffn":
                    if not early:
                        a.wait_ge(s.h_turned, k * 2 - 2)
                    a.activation(slot_h[:, parity, 0:BANK], psum[:, 2 * parity, :], ACT.Relu).then_inc(s.h_kept_s, 1)
                else:
                    if not isinstance(k, int) or k > 0:
                        a.wait_ge(s.h_kept_v, k)
                    a.activation(slot_silu[:], psum[:, 2 * parity, :], ACT.Silu).then_inc(s.h_kept_s, 1)

            def keep_ht(k):
                a.wait_ge(s.h_turned, k * 2 + 1 if x == "L1_ffn" else k + 1)
                if not isinstance(k, int) or k > 0:
                    a.wait_ge(s.y_ready, k)
                a.copy(slot_ht[:, 0:BANK], psum[:, 4, :]).then_inc(s.ht_ready_s, 1)

            def step(k, parity, early=False, last=False):
                keep_ht(k - 1)
                keep_h(k, parity, early)
                if not last:
                    keep_xt(k + 1, 1 - parity)

            keep_xt(0, 0, early=True)
            keep_h(0, 0, early=True)
            keep_xt(1, 1, early=True)
            step(1, 1, early=True)
            step(2, 0)
            with a.Fori(0, (SLOTS - 5) // 2) as j:
                step(j * 2 + 3, 1)
                step(j * 2 + 4, 0)
            step(SLOTS - 2, 1)
            step(SLOTS - 1, 0, last=True)
            keep_ht(SLOTS - 1)

        def moe_vector(v, x, inst):
            s = ml[x]
            v.wait_ge(s.b_loaded, 32)
            vstep(v, v.tensor_copy(split_b[:, 0, :], split_f[:, 0, :]))
            vstep(v, v.tensor_tensor(split_f[:, 1, :], split_f[:, 0, :], split_b[:, 0, :], ALU.subtract))
            vstep(v, v.tensor_copy(split_b[:, 1, :], split_f[:, 1, :]))
            vstep(v, v.tensor_tensor(split_f[:, 2, :], split_f[:, 1, :], split_b[:, 1, :], ALU.subtract))
            v.tensor_copy(split_b[:, 2, :], split_f[:, 2, :]).then_inc(s.b_split, 1)
            if x == "L2_ffn":
                vstep(v, v.memset(router_b[:], 0.0))
            for k, it in enumerate(moe_items()):
                if it[0] == "logits":
                    continue
                v.wait_ge(s.item_hi, k + 1)
                if it[0] == "weights":
                    ins = v.tensor_tensor(router_lo[:], router_raw[:], router_hi[:].bitcast(F32), ALU.subtract)
                else:
                    src, cols = turn_source(it[1], k)
                    ins = v.tensor_tensor(mturned_lo[:, :, cols], src, mturned_hi[:, :, cols].bitcast(F32), ALU.subtract)
                ins.then_inc(s.item_done, 1)
            logits, eq, rest = router_sb

            def rows(ap, width=E):
                return ap.to_broadcast([P, TILES, width])

            v.wait_ge(s.item_ready, len(moe_items()) - 1)
            src = psum[:, (len(moe_items()) - 1) % RING, 0:TILES * E].rearrange("p (t e) -> p t e", e=E)
            ins = v.tensor_tensor(logits[:], src, router_b[:].rearrange("p (o e) -> p o e", o=1)
                                  .to_broadcast([P, TILES, E]), ALU.add)
            ins.then_inc(s.logits, 1)
            v.wait_ge(s.logits, 1)
            for which, (frm, hot) in enumerate(((logits, first), (rest, second))):
                vstep(v, v.tensor_reduce(best[:, :, which], frm[:], AX.X, ALU.max))
                vstep(v, v.tensor_tensor(eq[:], frm[:], rows(best[:, :, which:which + 1]), ALU.is_equal))
                vstep(v, v.tensor_tensor(eq[:], eq[:], rank_down[:], ALU.mult))
                vstep(v, v.tensor_reduce(best[:, :, 2], eq[:], AX.X, ALU.max))
                vstep(v, v.tensor_tensor(hot[:], eq[:], rows(best[:, :, 2:3]), ALU.is_equal))
                if which == 0:
                    vstep(v, v.scalar_tensor_tensor(rest[:], first[:], LOWEST, logits[:], ALU.mult, ALU.add))
            vstep(v, v.tensor_tensor(logits[:], first[:], second[:], ALU.add))
            v.tensor_tensor(logits[:], logits[:], rows(valid[:].rearrange("p (t o) -> p t o", o=1)),
                            ALU.mult).then_inc(s.chosen, 1)
            v.tensor_tensor(best[:, :, 2:3], best[:, :, 1:2], best[:, :, 0:1], ALU.subtract).then_inc(s.gap, 1)
            v.wait_ge(s.gap_exp, 1)
            vstep(v, v.tensor_scalar(gate[:, :, 1:2], best[:, :, 3:4], 1.0, None, ALU.add))
            vstep(v, v.reciprocal(gate[:, :, 0:1], gate[:, :, 1:2]))
            v.tensor_tensor(gate[:, :, 1:2], best[:, :, 3:4], gate[:, :, 0:1], ALU.mult)
            v.wait_ge(s.counted, 1)
            vstep(v, v.tensor_copy(per_expert[:, 0, :], psum[:, 5, 0:E]))
            vstep(v, v.tensor_tensor(step_gt[:], per_expert[:, 0, :].rearrange("p (e o) -> p e o", o=1)
                                     .to_broadcast([P, E, TILES]), steps128[:], ALU.is_gt))
            vstep(v, v.tensor_reduce(per_expert[:, 1, :], step_gt[:], AX.X, ALU.add))
            vstep(v, v.tensor_tensor(lt_prod[:], expert_lt[:], per_expert[:, 1:2, :].to_broadcast([P, E, E]), ALU.mult))
            vstep(v, v.tensor_reduce(per_expert[:, 2, :], lt_prod[:], AX.X, ALU.add))
            vstep(v, v.tensor_tensor(per_expert[:, 3, :], per_expert[:, 2, :], per_expert[:, 1, :], ALU.add))
            vstep(v, v.tensor_tensor(slot_ge[:], slot_iota[:], per_expert[:, 3:4, :].to_broadcast([P, SLOTS, E]),
                                     ALU.is_ge))
            vstep(v, v.tensor_reduce(slot_f[:], slot_ge[:], AX.X, ALU.add))
            vstep(v, v.tensor_scalar(slot_expert[:], slot_f[:], E - 1.0, None, ALU.min))
            vstep(v, v.scalar_tensor_tensor(rest[:], per_expert[:, 2:3, :].to_broadcast([P, TILES, E]), float(P),
                                            psum[:, 4, 0:TILES * E].rearrange("p (t e) -> p t e", e=E),
                                            ALU.mult, ALU.add))
            for which, hot in enumerate((first, second)):
                vstep(v, v.tensor_tensor(eq[:], rest[:], hot[:], ALU.mult))
                vstep(v, v.tensor_reduce(pos[:, which, :], eq[:], AX.X, ALU.add))
            v.tensor_copy(pos_u[:], pos[:]).then_inc(s.placed, 1)

            def keep_h(k, parity, early=False):
                v.wait_ge(s.h_ready, k * 2 + 2)
                if not early:
                    v.wait_ge(s.h_turned, k * 2 - 2 if x == "L1_ffn" else k - 1)
                bank = psum[:, 2 * parity + 1, :]
                if x == "L1_ffn":
                    v.tensor_scalar(slot_h[:, parity, BANK:2 * BANK], bank, 0.0, None, ALU.max).then_inc(s.h_kept_v, 1)
                else:
                    v.wait_ge(s.h_kept_s, k + 1)
                    v.tensor_tensor(slot_h[:, parity, 0:BANK], bank, slot_silu[:], ALU.mult).then_inc(s.h_kept_v, 1)

            def keep_ht(k):
                if x == "L1_ffn":
                    v.wait_ge(s.h_turned, k * 2 + 2)
                    if not isinstance(k, int) or k > 0:
                        v.wait_ge(s.y_ready, k)
                    v.tensor_copy(slot_ht[:, BANK:2 * BANK], psum[:, 5, :]).then_inc(s.ht_ready_v, 1)

            def keep_y(k, parity, half):
                v.wait_ge(s.y_ready, k + 1)
                if not isinstance(k, int) or k > 1:
                    v.wait_ge(s.y_stored[parity], half * 16)
                v.tensor_copy(slot_y[:, parity, :], psum[:, 7, 0:D]).then_inc(s.y_kept, 1)

            def step(k, parity, half, early=False):
                keep_ht(k - 1)
                keep_h(k, parity, early)
                keep_y(k - 1, 1 - parity, half)

            keep_h(0, 0, early=True)
            step(1, 1, 0, early=True)
            step(2, 0, 0)
            with v.Fori(0, (SLOTS - 5) // 2) as j:
                step(j * 2 + 3, 1, j + 1)
                step(j * 2 + 4, 0, j + 1)
            step(SLOTS - 2, 1, (SLOTS - 3) // 2)
            step(SLOTS - 1, 0, (SLOTS - 3) // 2)
            keep_ht(SLOTS - 1)
            keep_y(SLOTS - 1, 0, (SLOTS - 1) // 2)
            for t in range(TILES):
                r_ = LAST if t == TILES - 1 else P
                v.wait_ge(gathered_ready[t], 32 * (inst + 1))
                for which in range(2):
                    vstep(v, v.scalar_tensor_tensor(resid[0:r_, t, :], gathered[0:r_, t, which, :],
                                                    gate[0:r_, t, which:which + 1], resid[0:r_, t, :],
                                                    ALU.mult, ALU.add))

        def moe_pool(p, x, inst):
            s = ml[x]
            p.wait_ge(slots_cleared, 16)
            p.wait_ge(s.placed, 1)
            for which in range(2):
                for t in range(TILES):
                    r_ = LAST if t == TILES - 1 else P
                    p.indirect_dma_start(slots_in, bass.IndirectOffsetOnAxis(pos_u[0:r_, which, t:t + 1], 0),
                                         normed[0:r_, t, :], None).then_inc(s.sent, 16)

            def store(k, parity):
                p.wait_ge(s.y_kept, k + 1)
                p.dma_start(slots_out[bass.ds(k * P, P), :], slot_y[:, parity, :]).then_inc(s.y_stored[parity], 16)

            store(0, 0)
            with p.Fori(0, (SLOTS - 1) // 2) as j:
                store(j * 2 + 1, 1)
                store(j * 2 + 2, 0)
            p.wait_ge(s.y_stored[0], 16 * ((SLOTS + 1) // 2))
            p.wait_ge(s.y_stored[1], 16 * (SLOTS // 2))
            for t in range(TILES):
                for which in range(2):
                    r_ = LAST if t == TILES - 1 else P
                    p.indirect_dma_start(gathered[0:r_, t, which, :], None, slots_out,
                                         bass.IndirectOffsetOnAxis(pos_u[0:r_, which, t:t + 1], 0)).then_inc(
                        gathered_ready[t], 16)

        def f_items():
            return ([("gates",)] + [("in", wh, kb, half) for wh in range(2) for kb in range(KD) for half in range(2)] +
                    [("out", e, kp) for e in range(E + 1) for kp in range(2)] +
                    [("turn", i) for i in range(0, TILES, 2)] + [("logits",)])

        FI = {it: k for k, it in enumerate(f_items())}

        def load_f(q):
            def every(b, width):
                return b.rearrange("(o n) -> o n", o=1).to_broadcast([P, width])

            for dst, src in ((gate_nat[0:2, :], d["L3_ffn_group_gate_w"]), (gate_nat[2:E + 2, :], d["L3_ffn_expert_gate_w"]),
                             (gate_b[:, 0:2], every(d["L3_ffn_group_bias"], 2)),
                             (gate_b[:, 2:E + 2], every(d["L3_ffn_expert_bias"], E)),
                             (ln_rows[:, 0, :], every(d["L3_ffn_ln_scale"], D)),
                             (ln_rows[:, 1, :], every(d["L3_ffn_ln_bias"], D)),
                             (bias9[0:E, :], d["L3_ffn_expert_out_bias"]),
                             (bias9[E:E + 1, :], d["L3_ffn_shared_out_b"].rearrange("(o n) -> o n", o=1))):
                q.dma_start(dst, src).then_inc(fs.loaded, 16)
            for wh, name in enumerate(("L3_ffn_shared_in_w", "L3_ffn_expert_in_w")):
                q.dma_start(nat_in[:, wh], d[name].rearrange("(b p) n -> p b n", p=P)).then_inc(fs.in_loaded[wh], 16)
            for e in range(E + 1):
                if e >= 2:
                    q.wait_ge(fs.item_done, FI[("out", e - 2, 1)] + 1)
                src = d["L3_ffn_expert_out_weight"][e] if e < E else d["L3_ffn_shared_out_w"]
                q.dma_start(nat_out[:, e % 2], src.rearrange("(b p) n -> p b n", p=P)).then_inc(fs.out_loaded[e % 2], 16)

        def f_source(it, k):
            bank = psum[:, k % RING, :]
            if it[0] == "gates":
                return bank[:, 0:KD * (E + 2)].rearrange("p (k n) -> p k n", k=KD), gate_hi[:], gate_lo[:]
            if it[0] == "in":
                _, wh, kb, half = it
                cols = slice(half * BANK, (half + 1) * BANK)
                return bank, in_hi[:, wh, kb, cols], in_lo[:, wh, kb, cols]
            if it[0] == "out":
                _, e, kp = it
                ix = (slice(None), slice(2 * kp, 2 * kp + 2), slice(e * D, (e + 1) * D))
                return bank.rearrange("p (k n) -> p k n", k=2), out_hi[ix], out_lo[ix]
            src, cols = turn_source(it[1], k)
            return src, f_turned_hi[:, :, cols], f_turned_lo[:, :, cols]

        def f_tensor(pe, rows_base):
            s = fs
            for k, it in enumerate(f_items()):
                ring_free(pe, s.item_done, k)
                if it[0] == "gates":
                    pe.wait_ge(s.loaded, 16 * 8)
                    for kb in range(KD):
                        ins = pe.transpose(psum[:, k % RING, kb * (E + 2):(kb + 1) * (E + 2)],
                                           gate_nat[:, kb * P:(kb + 1) * P], ident[0:E + 2, 0:E + 2])
                elif it[0] == "in":
                    _, wh, kb, half = it
                    pe.wait_ge(s.in_loaded[wh], 16)
                    for j in range(4):
                        ins = pe.transpose(psum[:, k % RING, j * P:(j + 1) * P],
                                           nat_in[:, wh, 4 * half + j, kb * P:(kb + 1) * P], ident[:])
                elif it[0] == "out":
                    _, e, kp = it
                    pe.wait_ge(s.out_loaded[e % 2], 16 * (e // 2 + 1))
                    for j in range(2):
                        for nb in range(2):
                            at = (2 * kp + j) * P
                            ins = pe.transpose(psum[:, k % RING, j * D + nb * P:j * D + (nb + 1) * P],
                                               nat_out[:, e % 2, nb, at:at + P], ident[:])
                elif it[0] == "turn":
                    ins = turn_tensor(pe, it[1], k, rows_base)
                else:
                    pe.wait_ge(s.item_done, k)
                    for t in range(TILES):
                        for kb in range(KD):
                            ins = product(pe, psum[:, k % RING, t * (E + 2):(t + 1) * (E + 2)],
                                          pairs(f_turned_hi, f_turned_lo)(slice(None), kb, slice(t * P, (t + 1) * P)),
                                          pairs(gate_hi, gate_lo)(slice(None), kb, slice(None)), kb == 0, kb == KD - 1)
                ins.then_inc(s.item_ready, 1)
            pe.wait_ge(s.item_done, len(f_items()))

            def hidden_(t, wh):
                k = 2 * t + wh
                if t >= 1:
                    pe.wait_ge(s.h_kept, k - 1)
                for half in range(2):
                    for kb in range(KD):
                        ins = product(pe, psum[:, 2 * wh + half, :],
                                      pairs(f_turned_hi, f_turned_lo)(slice(None), kb, slice(t * P, (t + 1) * P)),
                                      pairs(in_hi, in_lo)(slice(None), wh, kb, slice(half * BANK, (half + 1) * BANK)),
                                      kb == 0, kb == KD - 1)
                ins.then_inc(s.h_ready, 1)

            def turn(t, wh):
                k = 2 * t + wh
                pe.wait_ge(s.h_kept, k + 1)
                if k >= 1:
                    pe.wait_ge(s.ht_done, k)
                for j in range(4):
                    ins = pe.transpose(psum[:, 4, j * P:(j + 1) * P], act_h[:, wh, j * P:(j + 1) * P], ident[:])
                ins.then_inc(s.h_turned, 1)

            def outputs(t):
                k = 5 * t
                pe.wait_ge(s.ht_done, 2 * t + 1)
                if t >= 1:
                    pe.wait_ge(s.y_used, k - 4)
                if t == 0:
                    pe.wait_ge(s.cnt_kept, NG)
                pe.matmul(psum[:, 5, 0:D], cnt_t[:, t, :], bias9[:], start=True, stop=False)
                for kq in range(4):
                    ins = product(pe, psum[:, 5, 0:D], pairs(act_t_hi, act_t_lo)(slice(None), 0, slice(kq * P, (kq + 1) * P)),
                                  pairs(out_hi, out_lo)(slice(None), kq, slice(E * D, (E + 1) * D)), False, kq == 3)
                ins.then_inc(s.y_ready, 1)
                pe.wait_ge(s.ht_done, 2 * t + 2)
                for q in range(4):
                    n_ = k + 1 + q
                    if q >= 2:
                        pe.wait_ge(s.y_used, n_ - 1)
                    elif t >= 1:
                        pe.wait_ge(s.y_used, n_ - 2)
                    for kq in range(4):
                        ins = product(pe, psum[:, 6 + q % 2, :],
                                      pairs(act_t_hi, act_t_lo)(slice(None), 1, slice(kq * P, (kq + 1) * P)),
                                      pairs(out_hi, out_lo)(slice(None), kq, slice(q * BANK, (q + 1) * BANK)),
                                      kq == 0, kq == 3)
                    ins.then_inc(s.y_ready, 1)

            hidden_(0, 0)
            hidden_(0, 1)
            pe.wait_ge(s.cnt_ready, 1)
            for c, (t0, w_) in enumerate(GROUPS):
                for j in range(w_):
                    ins = pe.transpose(psum[0:E + 1, 5 + c, j * P:(j + 1) * P], cnt[:, t0 + j, :], ident[:])
                ins.then_inc(s.cnt_turned, 1)
            for t in range(TILES):
                turn(t, 0)
                if t + 1 < TILES:
                    hidden_(t + 1, 0)
                turn(t, 1)
                if t + 1 < TILES:
                    hidden_(t + 1, 1)
                outputs(t)

        def f_scalar(a):
            s = fs
            for k, it in enumerate(f_items()[:-1]):
                if it == ("turn", 0):
                    norm_scalar(a, norm_index["L3_ffn"] + 1)
                a.wait_ge(s.item_ready, k + 1)
                src, hi_, _ = f_source(it, k)
                a.copy(hi_, src).then_inc(s.item_hi, 1)
            a.wait_ge(s.exp_in, 1)
            a.activation(esel[:, 1], esel[:, 0], ACT.Exp).then_inc(s.exp_out, 1)

            def silu(t, wh):
                a.wait_ge(s.h_ready, 2 * t + wh + 1)
                if t >= 1:
                    a.wait_ge(s.h_kept, 2 * t + wh - 1)
                a.activation(act_silu[:, wh, :], psum[:, 2 * wh, :], ACT.Silu).then_inc(s.silu, 1)

            def hi(t, wh):
                a.wait_ge(s.h_turned, 2 * t + wh + 1)
                if t >= 1:
                    a.wait_ge(s.y_ready, 5 * t - 4 if wh == 0 else 5 * t)
                a.copy(act_t_hi[:, wh, :], psum[:, 4, :]).then_inc(s.ht_hi, 1)

            silu(0, 0)
            silu(0, 1)
            for c, (t0, w_) in enumerate(GROUPS):
                a.wait_ge(s.cnt_turned, c + 1)
                a.copy(cnt_t[:, t0:t0 + w_, :], psum[0:E + 1, 5 + c, 0:w_ * P].rearrange("p (t n) -> p t n", n=P)).then_inc(
                    s.cnt_kept, 1)
            for t in range(TILES):
                hi(t, 0)
                if t + 1 < TILES:
                    silu(t + 1, 0)
                hi(t, 1)
                if t + 1 < TILES:
                    silu(t + 1, 1)

        def f_norm(v, rows_base, index):
            v.wait_ge(rows_normed, rows_base + TILES)
            v.wait_ge(fs.loaded, 16 * 8)
            for t in range(TILES):
                ins = v.bn_stats(stats[:, t, :], normed[:, t, :])
            vstep(v, ins)
            for t in range(TILES):
                ins = v.bn_aggr(mean_var[:, t, :], stats[:, t, :])
            vstep(v, ins)
            v.tensor_scalar(var_eps[:], mean_var[:, :, 1], EPS, None, ALU.add).then_inc(var_ready, 1)
            v.wait_ge(std_ready, index + 1)
            vstep(v, v.reciprocal(rstd[:], std[:]))
            for t in range(TILES):
                ins = v.tensor_scalar(normed[:, t, :], normed[:, t, :], mean_var[:, t, 0:1], rstd[:, t:t + 1],
                                      ALU.subtract, ALU.mult)
            vstep(v, ins)
            vstep(v, v.tensor_tensor(normed[:], normed[:], ln_rows[:, 0:1, :].to_broadcast([P, TILES, D]), ALU.mult))
            for t in range(TILES):
                v.tensor_tensor(normed[:, t, :], normed[:, t, :], ln_rows[:, 1, :], ALU.add).then_inc(rows_normed, 1)

        def f_vector(v):
            s = fs
            for k, it in enumerate(f_items()[:-1]):
                if it == ("turn", 0):
                    f_norm(v, rows_at["L3_ffn"], norm_index["L3_ffn"] + 1)
                v.wait_ge(s.item_hi, k + 1)
                src, hi_, lo_ = f_source(it, k)
                v.tensor_tensor(lo_, src, hi_.bitcast(F32), ALU.subtract).then_inc(s.item_done, 1)
            v.wait_ge(s.item_ready, len(f_items()))
            bank = psum[:, (len(f_items()) - 1) % RING, 0:TILES * (E + 2)].rearrange("p (t e) -> p t e", t=TILES)
            ins = v.tensor_tensor(glog[:], bank, gate_b[:].rearrange("p (o e) -> p o e", o=1)
                                  .to_broadcast([P, TILES, E + 2]), ALU.add)
            ins.then_inc(s.item_done, 1)
            v.wait_ge(s.item_done, len(f_items()))

            def four(ap):
                return ap.to_broadcast([P, TILES, 4])

            def col_(i):
                return psel[:, i:i + 1, :].rearrange("p o t -> p t o")

            vstep(v, v.tensor_tensor(grp[:, :, 1:2], glog[:, :, 1:2], glog[:, :, 0:1], ALU.is_gt))
            vstep(v, v.tensor_scalar(grp[:, :, 0:1], grp[:, :, 1:2], -1.0, 1.0, ALU.mult, ALU.add))
            v.tensor_tensor(esel[:, 1], glog[:, :, 2:6], four(grp[:, :, 0:1]), ALU.mult)
            vstep(v, v.tensor_tensor(esel[:, 2], glog[:, :, 6:10], four(grp[:, :, 1:2]), ALU.mult))
            vstep(v, v.tensor_tensor(esel[:, 0], esel[:, 1], esel[:, 2], ALU.add))
            vstep(v, v.tensor_reduce(psel[:, 0, :], esel[:, 0], AX.X, ALU.max))
            v.tensor_tensor(esel[:, 0], esel[:, 0], four(col_(0)), ALU.subtract).then_inc(s.exp_in, 1)
            v.wait_ge(s.exp_out, 1)
            vstep(v, v.tensor_reduce(psel[:, 1, :], esel[:, 1], AX.X, ALU.add))
            vstep(v, v.reciprocal(psel[:, 1, :], psel[:, 1, :]))
            vstep(v, v.tensor_tensor(esel[:, 2], esel[:, 1], four(col_(1)), ALU.mult))
            probs4, hot1, rest4, hot2 = esel[:, 2], esel[:, 3], esel[:, 4], esel[:, 5]
            for which, (frm, hot) in enumerate(((probs4, hot1), (rest4, hot2))):
                vstep(v, v.tensor_reduce(psel[:, which, :], frm, AX.X, ALU.max))
                vstep(v, v.tensor_tensor(pk[:], frm, four(col_(which)), ALU.is_equal))
                vstep(v, v.tensor_tensor(pk[:], pk[:], rank_down[:, :, 4:8], ALU.mult))
                vstep(v, v.tensor_reduce(psel[:, 2, :], pk[:], AX.X, ALU.max))
                vstep(v, v.tensor_tensor(hot, pk[:], four(col_(2)), ALU.is_equal))
                if which == 0:
                    vstep(v, v.scalar_tensor_tensor(rest4, hot1, -8.0, probs4, ALU.mult, ALU.add))
            vstep(v, v.tensor_tensor(psel[:, 3, :], psel[:, 0, :], psel[:, 1, :], ALU.add))
            vstep(v, v.tensor_scalar(psel[:, 3, :], psel[:, 3, :], 1e-8, None, ALU.add))
            vstep(v, v.reciprocal(psel[:, 3, :], psel[:, 3, :]))
            vstep(v, v.tensor_tensor(esel[:, 0], hot1, hot2, ALU.add))
            vstep(v, v.tensor_tensor(esel[:, 1], esel[:, 0], probs4, ALU.mult))
            vstep(v, v.tensor_tensor(esel[:, 1], esel[:, 1], four(col_(3)), ALU.mult))
            for gi in range(2):
                v.tensor_tensor(comb[:, :, 4 * gi:4 * gi + 4], esel[:, 1], four(grp[:, :, gi:gi + 1]), ALU.mult)
                v.tensor_tensor(cnt[:, :, 4 * gi:4 * gi + 4], esel[:, 0], four(grp[:, :, gi:gi + 1]), ALU.mult)
            vstep(v, v.memset(cnt[:, :, E:E + 1], 1.0))
            v.engine_nop().then_inc(s.cnt_ready, 1)

            def gated(t, wh):
                k = 2 * t + wh
                v.wait_ge(s.silu, k + 1)
                if t >= 1:
                    v.wait_ge(s.h_turned, k - 1)
                v.tensor_tensor(act_h[:, wh, :], psum[:, 2 * wh + 1, :], act_silu[:, wh, :], ALU.mult).then_inc(s.h_kept, 1)

            def lo(t, wh):
                v.wait_ge(s.ht_hi, 2 * t + wh + 1)
                v.tensor_tensor(act_t_lo[:, wh, :], psum[:, 4, :], act_t_hi[:, wh, :].bitcast(F32),
                                ALU.subtract).then_inc(s.ht_done, 1)

            gated(0, 0)
            gated(0, 1)
            for t in range(TILES):
                lo(t, 0)
                if t + 1 < TILES:
                    gated(t + 1, 0)
                lo(t, 1)
                if t + 1 < TILES:
                    gated(t + 1, 1)
                v.wait_ge(s.y_ready, 5 * t + 1)
                ins = v.tensor_tensor(resid[:, t, :], psum[:, 5, 0:D], resid[:, t, :], ALU.add)
                ins.then_inc(s.y_used, 1)
                v.wait_ge(s.y_used, 5 * t + 1)
                for q in range(4):
                    v.wait_ge(s.y_ready, 5 * t + 2 + q)
                    for j in range(2):
                        ins = v.scalar_tensor_tensor(resid[:, t, :], psum[:, 6 + q % 2, j * D:(j + 1) * D],
                                                     comb[:, t, 2 * q + j:2 * q + j + 1], resid[:, t, :],
                                                     ALU.mult, ALU.add)
                        if j == 0:
                            vstep(v, ins)
                    ins.then_inc(s.y_used, 1)
                    v.wait_ge(s.y_used, 5 * t + 2 + q)

        numbers = {}
        rows_at = {}
        count = 1
        rows = 0
        for st in stages:
            if st == "L3_gnn":
                numbers["L3a"], numbers["L3b"] = count, count + 1
                rows_at["L3a"], rows_at["L3b"] = rows, rows + TILES
                rows += 3 * TILES
                count += 2
            else:
                numbers[st] = count
                rows_at[st] = rows
                rows += TILES * (2 if st == "L3_ffn" else 1)
                count += 1
        counts["rows_end_L3b"] = rows_at.get("L3b", 0) + 2 * TILES
        order = [x for st in stages for x in (("L3a", "L3b") if st == "L3_gnn" else (st,))]
        norm_index = {}
        for x in order:
            if x != "L3b":
                norm_index[x] = len(norm_index)

        @block.sync
        def _(sp):
            sp.wait_ge(consts_ready, 1)
            sp.dma_start(resid[:, 0:TILES - 1, :],
                         d["x"][0:(TILES - 1) * P, :].rearrange("(t p) n -> p t n", p=P)).then_inc(x_loaded, 16)
            sp.dma_start(resid[0:LAST, TILES - 1, :], d["x"][(TILES - 1) * P:N, :]).then_inc(x_loaded, 16)
            for x in order:
                if numbers[x] > 1:
                    sp.wait_ge(stage_done, 4 * (numbers[x] - 1))
                if x in gb:
                    load_weights(sp, x)
                    load_adjacency(sp, x)
                    if x == "L0_gnn" and "L0_ffn" in numbers:
                        load_nibble_weights(sp)
                elif x == "L0_ffn" and numbers[x] == 1:
                    load_nibble_weights(sp)
                elif x in ml:
                    load_router(sp, x)
                    load_experts(sp, x)
                    place_biases(sp, x)
                    load_slots(sp, x)
                elif x == "L3_ffn":
                    load_f(sp)
            sp.wait_ge(stage_done, 4 * (count - 1))
            sp.dma_start(out[0:(TILES - 1) * P, :].rearrange("(t p) n -> p t n", p=P),
                         resid[:, 0:TILES - 1, :]).then_inc(out_stored, 16)
            sp.dma_start(out[(TILES - 1) * P:N, :], resid[0:LAST, TILES - 1, :]).then_inc(out_stored, 16)
            sp.wait_ge(out_stored, 32)

        @block.gpsimd
        def _(p):
            pstep(p, p.memset(resid[:, TILES - 1, :], 0.0))
            p.memset(ident[:], 0.0)
            p.memset(valid[:], 1.0)
            p.memset(ones3[:], 1.0)
            p.memset(before[:], 1.0)
            pstep(p, p.memset(ones[:], 1.0))
            p.affine_select(out=ident[:], in_=ident[:], compare_op=ALU.not_equal, fill=1.0, base=0,
                            pattern=[[-1, P]], channel_multiplier=1)
            p.affine_select(out=before[:], in_=before[:], compare_op=ALU.is_gt, fill=0.0, base=0,
                            pattern=[[1, P]], channel_multiplier=-1)
            pstep(p, p.affine_select(out=valid[:], in_=valid[:], compare_op=ALU.is_gt, fill=0.0, base=N,
                                     pattern=[[-P, TILES]], channel_multiplier=-1))
            p.memset(nib_w[:], 0.0).then_inc(ns.w_zeroed, 1)
            for dst, pattern, start in ((rank_down[:], [[0, TILES], [-1, E]], E), (steps128[:], [[0, E], [P, TILES]], 0),
                                        (slot_iota[:], [[1, SLOTS], [0, E]], 0)):
                p.iota(dst, pattern=pattern, base=start, channel_multiplier=0, allow_small_or_imprecise_dtypes=True)
            pstep(p, p.memset(expert_lt[:], 1.0))
            p.affine_select(out=expert_lt[:], in_=expert_lt[:], compare_op=ALU.is_gt, fill=0.0, base=0,
                            pattern=[[1, E], [-1, E]], channel_multiplier=0)
            pstep(p, p.memset(slot_zero[:], 0.0))
            p.tensor_scalar(invalid_bias[:], valid[:], -1.0, 1e30, ALU.add, ALU.mult).then_inc(consts_ready, 1)
            p.dma_start(slots_in.rearrange("(s p) n -> p s n", p=P), slot_zero[:].rearrange("p (o n) -> p o n", o=1)
                        .to_broadcast([P, SLOTS, D])).then_inc(slots_cleared, 16)
            for x in order:
                if x in gb:
                    graph_pool(p, x)
                elif x == "L0_ffn":
                    nibble_pool(p)
                elif x in ml:
                    moe_pool(p, x, moe_layers.index(x))
                stage_end(p, numbers[x])

        @block.scalar
        def _(a):
            a.wait_ge(consts_ready, 1)
            for x in order:
                if x != "L3b":
                    norm_scalar(a, norm_index[x])
                if x in gb:
                    graph_scalar(a, x)
                elif x == "L0_ffn":
                    nibble_scalar(a)
                elif x in ml:
                    moe_scalar(a, x)
                elif x == "L3_ffn":
                    f_scalar(a)
                stage_end(a, numbers[x])

        @block.vector
        def _(v):
            v.wait_ge(consts_ready, 1)
            v.wait_ge(x_loaded, 32)
            for x in order:
                if x != "L3b":
                    norm_vector(v, resid, norm_index[x])
                if x in gb:
                    graph_vector(v, x)
                elif x == "L0_ffn":
                    nibble_vector(v, rows_at[x])
                elif x in ml:
                    moe_vector(v, x, moe_layers.index(x))
                elif x == "L3_ffn":
                    f_vector(v)
                stage_end(v, numbers[x])

        @block.tensor
        def _(pe):
            pe.wait_ge(consts_ready, 1)
            for x in order:
                if x in gb:
                    graph_tensor(pe, x, rows_at[x])
                elif x == "L0_ffn":
                    nibble_tensor(pe)
                elif x in ml:
                    moe_tensor(pe, x, rows_at[x])
                elif x == "L3_ffn":
                    f_tensor(pe, rows_at[x] + TILES)
                stage_end(pe, numbers[x])


_INPUTS = ("x", "adj", "L0_gnn_W", "L0_gnn_b", "L0_ffn_and_w1", "L0_ffn_and_b1", "L0_ffn_and_w2", "L0_ffn_and_b2",
           "L0_ffn_or_w1", "L0_ffn_or_b1", "L0_ffn_or_w2", "L0_ffn_or_b2", "L0_ffn_xor_w1", "L0_ffn_xor_b1",
           "L0_ffn_xor_w2", "L0_ffn_xor_b2", "L1_gnn_weight", "L1_gnn_bias", "L1_gnn_node_w", "L1_gnn_edge_w",
           "L1_ffn_Wr", "L1_ffn_br", "L1_ffn_W1", "L1_ffn_b1", "L1_ffn_W2", "L1_ffn_b2", "L2_gnn_W", "L2_gnn_a_w",
           "L2_gnn_a_b", "L2_gnn_fc_w", "L2_gnn_fc_b", "L2_ffn_Wg", "L2_ffn_Wgu", "L2_ffn_bgu", "L2_ffn_Wd",
           "L2_ffn_bd", "L3_gnn_W_stack", "L3_ffn_ln_scale", "L3_ffn_ln_bias", "L3_ffn_shared_in_w",
           "L3_ffn_shared_out_w", "L3_ffn_shared_out_b", "L3_ffn_expert_in_w", "L3_ffn_expert_out_weight",
           "L3_ffn_expert_out_bias", "L3_ffn_group_gate_w", "L3_ffn_expert_gate_w", "L3_ffn_group_bias",
           "L3_ffn_expert_bias")


def kernel(**inputs):
    import numpy as np
    import concourse.bacc as bacc
    from concourse.bass_utils import run_bass_kernel_spmd

    nc = bacc.Bacc("TRN2", target_bir_lowering=False, num_devices=1)
    arrays, drams = {}, {}
    for name in _INPUTS:
        a = np.ascontiguousarray(inputs[name])
        if name == "L2_gnn_a_b":
            a = a.reshape(1, 1)
        arrays["in_" + name] = a
        drams[name] = nc.dram_tensor("in_" + name, a.shape, mybir.dt.from_np(a.dtype), kind="ExternalInput").ap()
    result = nc.dram_tensor("result", (N, D), F32, kind="ExternalOutput").ap()
    build(nc, drams, result)
    r = run_bass_kernel_spmd(nc, [arrays], core_ids=[0])
    return r.results[0]["result"]
```

```python
from contextlib import ExitStack

import concourse.bass as bass
from concourse import mybir

F32, F32R, BF16 = mybir.dt.float32, mybir.dt.float32r, mybir.dt.bfloat16
I32, U32 = mybir.dt.int32, mybir.dt.uint32
ALU = mybir.AluOpType
ACT = mybir.ActivationFunctionType
AX = mybir.AxisListType

P = 128
N = 1354
D = 256
KD = D // P
TILES = -(-N // P)
LAST = N - (TILES - 1) * P
NP = TILES * P
BANK = 512
CHUNKS = [(a, min(BANK, N - a)) for a in range(0, N, BANK)]
PCHUNKS = [(a, min(BANK, NP - a)) for a in range(0, NP, BANK)]
GROUPS = [(a, min(4, TILES - a)) for a in range(0, TILES, 4)]
NG = len(GROUPS)
EPS = 1e-5
NEG_BIG = -9e15
LOWEST = -3e38
ROUND = 12582912.0
E = 8
SLOTS = (2 * N + E * (P - 1)) // P
LAG = 2
NPROB, NADJ, NPT, RING = 3, 3, 3, 4
GE = 160
STAGES = ("L0_gnn", "L0_ffn", "L1_gnn", "L1_ffn", "L2_gnn", "L2_ffn", "L3_gnn", "L3_ffn")


def build(nc, d, out, stages=STAGES):
    with ExitStack() as ctx:
        def sem(name):
            return ctx.enter_context(nc.semaphore(name))

        base = (nc.sbuf_base + 31) // 32 * 32
        top = nc.sbuf_usable_end

        class Area:

            def __init__(self, at):
                self.at = at

            def __call__(self, name, shape, dt=F32):
                words = 1
                for s in shape[1:]:
                    words *= s
                t = nc.alloc_sbuf_tensor_at(name, list(shape), dt, offset=self.at)
                self.at += (words * (2 if dt == BF16 else 4) + 31) // 32 * 32
                assert self.at <= top, (name, self.at, top)
                return t

        keep = Area(base)
        resid = keep("resid", [P, TILES, D])
        normed = keep("normed", [P, TILES, D])
        ident = keep("ident", [P, P])
        ones = keep("ones", [P, P])
        before_b = keep("before_b", [P, P], BF16)
        ones_b = keep("ones_b", [P, P], BF16)
        chosen_b = keep("chosen_b", [P, TILES, E], BF16)
        ones3 = keep("ones3", [3, P], BF16)
        valid = keep("valid", [P, TILES])
        invalid_bias = keep("invalid_bias", [P, TILES])
        stats = keep("stats", [P, TILES, 6])
        mean_var = keep("mean_var", [P, TILES, 2])
        var_eps = keep("var_eps", [P, TILES])
        std = keep("std", [P, TILES])
        rstd = keep("rstd", [P, TILES])
        chunk_max = keep("chunk_max", [P, TILES, NG])
        neg_max = keep("neg_max", [P, TILES])
        row_sum = keep("row_sum", [P, TILES])
        row_scale = keep("row_scale", [P, TILES])
        node_att = keep("node_att", [P, TILES])
        node_logit = keep("node_logit", [P, TILES])
        col = keep("col", [P, 4])
        deg_part = keep("deg_part", [P, TILES, 12])
        deg = keep("deg", [P, TILES])
        first = keep("first", [P, TILES, E])
        second = keep("second", [P, TILES, E])
        gate = keep("gate", [P, TILES, 2])
        rank_down = keep("rank_down", [P, TILES, E])
        router_sb = [keep(f"router_sb{i}", [P, TILES, E]) for i in range(3)]
        best = keep("best", [P, TILES, 4])
        pos = keep("pos", [P, 2, TILES])
        steps128 = keep("steps128", [P, E, TILES])
        step_gt = keep("step_gt", [P, E, TILES])
        expert_lt = keep("expert_lt", [P, E, E])
        lt_prod = keep("lt_prod", [P, E, E])
        per_expert = keep("per_expert", [P, 4, E])
        slot_iota = keep("slot_iota", [P, SLOTS, E])
        slot_ge = keep("slot_ge", [P, SLOTS, E])
        slot_f = keep("slot_f", [P, SLOTS])
        slot_expert = keep("slot_expert", [P, SLOTS], I32)
        nib_w = keep("nib_w", [64, 2 * GE + 2])
        place_row = keep("place_row", [P, P])
        place_slot = keep("place_slot", [P, SLOTS])
        spare_row = keep("spare_row", [P, SLOTS])
        tile_p = keep("tile_p", [P, 2, 2, TILES])
        split_pos = keep("split_pos", [P, 2, 2, TILES])
        mapped = keep("mapped", [P, 2, SLOTS])
        source_f = keep("source_f", [P, SLOTS])
        target_f = keep("target_f", [P, SLOTS])
        spare_f = keep("spare_f", [P, SLOTS])
        map_base = keep("map_base", [P, SLOTS])
        source_row = keep("source_row", [P, SLOTS], U32)
        target_row = keep("target_row", [P, SLOTS], U32)
        shared_at = keep.at

        g0 = Area(shared_at)
        turned_hi = g0("turned_hi", [P, KD, NP], F32R)
        turned_lo = g0("turned_lo", [P, KD, NP], F32R)
        w_raw = g0("w_raw", [P, KD, 2 * D + 2])
        w_hi = g0("w_hi", [P, KD, 2 * D + 2], F32R)
        w_lo = g0("w_lo", [P, KD, 2 * D + 2], F32R)
        ATTENTION_BYTES = 4 * (TILES * D * 2 + KD * NP * 2 + NPROB * NP + NADJ * N + 2 * NPT * BANK + N + 4 * D) + 512
        g = Area((top - ATTENTION_BYTES) // 32 * 32)
        attention_at = g.at
        before = Area(attention_at)("before", [P, P])
        values_hi = g("values_hi", [P, TILES, D], F32R)
        values_lo = g("values_lo", [P, TILES, D], F32R)
        q_hi = g("q_hi", [P, KD, NP], F32R)
        q_lo = g("q_lo", [P, KD, NP], F32R)
        probs = g("probs", [P, NPROB, NP])
        adj_rows = g("adj_rows", [P, NADJ, N])
        pt_hi = g("pt_hi", [P, NPT, BANK], F32R)
        pt_lo = g("pt_lo", [P, NPT, BANK], F32R)
        mask_bias = g("mask_bias", [P, 2, N], BF16)
        bias_row = g("bias_row", [P, D])
        biased = g("biased", [P, 3, D])
        k_at = (attention_at - 4 * (3 * N + D + 3 * KD * D + 2 * KD * P) - 512) // 32 * 32
        keys_at = attention_at - 4 * 2 * KD * NP
        g1 = Area(keys_at)
        k_hi = g1("k_hi", [P, KD, NP], F32R)
        k_lo = g1("k_lo", [P, KD, NP], F32R)
        g2 = Area(k_at)
        unscaled = g2("unscaled", [P, TILES, D])
        g3 = Area(k_at)
        s2_row = g3("s2_row", [P, N])
        a_row = g3("a_row", [P, D])
        a_prod = g3("a_prod", [P, 2, KD, D], BF16)
        attn_w = g3("attn_w", [P, 2, KD])
        attn_raw = g3("attn_raw", [P, 2, KD, D])
        rep_hi = g3("rep_hi", [P, KD, P], F32R)
        rep_lo = g3("rep_lo", [P, KD, P], F32R)
        s1 = g3("s1", [P, TILES])
        s1_fifth = g3("s1_fifth", [P, TILES])
        ab = g3("ab", [P, 1])
        leaky = g3("leaky", [P, 2, N])
        assert g0.at <= min(k_at, keys_at) and max(g1.at, g2.at, g3.at) <= attention_at

        n = Area(shared_at)
        bit_w = n("bit_w", [P, TILES, 64])
        bits = n("bits", [P, TILES, 64])
        nib_max = n("nib_max", [P, TILES, 4])
        nib_rev = n("nib_rev", [P, TILES, 4])
        nib = n("nib", [P, TILES, 4])
        opf = n("opf", [P, TILES, 3])
        opn = n("opn", [P, TILES, 2])
        sel = n("sel", [P, TILES, 3])
        active = n("active", [P, TILES, 3])
        feat6 = n("feat6", [P, 2, TILES, 6])
        feats = n("feats", [P, TILES, 64])
        feats_t = n("feats_t", [64, TILES, P])
        hidden = n("hidden", [P, 2, GE])
        nib_prod = n("nib_prod", [P, 2, GE])
        res_b = n("res_b", [P, TILES, 2])
        res = n("res", [P, TILES, 2])
        digit = n("digit", [P, 2 * TILES, 16])
        onehot = n("onehot", [P, 2 * TILES, 16])

        m = Area(shared_at)
        expert_w = m("expert_w", [P, E * 4096])
        logits_t = Area(m.at)("logits_t", [E, NP])
        bias3 = m("bias3", [3, E * 1280], BF16)
        m_at = m.at
        mturned_hi = m("mturned_hi", [P, KD, NP], F32R)
        mturned_lo = m("mturned_lo", [P, KD, NP], F32R)
        m2 = Area(m_at)
        slot_x = m2("slot_x", [P, 2, D])
        slot_xt = m2("slot_xt", [P, 2, KD, P])
        slot_h = m2("slot_h", [P, 2, 1024])
        slot_ht = m2("slot_ht", [P, 1024])
        slot_silu = m2("slot_silu", [P, BANK])
        slot_y = m2("slot_y", [P, 2, D])
        m5 = Area(m_at + 4 * 4 * D)
        place_hot = m5("place_hot", [P, 2 * TILES, P], BF16)
        slot_hot = m5("slot_hot", [P, 2 * TILES, SLOTS], BF16)
        slot_vals = m5("slot_vals", [P, 2 * TILES, 2, SLOTS], BF16)
        m3 = Area(max(m.at, m2.at, m5.at))
        router_raw = m3("router_raw", [P, KD, E])
        router_hi = m3("router_hi", [P, KD, E], F32R)
        router_lo = m3("router_lo", [P, KD, E], F32R)
        router_b = m3("router_b", [P, E])
        split_f = m3("split_f", [80, 3, P])
        split_b = m3("split_b", [80, 3, P], BF16)
        m4 = Area(shared_at)
        gathered = m4("gathered", [P, TILES, 2, D])

        f = Area(shared_at)
        nat_in = f("nat_in", [P, 2, 8, D])
        nat_out = f("nat_out", [P, E + 1, KD, BANK])
        assert f.at <= keys_at, (f.at, keys_at)
        f1 = Area(shared_at)
        act_silu = f1("act_silu", [P, 2, BANK])
        act_h = f1("act_h", [P, 2, BANK])
        act_t_hi = f1("act_t_hi", [P, 2, BANK], F32R)
        act_t_lo = f1("act_t_lo", [P, 2, BANK], F32R)
        f_turned_hi = f1("f_turned_hi", [P, KD, NP], F32R)
        f_turned_lo = f1("f_turned_lo", [P, KD, NP], F32R)
        f.at = max(f.at, f1.at)
        in_hi = f("in_hi", [P, 2, KD, 1024], F32R)
        in_lo = f("in_lo", [P, 2, KD, 1024], F32R)
        out_hi = f("out_hi", [P, 4, 9 * D], F32R)
        out_lo = f("out_lo", [P, 4, 9 * D], F32R)
        gate_nat = f("gate_nat", [E + 2, D])
        gate_hi = f("gate_hi", [P, KD, E + 2], F32R)
        gate_lo = f("gate_lo", [P, KD, E + 2], F32R)
        ln_rows = f("ln_rows", [P, 2, D])
        gate_b = f("gate_b", [P, E + 2])
        glog = f("glog", [P, TILES, E + 2])
        grp = f("grp", [P, TILES, 2])
        esel = f("esel", [P, 6, TILES, 4])
        pk = f("pk", [P, TILES, 4])
        comb = f("comb", [P, TILES, E])
        psel = f("psel", [P, 4, TILES])
        cnt = f("cnt", [P, TILES, E + 1])
        f_logits_t = Area(f.at)("f_logits_t", [E + 2, NP])
        cnt_t = f("cnt_t", [E + 1, TILES, P])
        bias9 = f("bias9", [E + 1, D])

        psum = ctx.enter_context(nc.psum_tensor("psum", [P, 8, BANK], F32))

        x_rows = nc.dram_tensor("x_rows", [NP, D], F32).ap()
        y_rows = nc.dram_tensor("y_rows", [2 * NP + SLOTS * P, D], F32).ap()
        bias_scratch = nc.dram_tensor("bias_scratch", [3, E * 1280], BF16).ap()

        stage_done = sem("stage_done")
        vector_step = sem("vector_step")
        scalar_step = sem("scalar_step")
        pool_step = sem("pool_step")
        consts_ready = sem("consts_ready")
        x_loaded = [sem(f"x_loaded{i}") for i in range(NG)]
        padding_zeroed = sem("padding_zeroed")
        out_stored = sem("out_stored")
        var_ready = sem("var_ready")
        std_ready = sem("std_ready")
        rows_normed = sem("rows_normed")
        block = ctx.enter_context(nc.Block())

        counts = {"v": 0, "s": 0, "p": 0, "norms": 0}

        def vstep(v, ins):
            counts["v"] += 1
            ins.then_inc(vector_step, 1)
            v.wait_ge(vector_step, counts["v"])

        def sstep(a, ins):
            counts["s"] += 1
            ins.then_inc(scalar_step, 1)
            a.wait_ge(scalar_step, counts["s"])

        def pstep(p, ins):
            counts["p"] += 1
            ins.then_inc(pool_step, 1)
            p.wait_ge(pool_step, counts["p"])

        def stage_end(eng, number):
            eng.drain().then_inc(stage_done, 1)
            eng.wait_ge(stage_done, 4 * number)

        def graph_items(layer):
            items = [("turn", i) for i in range(0, TILES, 2)]
            items.insert(2, ("weights",))
            if layer in ("L1_gnn", "L3a", "L3b"):
                items += [("features", "q", mb, c) for c in range(3) for mb in range(KD)]
            if layer in ("L3a", "L3b"):
                items += [("features", "k", mb, c) for c in range(3) for mb in range(KD)]
            items += [("values", t) for t in range(TILES)]
            if layer == "L2_gnn":
                items += [("s2", c) for c in range(3)]
            return items

        graph_layers = [s for s in stages if s.endswith("gnn")]
        graph_layers = [x for s in graph_layers for x in (("L3a", "L3b") if s == "L3_gnn" else (s,))]
        moe_layers = [s for s in stages if s in ("L1_ffn", "L2_ffn")]
        w_cols = {"L0_gnn": D, "L1_gnn": 2 * D + 2, "L2_gnn": D + 2, "L3a": 2 * D, "L3b": 2 * D}
        v_col = {"L0_gnn": 0, "L1_gnn": D, "L2_gnn": 0, "L3a": 0, "L3b": 0}

        class gs:
            w_loaded = sem("w_loaded")
            adj_loaded = [sem(f"adj_loaded{i}") for i in range(NADJ)]
            cleared = sem("cleared")
            item_ready = sem("item_ready")
            item_hi = sem("item_hi")
            item_done = sem("item_done")
            scores_ready = sem("scores_ready")
            scores_free = sem("scores_free")
            max_ready = sem("max_ready")
            exp_done = sem("exp_done")
            probs_ready = sem("probs_ready")
            adj_used = sem("adj_used")
            turned = sem("turned")
            pt_hi_ready = sem("pt_hi_ready")
            pt_ready = sem("pt_ready")
            pt_used = sem("pt_used")
            mixed_taken = sem("mixed_taken")
            node_max = sem("node_max")
            node_exp = sem("node_exp")
            node_sum = sem("node_sum")
            attn_split = sem("attn_split")
            biased_ready = sem("biased_ready")
            leaky_used = sem("leaky_used")
        w_dmas = {"L0_gnn": 2, "L1_gnn": 4, "L2_gnn": 5, "L3a": 1, "L3b": 1}

        def graph_counts(x):
            scored, items = x in ("L1_gnn", "L3a", "L3b"), len(graph_items(x))
            return dict(
                w_loaded=16 * w_dmas[x], cleared=1, item_ready=items - 1, item_hi=items, item_done=items,
                scores_ready=NG * TILES if scored else TILES if x == "L2_gnn" else 0,
                scores_free=NG * TILES if scored else 0, max_ready=TILES if x != "L0_gnn" else 0,
                exp_done=TILES if scored else 0, probs_ready=TILES, adj_used=TILES if x == "L2_gnn" else 0,
                turned=NG * TILES, pt_hi_ready=NG * TILES, pt_ready=NG * TILES, pt_used=NG * TILES,
                mixed_taken=TILES, node_max=2 if x == "L1_gnn" else 0, node_exp=1 if x == "L1_gnn" else 0,
                node_sum=1 if x == "L1_gnn" else 0, attn_split=KD if x == "L2_gnn" else 0,
                biased_ready=TILES + (x == "L2_gnn") if x in ("L0_gnn", "L2_gnn") else 0, leaky_used=TILES if x == "L2_gnn" else 0)

        gb = {}
        so_far, adj_so_far = {name: 0 for name in graph_counts("L0_gnn")}, [0] * NADJ
        for x in graph_layers:
            gb[x] = dict(adj_loaded=list(adj_so_far), **so_far)
            so_far = {name: so_far[name] + n_ for name, n_ in graph_counts(x).items()}
            adj_so_far = [adj_so_far[i] + 16 * len(range(i, TILES, NADJ)) for i in range(NADJ)]
        ml = {}
        for x in moe_layers:
            class sems:
                w_loaded = sem(f"{x}_w_loaded")
                r_loaded = sem(f"{x}_r_loaded")
                b_loaded = sem(f"{x}_b_loaded")
                b_split = sem(f"{x}_b_split")
                b_placed = sem(f"{x}_b_placed")
                b_spread = sem(f"{x}_b_spread")
                item_ready = sem(f"{x}_item_ready")
                item_hi = sem(f"{x}_item_hi")
                item_done = sem(f"{x}_item_done")
                logits = sem(f"{x}_logits")
                gap = sem(f"{x}_gap")
                gap_exp = sem(f"{x}_gap_exp")
                chosen = sem(f"{x}_chosen")
                counted = sem(f"{x}_counted")
                placed = sem(f"{x}_placed")
                rows_stored = sem(f"{x}_rows_stored")
                hot_ready = sem(f"{x}_hot_ready")
                mapped = sem(f"{x}_mapped")
                sources_ready = sem(f"{x}_sources_ready")
                x_loaded = [sem(f"{x}_x_loaded{i}") for i in range(2)]
                x_turned = sem(f"{x}_x_turned")
                xt_ready = sem(f"{x}_xt_ready")
                h_ready = sem(f"{x}_h_ready")
                silu_ready = sem(f"{x}_silu_ready")
                silu_used = sem(f"{x}_silu_used")
                h_kept_s = sem(f"{x}_h_kept_s")
                h_kept_v = sem(f"{x}_h_kept_v")
                h_turned = sem(f"{x}_h_turned")
                ht_ready_s = sem(f"{x}_ht_ready_s")
                ht_ready_v = sem(f"{x}_ht_ready_v")
                y_ready = sem(f"{x}_y_ready")
                y_kept = sem(f"{x}_y_kept")
                y_stored = [sem(f"{x}_y_stored{i}") for i in range(2)]
            ml[x] = sems
        if moe_layers:
            y_loaded = [sem(f"y_loaded{i}") for i in range(NG)]

        class ns:
            w_zeroed = sem("nib_w_zeroed")
            w_loaded = sem("nib_w_loaded")
            feats_ready = sem("nib_feats_ready")
            turned = sem("nib_turned")
            turned_kept = sem("nib_turned_kept")
            hidden = sem("nib_hidden")
            relu = sem("nib_relu")
            used = sem("nib_used")
            iota = sem("nib_iota")
        class fs:
            loaded = sem("f_loaded")
            in_loaded = [sem(f"f_in_loaded{i}") for i in range(2)]
            out_loaded = sem("f_out_loaded")
            item_ready = sem("f_item_ready")
            item_hi = sem("f_item_hi")
            item_done = sem("f_item_done")
            logits = sem("f_logits")
            exp_in = sem("f_exp_in")
            exp_out = sem("f_exp_out")
            cnt_ready = sem("f_cnt_ready")
            cnt_turned = sem("f_cnt_turned")
            cnt_kept = sem("f_cnt_kept")
            h_ready = sem("f_h_ready")
            silu = sem("f_silu")
            h_kept = sem("f_h_kept")
            h_turned = sem("f_h_turned")
            ht_hi = sem("f_ht_hi")
            ht_done = sem("f_ht_done")
            ht_used = sem("f_ht_used")
            y_ready = sem("f_y_ready")
            y_used = sem("f_y_used")

        def pairs(hi, lo):
            return lambda *ix: (hi[ix], lo[ix])

        def product(eng, o, lhs, rhs, start, stop):
            eng.matmul(o, lhs[0], rhs[0], start=start, stop=False)
            eng.matmul(o, lhs[0], rhs[1], start=False, stop=False)
            return eng.matmul(o, lhs[1], rhs[0], start=False, stop=stop)

        def row_stats(v, t):
            v.bn_stats(stats[:, t, :], resid[:, t, :])

        def norm_vector(v, src, index):
            vstep(v, v.engine_nop())
            for t in range(TILES):
                ins = v.bn_aggr(mean_var[:, t, :], stats[:, t, :])
            vstep(v, ins)
            v.tensor_scalar(var_eps[:], mean_var[:, :, 1], EPS, None, ALU.add).then_inc(var_ready, 1)
            v.wait_ge(std_ready, index + 1)
            vstep(v, v.reciprocal(rstd[:], std[:]))
            for t in range(TILES):
                v.tensor_scalar(normed[:, t, :], src[:, t, :], mean_var[:, t, 0:1], rstd[:, t:t + 1],
                                ALU.subtract, ALU.mult).then_inc(rows_normed, 1)

        def norm_scalar(a, index):
            a.wait_ge(var_ready, index + 1)
            a.activation(std[:], var_eps[:], ACT.Sqrt).then_inc(std_ready, 1)

        def ring_free(eng, done, k, start=0):
            if k >= RING:
                eng.wait_ge(done, start + k - RING + 1)

        def turn_tensor(pe, i, k, wait_rows):
            for j in range(min(2, TILES - i)):
                pe.wait_ge(rows_normed, wait_rows + i + j + 1)
                for kb in range(KD):
                    ins = pe.transpose(psum[:, k % RING, kb * 256 + j * P:kb * 256 + (j + 1) * P],
                                       normed[:, i + j, kb * P:(kb + 1) * P], ident[:])
            return ins

        def turn_source(i, k):
            w = min(2, TILES - i) * P
            return psum[:, k % RING, :].rearrange("p (k n) -> p k n", k=KD)[:, :, 0:w], slice(i * P, i * P + w)

        def graph_tensor(pe, x, rows_base):
            s, b, items = gs, gb[x], graph_items(x)
            where = {it: k for k, it in enumerate(items)}
            turned, w = pairs(turned_hi, turned_lo), pairs(w_hi, w_lo)
            for k, it in enumerate(items):
                if it[0] == "weights":
                    continue
                ring_free(pe, s.item_done, k, b["item_done"])
                if it[0] == "turn":
                    ins = turn_tensor(pe, it[1], k, rows_base)
                elif it[0] == "features":
                    _, dst, mb, c = it
                    a, width = PCHUNKS[c]
                    last = max(where[("turn", min(4 * c + 2, (TILES - 1) // 2 * 2))], where[("weights",)])
                    pe.wait_ge(s.item_done, b["item_done"] + last + 1)
                    off = (D if dst == "k" else 0) + mb * P
                    for kb in range(KD):
                        ins = product(pe, psum[:, k % RING, 0:width], w(slice(None), kb, slice(off, off + P)),
                                      turned(slice(None), kb, slice(a, a + width)), kb == 0, kb == KD - 1)
                elif it[0] == "values":
                    t = it[1]
                    last = max(where[("turn", t // 2 * 2)], where[("weights",)])
                    pe.wait_ge(s.item_done, b["item_done"] + last + 1)
                    width = D + 2 if x in ("L1_gnn", "L2_gnn") else D
                    for kb in range(KD):
                        ins = product(pe, psum[:, k % RING, 0:width], turned(slice(None), kb, slice(t * P, t * P + P)),
                                      w(slice(None), kb, slice(v_col[x], v_col[x] + width)), kb == 0, kb == KD - 1)
                elif it[0] == "s2":
                    a, width = CHUNKS[it[1]]
                    pe.wait_ge(s.attn_split, b["attn_split"] + KD)
                    for kb in range(KD):
                        ins = product(pe, psum[:, k % RING, 0:width], pairs(rep_hi, rep_lo)(slice(None), kb, slice(None)),
                                      turned(slice(None), kb, slice(a, a + width)), kb == 0, kb == KD - 1)
                ins.then_inc(s.item_ready, 1)
            pe.wait_ge(s.item_done, b["item_done"] + len(items))

            q = pairs(q_hi, q_lo)
            keys = pairs(k_hi, k_lo) if x in ("L3a", "L3b") else q
            scored = x in ("L1_gnn", "L3a", "L3b")
            pt, vals = pairs(pt_hi, pt_lo), pairs(values_hi, values_lo)

            def scores(r):
                for c, (a, width) in enumerate(CHUNKS):
                    n_ = r * NG + c
                    if n_ >= RING:
                        pe.wait_ge(s.scores_free, b["scores_free"] + n_ - RING + 1)
                    for kb in range(KD):
                        ins = product(pe, psum[:, n_ % RING, 0:width], q(slice(None), kb, slice(r * P, r * P + P)),
                                      keys(slice(None), kb, slice(a, a + width)), kb == 0, kb == KD - 1)
                    ins.then_inc(s.scores_ready, 1)

            def turn(r, c):
                n_ = r * NG + c
                if n_ >= 2:
                    pe.wait_ge(s.pt_ready, b["pt_ready"] + n_ - 1)
                a, w_ = GROUPS[c]
                for j in range(w_):
                    ins = pe.transpose(psum[:, 4 + n_ % 2, j * P:(j + 1) * P],
                                       probs[:, r % NPROB, (a + j) * P:(a + j + 1) * P], ident[:])
                ins.then_inc(s.turned, 1)

            def mix(r, c):
                n_ = r * NG + c
                pe.wait_ge(s.pt_ready, b["pt_ready"] + n_ + 1)
                a, w_ = GROUPS[c]
                o = psum[:, 6 + r % 2, 0:D]
                for j in range(w_):
                    l = pt(slice(None), n_ % NPT, slice(j * P, (j + 1) * P))
                    rr = vals(slice(None), a + j, slice(None))
                    st, sp = c == 0 and j == 0, c == NG - 1 and j == w_ - 1
                    if x == "L0_gnn":
                        pe.matmul(o, l[0], rr[0], start=st, stop=False)
                        ins = pe.matmul(o, l[0], rr[1], start=False, stop=sp)
                    else:
                        ins = product(pe, o, l, rr, st, sp)
                ins.then_inc(s.pt_used, 1)

            pe.wait_ge(s.cleared, b["cleared"] + 1)
            for i in range(TILES + LAG):
                r = i - LAG
                if r >= 0:
                    pe.wait_ge(s.probs_ready, b["probs_ready"] + r + 1)
                    turn(r, 0)
                    turn(r, 1)
                if i < TILES and scored:
                    scores(i)
                if r >= 0:
                    if r >= 2:
                        pe.wait_ge(s.mixed_taken, b["mixed_taken"] + r - 1)
                    mix(r, 0)
                    turn(r, 2)
                    mix(r, 1)
                    mix(r, 2)

        def graph_scalar(a, x):
            s, b, items = gs, gb[x], graph_items(x)
            n_pe = 0
            for k, it in enumerate(items):
                if it[0] == "weights":
                    a.wait_ge(s.w_loaded, b["w_loaded"] + 16 * w_dmas[x])
                    a.wait_ge(s.cleared, b["cleared"] + 1)
                    if x == "L2_gnn":
                        a.wait_ge(s.attn_split, b["attn_split"] + KD)
                    a.copy(w_hi[:, :, 0:w_cols[x]], w_raw[:, :, 0:w_cols[x]]).then_inc(s.item_hi, 1)
                    continue
                n_pe += 1
                a.wait_ge(s.item_ready, b["item_ready"] + n_pe)
                bank = psum[:, k % RING, :]
                if it[0] == "turn":
                    src, cols = turn_source(it[1], k)
                    ins = a.copy(turned_hi[:, :, cols], src)
                elif it[0] == "features":
                    _, dst, mb, c = it
                    at, width = PCHUNKS[c]
                    ins = a.copy((q_hi if dst == "q" else k_hi)[:, mb, at:at + width], bank[:, 0:width])
                elif it[0] == "values":
                    if x in ("L0_gnn", "L2_gnn"):
                        a.wait_ge(s.biased_ready, b["biased_ready"] + it[1] + 1)
                        ins = a.copy(values_hi[:, it[1], :], biased[:, it[1] % 3, :])
                    else:
                        ins = a.copy(values_hi[:, it[1], :], bank[:, 0:D])
                else:
                    at, width = CHUNKS[it[1]]
                    ins = a.copy(s2_row[:, at:at + width], bank[:, 0:width])
                ins.then_inc(s.item_hi, 1)
            if x == "L1_gnn":
                a.wait_ge(s.node_max, b["node_max"] + 2)
                a.activation(node_att[:], node_logit[:], ACT.Exp, bias=col[:, 1:2],
                             accum_out=col[:, 2:3]).then_inc(s.node_exp, 1)
            if x == "L2_gnn":
                a.wait_ge(s.item_done, b["item_done"] + len(items))
                a.wait_ge(s.biased_ready, b["biased_ready"] + TILES + 1)

            def slope(r):
                if r >= 2:
                    a.wait_ge(s.leaky_used, b["leaky_used"] + r - 1)
                a.activation(leaky[:, r % 2, :], s2_row[:], ACT.Identity, bias=s1_fifth[:, r:r + 1],
                             scale=0.2).then_inc(s.scores_ready, 1)

            def exp(r):
                a.wait_ge(s.max_ready, b["max_ready"] + r + 1)
                a.activation(probs[:, r % NPROB, 0:N], probs[:, r % NPROB, 0:N], ACT.Exp, bias=neg_max[:, r:r + 1],
                             accum_out=row_sum[:, r:r + 1]).then_inc(s.exp_done if x != "L2_gnn" else s.probs_ready, 1)

            def hi(r, c):
                n_ = r * NG + c
                a.wait_ge(s.turned, b["turned"] + n_ + 1)
                if n_ >= NPT:
                    a.wait_ge(s.pt_used, b["pt_used"] + n_ - NPT + 1)
                w_ = GROUPS[c][1] * P
                a.copy(pt_hi[:, n_ % NPT, 0:w_], psum[:, 4 + n_ % 2, 0:w_]).then_inc(s.pt_hi_ready, 1)

            for i in range(TILES + LAG):
                if x == "L2_gnn" and i < TILES:
                    slope(i)
                if i >= LAG:
                    hi(i - LAG, 0)
                    hi(i - LAG, 1)
                if x != "L0_gnn" and 1 <= i <= TILES:
                    exp(i - 1)
                if i >= LAG:
                    hi(i - LAG, 2)

        def graph_vector(v, x):
            s, b, items = gs, gb[x], graph_items(x)
            masked = x == "L1_gnn"
            if x == "L2_gnn":
                v.wait_ge(s.w_loaded, b["w_loaded"] + 16 * w_dmas[x])
                v.wait_ge(s.cleared, b["cleared"] + 1)
                for half in range(2):
                    for kb in range(KD):
                        to = w_raw[:, kb, D:D + 1] if half == 0 else attn_w[:, 1, kb:kb + 1]
                        ins = v.tensor_tensor_reduce(a_prod[:, half, kb, :], attn_raw[:, half, kb, :], a_row[:], 1.0, 0.0,
                                                     ALU.mult, ALU.add, to)
                vstep(v, ins)
                for kb in range(KD):
                    vstep(v, v.tensor_scalar(rep_hi[:, kb, :], ones[:], attn_w[:, 1, kb:kb + 1], None, ALU.mult))
                    v.scalar_tensor_tensor(rep_lo[:, kb, :], ones[:], attn_w[:, 1, kb:kb + 1],
                                           rep_hi[:, kb, :].bitcast(F32), ALU.mult, ALU.subtract).then_inc(s.attn_split, 1)
            n_pe = 0

            def add_bias(t, k, nth):
                bank = psum[:, k % RING, :]
                v.wait_ge(s.w_loaded, b["w_loaded"] + 16 * w_dmas[x])
                v.wait_ge(s.item_ready, b["item_ready"] + nth)
                if x == "L2_gnn":
                    v.tensor_scalar(s1[:, t:t + 1], bank[:, D:D + 1], ab[:, 0:1], None, ALU.add)
                v.tensor_tensor(biased[:, t % 3, :], bank[:, 0:D], bias_row[:], ALU.add).then_inc(s.biased_ready, 1)

            for k, it in enumerate(items):
                bank = psum[:, k % RING, :]
                n_pe += it[0] != "weights"
                if it[0] == "values" and x in ("L0_gnn", "L2_gnn"):
                    t = it[1]
                    if t == 0:
                        add_bias(0, k, n_pe)
                    if t + 1 < TILES:
                        if t >= 2:
                            v.wait_ge(s.item_done, b["item_done"] + k - 1)
                        add_bias(t + 1, k + 1, n_pe + 1)
                    v.wait_ge(s.item_hi, b["item_hi"] + k + 1)
                    v.tensor_tensor(values_lo[:, t, :], biased[:, t % 3, :], values_hi[:, t, :].bitcast(F32),
                                    ALU.subtract).then_inc(s.item_done, 1)
                    continue
                v.wait_ge(s.item_hi, b["item_hi"] + k + 1)
                if it[0] == "weights":
                    ins = v.tensor_tensor(w_lo[:, :, 0:w_cols[x]], w_raw[:, :, 0:w_cols[x]],
                                          w_hi[:, :, 0:w_cols[x]].bitcast(F32), ALU.subtract)
                elif it[0] == "turn":
                    src, cols = turn_source(it[1], k)
                    ins = v.tensor_tensor(turned_lo[:, :, cols], src, turned_hi[:, :, cols].bitcast(F32), ALU.subtract)
                elif it[0] == "features":
                    _, dst, mb, c = it
                    at, width = PCHUNKS[c]
                    h_, l_ = (q_hi, q_lo) if dst == "q" else (k_hi, k_lo)
                    ins = v.tensor_tensor(l_[:, mb, at:at + width], bank[:, 0:width],
                                          h_[:, mb, at:at + width].bitcast(F32), ALU.subtract)
                elif it[0] == "values":
                    t = it[1]
                    if x == "L1_gnn":
                        v.tensor_copy(node_logit[:, t:t + 1], bank[:, D:D + 1])
                    ins = v.tensor_tensor(values_lo[:, t, :], bank[:, 0:D], values_hi[:, t, :].bitcast(F32), ALU.subtract)
                else:
                    ins = v.engine_nop()
                ins.then_inc(s.item_done, 1)
            if x == "L2_gnn":
                v.tensor_scalar(s1_fifth[:], s1[:], 0.2, None, ALU.mult).then_inc(s.biased_ready, 1)
            v.wait_ge(s.item_done, b["item_done"] + len(items))
            if x == "L1_gnn":
                vstep(v, v.tensor_tensor(node_logit[:], node_logit[:], valid[:], ALU.mult))
                vstep(v, v.tensor_tensor(node_logit[:], node_logit[:], invalid_bias[:], ALU.add))
                v.tensor_reduce(col[:, 0:1], node_logit[:], AX.X, ALU.max).then_inc(s.node_max, 1)

            def leaky_scores(r):
                pr = probs[:, r % NPROB, 0:N]
                if r >= NPROB:
                    v.wait_ge(s.turned, b["turned"] + (r - NPROB + 1) * NG)
                v.wait_ge(s.scores_ready, b["scores_ready"] + r + 1)
                v.scalar_tensor_tensor(pr, s2_row[:], s1[:, r:r + 1], leaky[:, r % 2, :],
                                       ALU.add, ALU.max).then_inc(s.leaky_used, 1)

            def masked_max(r):
                pr, mb = probs[:, r % NPROB, 0:N], mask_bias[:, r % 2, :]
                v.wait_ge(s.leaky_used, b["leaky_used"] + r + 1)
                v.wait_ge(s.adj_used, b["adj_used"] + r + 1)
                vstep(v, v.tensor_tensor_reduce(pr, pr, mb, 1.0, LOWEST, ALU.add, ALU.max, chunk_max[:, r, 0:1]))
                v.tensor_scalar(neg_max[:, r:r + 1], chunk_max[:, r, 0:1], -1.0, None, ALU.mult).then_inc(s.max_ready, 1)

            def front(r):
                pr, ad = probs[:, r % NPROB, 0:N], adj_rows[:, r % NADJ, :]
                if r >= NPROB:
                    v.wait_ge(s.turned, b["turned"] + (r - NPROB + 1) * NG)
                if x == "L0_gnn":
                    v.wait_ge(s.adj_loaded[r % NADJ], b["adj_loaded"][r % NADJ] + 16 * (r // NADJ + 1))
                    v.tensor_scalar(pr, ad, 0.0, None, ALU.not_equal).then_inc(s.probs_ready, 1)
                    return
                mb = mask_bias[:, r % 2, :]
                if x == "L1_gnn":
                    v.wait_ge(s.adj_loaded[r % NADJ], b["adj_loaded"][r % NADJ] + 16 * (r // NADJ + 1))
                    vstep(v, v.tensor_scalar(mb, ad, 0.0, NEG_BIG, ALU.is_le, ALU.mult))
                for c, (at, width) in enumerate(CHUNKS):
                    n_ = r * NG + c
                    v.wait_ge(s.scores_ready, b["scores_ready"] + n_ + 1)
                    bank = psum[:, n_ % RING, 0:width]
                    if masked:
                        ins = v.tensor_tensor_reduce(pr[:, at:at + width], bank, mb[:, at:at + width], 1.0, LOWEST,
                                                     ALU.add, ALU.max, chunk_max[:, r, c:c + 1])
                    else:
                        ins = v.tensor_scalar(pr[:, at:at + width], bank, 1.0, None, ALU.mult, ALU.max,
                                              accum_out=chunk_max[:, r, c:c + 1])
                    ins.then_inc(s.scores_free, 1)
                v.wait_ge(s.scores_free, b["scores_free"] + (r + 1) * NG)
                v.tensor_reduce(neg_max[:, r:r + 1], chunk_max[:, r, :], AX.X, ALU.max, negate=True).then_inc(s.max_ready, 1)

            def lo(r, c):
                n_ = r * NG + c
                v.wait_ge(s.pt_hi_ready, b["pt_hi_ready"] + n_ + 1)
                a_, w_ = GROUPS[c]
                if x == "L0_gnn":
                    rows = LAST if r == TILES - 1 else P
                    v.tensor_reduce(deg_part[:, r, a_:a_ + w_],
                                    psum[:, 4 + n_ % 2, 0:w_ * P].rearrange("p (b n) -> p b n", n=P)[:, :, 0:rows],
                                    AX.X, ALU.add).then_inc(s.pt_ready, 1)
                else:
                    v.tensor_tensor(pt_lo[:, n_ % NPT, 0:w_ * P], psum[:, 4 + n_ % 2, 0:w_ * P],
                                    pt_hi[:, n_ % NPT, 0:w_ * P].bitcast(F32), ALU.subtract).then_inc(s.pt_ready, 1)

            def back(r):
                v.wait_ge(s.pt_used, b["pt_used"] + (r + 1) * NG)
                o = psum[:, 6 + r % 2, 0:D]
                if x == "L0_gnn":
                    v.tensor_copy(unscaled[:, r, :], o).then_inc(s.mixed_taken, 1)
                    return
                vstep(v, v.reciprocal(row_scale[:, r:r + 1], row_sum[:, r:r + 1]))
                if x == "L1_gnn":
                    vstep(v, v.tensor_tensor(row_scale[:, r:r + 1], row_scale[:, r:r + 1], node_att[:, r:r + 1], ALU.mult))
                if x in ("L1_gnn", "L2_gnn"):
                    v.scalar_tensor_tensor(resid[:, r, :], o, row_scale[:, r:r + 1], resid[:, r, :],
                                           ALU.mult, ALU.add).then_inc(s.mixed_taken, 1)
                else:
                    ins = v.scalar_tensor_tensor(normed[:, r, :], o, row_scale[:, r:r + 1], normed[:, r, :],
                                                 ALU.mult, ALU.add)
                    ins.then_inc(s.mixed_taken, 1)
                    v.wait_ge(s.mixed_taken, b["mixed_taken"] + r + 1)
                    v.scalar_tensor_tensor(normed[:, r, :], normed[:, r, :], 0.01, normed[:, r, :],
                                           ALU.mult, ALU.max).then_inc(rows_normed, 1)
                    if x == "L3b":
                        v.wait_ge(rows_normed, counts["rows_end_" + x] - TILES + r + 1)
                        vstep(v, v.tensor_tensor(resid[:, r, :], resid[:, r, :], normed[:, r, :], ALU.add))
                        row_stats(v, r)

            for i in range(TILES + LAG + 1):
                if LAG <= i < TILES + LAG:
                    lo(i - LAG, 0)
                    lo(i - LAG, 1)
                if x == "L2_gnn" and i < TILES:
                    leaky_scores(i)
                if LAG <= i < TILES + LAG:
                    lo(i - LAG, 2)
                if i > LAG:
                    back(i - LAG - 1)
                if x == "L2_gnn" and i < TILES:
                    masked_max(i)
                elif i < TILES:
                    front(i)
                if x == "L1_gnn" and i == 1:
                    v.wait_ge(s.node_sum, b["node_sum"] + 1)
                    vstep(v, v.reciprocal(col[:, 3:4], col[:, 3:4]))
                    vstep(v, v.tensor_scalar(node_att[:], node_att[:], col[:, 3:4], None, ALU.mult))
                if i > LAG + 1 and x in ("L1_gnn", "L2_gnn"):
                    v.wait_ge(s.mixed_taken, b["mixed_taken"] + i - LAG - 1)
                    row_stats(v, i - LAG - 2)
            if x in ("L1_gnn", "L2_gnn"):
                v.wait_ge(s.mixed_taken, b["mixed_taken"] + TILES)
                row_stats(v, TILES - 1)
            if x == "L0_gnn":
                v.wait_ge(s.pt_ready, b["pt_ready"] + TILES * NG)
                vstep(v, v.tensor_reduce(deg[:], deg_part[:, :, 0:TILES].rearrange("p r b -> p b r"), AX.X, ALU.add))
                vstep(v, v.scalar_tensor_tensor(deg[:], valid[:], -1.0, deg[:], ALU.mult, ALU.add))
                vstep(v, v.tensor_scalar(deg[:], deg[:], 1.0, None, ALU.add))
                vstep(v, v.reciprocal(row_scale[:], deg[:]))
                v.wait_ge(s.mixed_taken, b["mixed_taken"] + TILES)
                for t in range(TILES):
                    ins = v.scalar_tensor_tensor(resid[:, t, :], unscaled[:, t, :], row_scale[:, t:t + 1],
                                                 resid[:, t, :], ALU.mult, ALU.add)
                vstep(v, ins)
                for t in range(TILES):
                    row_stats(v, t)

        def graph_pool(p, x):
            s, b = gs, gb[x]
            p.memset({"L1_gnn": w_raw[:, :, 2 * D + 1:2 * D + 2], "L2_gnn": w_raw[:, :, D:D + 2]}.get(
                x, w_raw[:, :, 2 * D:2 * D + 2]), 0.0)
            p.memset(probs[:, :, N:NP], 0.0).then_inc(s.cleared, 1)
            if x == "L1_gnn":
                p.wait_ge(s.node_max, b["node_max"] + 1)
                pstep(p, p.partition_all_reduce(col[:, 1:2], col[:, 0:1], P, bass.bass_isa.ReduceOp.max))
                p.tensor_scalar(col[:, 1:2], col[:, 1:2], -1.0, 0.0, ALU.mult, ALU.add).then_inc(s.node_max, 1)
                p.wait_ge(s.w_loaded, b["w_loaded"] + 16 * w_dmas[x])
                for t in range(TILES):
                    ins = p.tensor_tensor(resid[:, t, :], resid[:, t, :], bias_row[:], ALU.add)
                p.wait_ge(s.node_exp, b["node_exp"] + 1)
                p.partition_all_reduce(col[:, 3:4], col[:, 2:3], P, bass.bass_isa.ReduceOp.add).then_inc(s.node_sum, 1)
            if x == "L2_gnn":
                for r in range(TILES):
                    p.wait_ge(s.adj_loaded[r % NADJ], b["adj_loaded"][r % NADJ] + 16 * (r // NADJ + 1))
                    if r >= 2:
                        p.wait_ge(s.max_ready, b["max_ready"] + r - 1)
                    p.tensor_scalar(mask_bias[:, r % 2, :], adj_rows[:, r % NADJ, :], 0.0, NEG_BIG,
                                    ALU.is_le, ALU.mult).then_inc(s.adj_used, 1)
            if x in ("L1_gnn", "L3a", "L3b"):
                for r in range(TILES):
                    p.wait_ge(s.exp_done, b["exp_done"] + r + 1)
                    p.wait_ge(s.adj_loaded[r % NADJ], b["adj_loaded"][r % NADJ] + 16 * (r // NADJ + 1))
                    ins = p.tensor_tensor(probs[:, r % NPROB, 0:N], probs[:, r % NPROB, 0:N], adj_rows[:, r % NADJ, :],
                                          ALU.mult)
                    ins.then_inc(s.probs_ready, 1)

        def load_weights(q, x):
            s, b = gs, gb[x]

            def put(dst, src):
                q.dma_start(dst, src).then_inc(s.w_loaded, 16)

            def rows(w):
                return w.rearrange("(k p) n -> p k n", p=P)

            def every(b):
                return b.rearrange("(o n) -> o n", o=1).to_broadcast([P, D])

            if x == "L0_gnn":
                put(w_raw[:, :, 0:D], rows(d["L0_gnn_W"]))
                put(bias_row[:], every(d["L0_gnn_b"]))
            elif x == "L1_gnn":
                put(w_raw[:, :, 0:D], rows(d["L1_gnn_edge_w"]))
                put(w_raw[:, :, D:2 * D], rows(d["L1_gnn_weight"]))
                with nc.allow_non_contiguous_dma(reason="one column of 256 numbers"):
                    put(w_raw[:, :, 2 * D:2 * D + 1], rows(d["L1_gnn_node_w"]))
                put(bias_row[:], every(d["L1_gnn_bias"]))
            elif x == "L2_gnn":
                put(w_raw[:, :, 0:D], rows(d["L2_gnn_fc_w"]))
                put(attn_raw[:], d["L2_gnn_W"].rearrange("(h k p) n -> p h k n", h=2, p=P))
                put(bias_row[:], every(d["L2_gnn_fc_b"]))
                put(a_row[:], every(d["L2_gnn_a_w"]))
                put(ab[:], d["L2_gnn_a_b"].to_broadcast([P, 1]))
            else:
                put(w_raw[:, :, 0:2 * D], rows(d["L3_gnn_W_stack"][0 if x == "L3a" else 1]))

        def load_adjacency(q, x, ahead):
            s, b = gs, gb[x]
            for r in range(TILES):
                if r >= NADJ:
                    if x == "L2_gnn":
                        q.wait_ge(s.adj_used, b["adj_used"] + r - NADJ + 1)
                    else:
                        q.wait_ge(s.probs_ready, b["probs_ready"] + r - NADJ + 1)
                rows = LAST if r == TILES - 1 else P
                q.dma_start(adj_rows[0:rows, r % NADJ, :], d["adj"][r * P:r * P + rows, :]).then_inc(
                    s.adj_loaded[r % NADJ], 16)
                if r == NADJ:
                    q.wait_ge(s.item_done, b["item_done"] + len(graph_items(x)))
                if r >= NADJ:
                    for load in ahead[(r - NADJ) * 2:(r - NADJ) * 2 + 2]:
                        load()

        def load_nibble_weights(q):
            q.wait_ge(ns.w_zeroed, 1)
            for o, op in enumerate(("and", "or", "xor")):
                w1, b1 = d[f"L0_ffn_{op}_w1"], d[f"L0_ffn_{op}_b1"]
                w2, b2 = d[f"L0_ffn_{op}_w2"], d[f"L0_ffn_{op}_b2"]
                r = 6 * o
                with nc.allow_non_contiguous_dma(reason="one column of the second layer"):
                    for dst, src in ((nib_w[r:r + 2, 0:GE], w1[0:2, :]), (nib_w[r + 2:r + 5, 0:GE], w1[44:47, :]),
                                     (nib_w[r + 5:r + 6, 0:GE], b1.rearrange("(o n) -> o n", o=1)),
                                     (nib_w[r + 5:r + 6, GE:2 * GE], w2[:, 64:65].rearrange("n o -> o n")),
                                     (nib_w[r + 5:r + 6, 2 * GE:2 * GE + 1], b2.rearrange("(o n) -> o n", o=1)[:, 64:65])):
                        q.dma_start(dst, src).then_inc(ns.w_loaded, 16)
            q.wait_ge(ns.w_loaded, 16 * 15)
            q.dma_start(nib_w[32:50, :], nib_w[0:18, :]).then_inc(ns.w_loaded, 16)

        NIB_BANKS = 4

        def nibble_pool(p):
            p.iota(bit_w[:].rearrange("p t (k j) -> p t k j", j=16), pattern=[[0, TILES], [0, 4], [-1, 16]], base=16,
                   channel_multiplier=0, allow_small_or_imprecise_dtypes=True)
            p.iota(digit[:], pattern=[[0, 2 * TILES], [1, 16]], base=0, channel_multiplier=0,
                   allow_small_or_imprecise_dtypes=True)
            p.memset(feats[:], 0.0).then_inc(ns.iota, 1)

        def nibble_vector(v, rows_base):
            v.wait_ge(ns.iota, 1)
            v.wait_ge(rows_normed, rows_base + TILES)
            vstep(v, v.scalar_tensor_tensor(bits[:], normed[:, :, 16:80], 0.5, bit_w[:], ALU.is_gt, ALU.mult))
            vstep(v, v.tensor_reduce(nib_max[:].rearrange("p t k -> p (t k)"),
                                     bits[:].rearrange("p t (k j) -> p (t k) j", j=16), AX.X, ALU.max))
            vstep(v, v.tensor_scalar(nib_rev[:], nib_max[:], -1.0, 16.0, ALU.mult, ALU.add))
            v.scalar_tensor_tensor(nib[:], nib_max[:], 0.0, nib_rev[:], ALU.is_gt, ALU.mult)
            vstep(v, v.tensor_scalar(opf[:], normed[:, :, 1:4], 0.5, None, ALU.is_gt))
            vstep(v, v.tensor_scalar(opn[:], opf[:, :, 0:2], -1.0, 1.0, ALU.mult, ALU.add))
            v.tensor_copy(sel[:, :, 0:1], opf[:, :, 0:1])
            v.tensor_tensor(sel[:, :, 1:2], opf[:, :, 1:2], opn[:, :, 0:1], ALU.mult)
            v.tensor_tensor(sel[:, :, 2:3], opn[:, :, 0:1], opn[:, :, 1:2], ALU.mult)
            vstep(v, v.tensor_tensor(active[:, :, 0:1], opf[:, :, 0:1], opf[:, :, 1:2], ALU.max))
            vstep(v, v.tensor_tensor(active[:, :, 1:2], active[:, :, 0:1], opf[:, :, 2:3], ALU.max))
            vstep(v, v.scalar_tensor_tensor(active[:, :, 2:3], normed[:, :, 0:1], 0.5, active[:, :, 1:2],
                                            ALU.is_ge, ALU.mult))
            vstep(v, v.tensor_scalar(active[:, :, 0:1], active[:, :, 2:3], 2.0, None, ALU.mult))
            for row in range(2):
                v.tensor_copy(feat6[:, row, :, 0:1], nib[:, :, row:row + 1])
                v.tensor_copy(feat6[:, row, :, 1:2], nib[:, :, 2 + row:3 + row])
                v.tensor_copy(feat6[:, row, :, 2:4], normed[:, :, 2:4])
                v.tensor_copy(feat6[:, row, :, 4:5], normed[:, :, 1:2])
                ins = v.memset(feat6[:, row, :, 5:6], 1.0)
            vstep(v, ins)
            for row in range(2):
                for o in range(3):
                    at = 32 * row + 6 * o
                    ins = v.tensor_tensor(feats[:, :, at:at + 6], feat6[:, row, :, :],
                                          sel[:, :, o:o + 1].to_broadcast([P, TILES, 6]), ALU.mult)
            ins.then_inc(ns.feats_ready, 1)
            for k in range(2 * TILES):
                t, row = k // 2, k % 2
                bank = psum[:, 4 + k % NIB_BANKS, :]
                v.wait_ge(ns.relu, k + 1)
                v.tensor_tensor_reduce(nib_prod[:, k % 2, :], hidden[:, k % 2, :], bank[:, GE:2 * GE], 1.0, 0.0,
                                       ALU.mult, ALU.add, res[:, t, row:row + 1])
                v.tensor_copy(res_b[:, t, row:row + 1], bank[:, 2 * GE:2 * GE + 1]).then_inc(ns.used, 1)
            v.wait_ge(ns.used, 2 * TILES)
            vstep(v, v.tensor_tensor(res[:], res[:], res_b[:], ALU.add))
            vstep(v, v.tensor_scalar(res[:], res[:], 0.0, 15.0, ALU.max, ALU.min))
            vstep(v, v.tensor_scalar(res[:], res[:], ROUND, ROUND, ALU.add, ALU.subtract))
            vstep(v, v.tensor_tensor(onehot[:], digit[:], res[:].rearrange("p t (r o) -> p (t r) o", o=1)
                                     .to_broadcast([P, 2 * TILES, 16]), ALU.is_equal))
            both = onehot[:].rearrange("p (t r) j -> p t (r j)", r=2)
            vstep(v, v.tensor_tensor(both, both, active[:, :, 0:1].to_broadcast([P, TILES, 32]), ALU.mult))
            vstep(v, v.tensor_tensor(resid[:], resid[:], normed[:], ALU.add))
            vstep(v, v.tensor_tensor(resid[:, :, 80:112], resid[:, :, 80:112], both, ALU.add))
            for t in range(TILES):
                row_stats(v, t)

        def nibble_scalar(a):
            for c, (t0, w_) in enumerate(GROUPS):
                a.wait_ge(ns.turned, c + 1)
                a.copy(feats_t[:, t0:t0 + w_, :], psum[0:64, c, 0:w_ * P].rearrange("p (t n) -> p t n", n=P)).then_inc(
                    ns.turned_kept, 1)
            for k in range(2 * TILES):
                a.wait_ge(ns.hidden, k + 1)
                if k >= 2:
                    a.wait_ge(ns.used, k - 1)
                a.activation(hidden[:, k % 2, :], psum[:, 4 + k % NIB_BANKS, 0:GE], ACT.Relu).then_inc(ns.relu, 1)

        def nibble_tensor(pe):
            pe.wait_ge(ns.feats_ready, 1)
            for c, (t0, w_) in enumerate(GROUPS):
                for j in range(w_):
                    ins = pe.transpose(psum[0:64, c, j * P:(j + 1) * P], feats[:, t0 + j, :], ident[:])
                ins.then_inc(ns.turned, 1)
            pe.wait_ge(ns.w_loaded, 16 * 16)
            for k in range(2 * TILES):
                t, row = k // 2, k % 2
                pe.wait_ge(ns.turned_kept, t // 4 + 1)
                if k >= NIB_BANKS:
                    pe.wait_ge(ns.used, k - NIB_BANKS + 1)
                at = 32 * row
                pe.matmul(psum[:, 4 + k % NIB_BANKS, 0:2 * GE + 1], feats_t[at:at + 18, t, :],
                          nib_w[at:at + 18, 0:2 * GE + 1], start=True, stop=True).then_inc(ns.hidden, 1)

        MOE = {"L1_ffn": ("L1_ffn_W1", "L1_ffn_b1", "L1_ffn_W2", "L1_ffn_b2", "L1_ffn_Wr"),
               "L2_ffn": ("L2_ffn_Wgu", "L2_ffn_bgu", "L2_ffn_Wd", "L2_ffn_bd", "L2_ffn_Wg")}
        UP = KD * 1024
        up_w = expert_w[:, 0:E * UP].rearrange("p (e k n) -> p e k n", e=E, k=KD)
        down = {x: expert_w[:, E * UP:E * (UP + kh * D)].rearrange("p (e k n) -> p e k n", e=E, k=kh)
                for x, kh in (("L1_ffn", 8), ("L2_ffn", 4))}
        up_b = bias3[:, 0:E * 1024].rearrange("p (e n) -> p e n", e=E)
        down_b = bias3[:, E * 1024:E * 1280].rearrange("p (e n) -> p e n", e=E)

        y_loads = [32, 32, 64]

        def logit_items():
            turns = [("turn", i) for i in range(0, TILES, 2)]
            return (turns[0:3] + [("chunk", 0)] + turns[3:5] + [("chunk", 1)] + turns[5:] + [("chunk", 2), ("logits",)])

        def moe_items():
            return [("weights",)] + logit_items()

        def logits_tensor(pe, it, items, k, width, turned, w, logits_t, done):
            if it[0] == "chunk":
                a_, cols = PCHUNKS[it[1]]
                pe.wait_ge(done, items.index(("turn", min(4 * it[1] + 2, (TILES - 1) // 2 * 2))) + 1)
                for kb in range(KD):
                    ins = product(pe, psum[0:width, k % RING, 0:cols], w(slice(None), kb, slice(None)),
                                  turned(slice(None), kb, slice(a_, a_ + cols)), kb == 0, kb == KD - 1)
            else:
                pe.wait_ge(done, k)
                for t in range(TILES):
                    ins = pe.transpose(psum[:, k % RING, t * width:(t + 1) * width], logits_t[:, t * P:(t + 1) * P],
                                       ident[0:width, 0:width])
            return ins

        def load_router(q, x):
            s = ml[x]
            q.dma_start(router_raw[:], d[MOE[x][4]].rearrange("(k p) e -> p k e", p=P)).then_inc(s.r_loaded, 16)
            if x == "L1_ffn":
                q.dma_start(router_b[:], d["L1_ffn_br"].rearrange("(o n) -> o n", o=1).to_broadcast([P, E])).then_inc(
                    s.r_loaded, 16)
            q.dma_start(split_f[0:64, 0, :], d[MOE[x][1]].rearrange("e (j n) -> (e j) n", n=P)).then_inc(s.b_loaded, 16)
            q.dma_start(split_f[64:80, 0, :], d[MOE[x][3]].rearrange("e (j n) -> (e j) n", n=P)).then_inc(s.b_loaded, 16)

        def load_up(q, x, e):
            q.dma_start(up_w[:, e], d[MOE[x][0]][e].rearrange("(k p) n -> p k n", p=P)).then_inc(ml[x].w_loaded, 16)

        def load_down(q, x, e):
            q.dma_start(down[x][:, e], d[MOE[x][2]][e].rearrange("(k p) n -> p k n", p=P)).then_inc(ml[x].w_loaded, 16)

        up_ahead = {"L1_ffn": min(E, (attention_at - shared_at) // (4 * UP)) if "L1_gnn" in stages else 0,
                    "L2_ffn": min(E, (k_at - shared_at) // (4 * UP)) if "L2_gnn" in stages else 0}

        def place_biases(q, x):
            s = ml[x]
            q.wait_ge(s.b_split, 1)
            for i in range(3):
                q.dma_start(bias_scratch[i].rearrange("(a n) -> a n", n=P), split_b[:, i, :]).then_inc(s.b_placed, 16)
            q.wait_ge(s.b_placed, 48)
            q.wait_ge(s.logits, 1)
            q.dma_start(bias3[:], bias_scratch).then_inc(s.b_spread, 16)

        def store_rows(q, x, rows_base):
            q.wait_ge(rows_normed, rows_base + TILES)
            q.dma_start(x_rows.rearrange("(t p) n -> p t n", p=P), normed[:]).then_inc(ml[x].rows_stored, 16)

        def load_results(q, x):
            q.wait_ge(ml[x].y_stored[0], 16 * ((SLOTS + 1) // 2))
            q.wait_ge(ml[x].y_stored[1], 16 * (SLOTS // 2))
            for c, (t0, w_) in enumerate(GROUPS):
                for which in range(2):
                    base_ = which * NP
                    whole = w_ if t0 + w_ < TILES else w_ - 1
                    q.dma_start(gathered[:, t0:t0 + whole, which, :], y_rows[base_ + t0 * P:base_ + (t0 + whole) * P, :]
                                .rearrange("(t p) n -> p t n", p=P)).then_inc(y_loaded[c], 16)
                    if whole < w_:
                        q.dma_start(gathered[0:LAST, TILES - 1, which, :],
                                    y_rows[base_ + (TILES - 1) * P:base_ + N, :]).then_inc(y_loaded[c], 16)

        def moe_tensor(pe, x, rows_base):
            s = ml[x]
            turned, w = pairs(mturned_hi, mturned_lo), pairs(router_hi, router_lo)
            for k, it in enumerate(moe_items()):
                if it[0] == "weights":
                    continue
                ring_free(pe, s.item_done, k)
                if it[0] == "turn":
                    ins = turn_tensor(pe, it[1], k, rows_base)
                else:
                    ins = logits_tensor(pe, it, moe_items(), k, E, turned, w, logits_t, s.item_done)
                ins.then_inc(s.item_ready, 1)
            pe.wait_ge(s.chosen, 1)
            both = chosen_b
            flat = psum[:, 4, 0:TILES * E]
            pe.matmul(flat, before_b[:], both[:].rearrange("p t e -> p (t e)"), start=True, stop=False)
            for t in range(TILES - 1):
                rest = TILES - 1 - t
                pe.matmul(psum[:, 4, (t + 1) * E:TILES * E].rearrange("p (t e) -> p t e", e=E), ones_b[:],
                          both[:, t:t + 1, :].to_broadcast([P, rest, E]), start=False, stop=t == TILES - 2)
            for t in range(TILES):
                ins = pe.matmul(psum[:, 5, 0:E], ones_b[:], both[:, t, :], start=t == 0, stop=t == TILES - 1)
            ins.then_inc(s.counted, 1)

            pe.wait_ge(s.hot_ready, 1)
            for i in range(2 * TILES):
                ins = pe.matmul(psum[:, 6, 0:2 * SLOTS], place_hot[:, i, :],
                                slot_vals[:, i, :, :].rearrange("p c k -> p (c k)"), start=i == 0, stop=i == 2 * TILES - 1)
            ins.then_inc(s.mapped, 1)

            HB = 8 if x == "L1_ffn" else 4
            pe.wait_ge(s.placed, 1)

            def expert(k):
                return bass.ds(pe.value_load(slot_expert[0:1, bass.ds(k, 1)], min_val=0, max_val=E - 1), 1)

            def one(ap):
                return ap.rearrange("p o n -> p (o n)")

            def turn_x(k, parity, half):
                pe.wait_ge(s.x_loaded[parity], (half + 1) * 16)
                for kb in range(KD):
                    ins = pe.transpose(psum[:, 6, kb * P:(kb + 1) * P], slot_x[:, parity, kb * P:(kb + 1) * P], ident[:])
                ins.then_inc(s.x_turned, 1)

            def up(k, parity, early=False):
                e = expert(k)
                pe.wait_ge(s.xt_ready, k + 1)
                if not early:
                    pe.wait_ge(s.h_kept_s, k - 1)
                    pe.wait_ge(s.h_kept_v, k - 1)
                for c in range(2):
                    o = psum[:, 2 * parity + c, :]
                    pe.matmul(o, ones3[:], one(up_b[:, e, c * BANK:(c + 1) * BANK]), start=True, stop=False)
                    for kb in range(KD):
                        ins = pe.matmul(o, slot_xt[:, parity, kb, :], one(up_w[:, e, kb, c * BANK:(c + 1) * BANK]),
                                        start=False, stop=kb == KD - 1)
                    ins.then_inc(s.h_ready, 1)

            def turn_h(k, parity):
                pe.wait_ge(s.h_kept_s, k + 1)
                if x == "L2_ffn":
                    pe.wait_ge(s.h_kept_v, k + 1)
                if not isinstance(k, int) or k > 0:
                    pe.wait_ge(s.ht_ready_s, k)
                for b in range(HB):
                    if b == 4:
                        pe.wait_ge(s.h_kept_v, k + 1)
                        if not isinstance(k, int) or k > 0:
                            pe.wait_ge(s.ht_ready_v, k)
                    ins = pe.transpose(psum[:, 4 + b // 4, b % 4 * P:(b % 4 + 1) * P],
                                       slot_h[:, parity, b * P:(b + 1) * P], ident[:])
                    if b % 4 == 3:
                        ins.then_inc(s.h_turned, 1)

            def down_(k):
                e = expert(k)
                if not isinstance(k, int) or k > 0:
                    pe.wait_ge(s.y_kept, k)
                o = psum[:, 7, 0:D]
                pe.matmul(o, ones3[:], one(down_b[:, e, :]), start=True, stop=False)
                pe.wait_ge(s.ht_ready_s, k + 1)
                for b in range(HB):
                    if b == 4:
                        pe.wait_ge(s.ht_ready_v, k + 1)
                    ins = pe.matmul(o, slot_ht[:, b * P:(b + 1) * P], one(down[x][:, e, b, :]),
                                    start=False, stop=b == HB - 1)
                ins.then_inc(s.y_ready, 1)

            def step(k, parity, half, early=False, last=False):
                turn_h(k - 1, 1 - parity)
                up(k, parity, early)
                if not last:
                    turn_x(k + 1, 1 - parity, half + parity)
                down_(k - 1)

            pe.wait_ge(s.w_loaded, 16 * 2 * E)
            pe.wait_ge(s.b_spread, 16)
            turn_x(0, 0, 0)
            up(0, 0, early=True)
            turn_x(1, 1, 0)
            step(1, 1, 0, early=True)
            step(2, 0, 1)
            with pe.Fori(0, (SLOTS - 5) // 2) as j:
                step(j * 2 + 3, 1, j + 1)
                step(j * 2 + 4, 0, j + 2)
            step(SLOTS - 2, 1, (SLOTS - 2) // 2)
            step(SLOTS - 1, 0, (SLOTS - 1) // 2, last=True)
            turn_h(SLOTS - 1, 0)
            down_(SLOTS - 1)

        def moe_scalar(a, x):
            s = ml[x]
            n_pe = 0
            for k, it in enumerate(moe_items()):
                if it[0] == "weights":
                    a.wait_ge(s.r_loaded, 32 if x == "L1_ffn" else 16)
                    a.copy(router_hi[:], router_raw[:]).then_inc(s.item_hi, 1)
                elif it[0] == "turn":
                    n_pe += 1
                    a.wait_ge(s.item_ready, n_pe)
                    src, cols = turn_source(it[1], k)
                    a.copy(mturned_hi[:, :, cols], src).then_inc(s.item_hi, 1)
                elif it[0] == "chunk":
                    n_pe += 1
                    a.wait_ge(s.item_ready, n_pe)
                    a_, cols = PCHUNKS[it[1]]
                    a.copy(logits_t[:, a_:a_ + cols], psum[0:E, k % RING, 0:cols]).then_inc(s.item_hi, 1)
            a.wait_ge(s.gap, 1)
            a.activation(best[:, :, 3], best[:, :, 2], ACT.Exp).then_inc(s.gap_exp, 1)

            def keep_xt(k, parity, early=False):
                a.wait_ge(s.x_turned, k + 1)
                if not early:
                    a.wait_ge(s.h_ready, k * 2 - 2)
                a.copy(slot_xt[:, parity, :, :], psum[:, 6, 0:D].rearrange("p (k n) -> p k n", k=KD)).then_inc(
                    s.xt_ready, 1)

            def keep_h(k, parity, early=False):
                a.wait_ge(s.h_ready, k * 2 + 1)
                if x == "L1_ffn":
                    if not early:
                        a.wait_ge(s.h_turned, k * 2 - 2)
                    a.activation(slot_h[:, parity, 0:BANK], psum[:, 2 * parity, :], ACT.Relu).then_inc(s.h_kept_s, 1)
                else:
                    if not isinstance(k, int) or k > 0:
                        a.wait_ge(s.h_kept_v, k)
                    a.activation(slot_silu[:], psum[:, 2 * parity, :], ACT.Silu).then_inc(s.h_kept_s, 1)

            def keep_ht(k):
                a.wait_ge(s.h_turned, k * 2 + 1 if x == "L1_ffn" else k + 1)
                if not isinstance(k, int) or k > 0:
                    a.wait_ge(s.y_ready, k)
                a.copy(slot_ht[:, 0:BANK], psum[:, 4, :]).then_inc(s.ht_ready_s, 1)

            def step(k, parity, early=False, last=False):
                keep_ht(k - 1)
                keep_h(k, parity, early)
                if not last:
                    keep_xt(k + 1, 1 - parity)

            keep_xt(0, 0, early=True)
            keep_h(0, 0, early=True)
            keep_xt(1, 1, early=True)
            step(1, 1, early=True)
            step(2, 0)
            with a.Fori(0, (SLOTS - 5) // 2) as j:
                step(j * 2 + 3, 1)
                step(j * 2 + 4, 0)
            step(SLOTS - 2, 1)
            step(SLOTS - 1, 0, last=True)
            keep_ht(SLOTS - 1)

        def moe_vector(v, x, inst):
            s = ml[x]
            v.wait_ge(s.b_loaded, 32)
            vstep(v, v.tensor_copy(split_b[:, 0, :], split_f[:, 0, :]))
            vstep(v, v.tensor_tensor(split_f[:, 1, :], split_f[:, 0, :], split_b[:, 0, :], ALU.subtract))
            vstep(v, v.tensor_copy(split_b[:, 1, :], split_f[:, 1, :]))
            vstep(v, v.tensor_tensor(split_f[:, 2, :], split_f[:, 1, :], split_b[:, 1, :], ALU.subtract))
            v.tensor_copy(split_b[:, 2, :], split_f[:, 2, :]).then_inc(s.b_split, 1)
            if x == "L2_ffn":
                vstep(v, v.memset(router_b[:], 0.0))
            for k, it in enumerate(moe_items()):
                if it[0] == "logits":
                    continue
                v.wait_ge(s.item_hi, k + 1)
                if it[0] == "weights":
                    ins = v.tensor_tensor(router_lo[:], router_raw[:], router_hi[:].bitcast(F32), ALU.subtract)
                elif it[0] == "chunk":
                    ins = v.engine_nop()
                else:
                    src, cols = turn_source(it[1], k)
                    ins = v.tensor_tensor(mturned_lo[:, :, cols], src, mturned_hi[:, :, cols].bitcast(F32), ALU.subtract)
                ins.then_inc(s.item_done, 1)
            logits, eq, rest = router_sb

            def rows(ap, width=E):
                return ap.to_broadcast([P, TILES, width])

            v.wait_ge(s.item_ready, len(moe_items()) - 1)
            src = psum[:, (len(moe_items()) - 1) % RING, 0:TILES * E].rearrange("p (t e) -> p t e", e=E)
            ins = v.tensor_tensor(logits[:], src, router_b[:].rearrange("p (o e) -> p o e", o=1)
                                  .to_broadcast([P, TILES, E]), ALU.add)
            ins.then_inc(s.logits, 1)
            v.wait_ge(s.logits, 1)
            for which, (frm, hot) in enumerate(((logits, first), (rest, second))):
                vstep(v, v.tensor_reduce(best[:, :, which], frm[:], AX.X, ALU.max))
                vstep(v, v.tensor_tensor(eq[:], frm[:], rows(best[:, :, which:which + 1]), ALU.is_equal))
                vstep(v, v.tensor_tensor(eq[:], eq[:], rank_down[:], ALU.mult))
                vstep(v, v.tensor_reduce(best[:, :, 2], eq[:], AX.X, ALU.max))
                vstep(v, v.tensor_tensor(hot[:], eq[:], rows(best[:, :, 2:3]), ALU.is_equal))
                if which == 0:
                    vstep(v, v.scalar_tensor_tensor(rest[:], first[:], LOWEST, logits[:], ALU.mult, ALU.add))
            vstep(v, v.tensor_tensor(logits[:], first[:], second[:], ALU.add))
            v.tensor_tensor(chosen_b[:], logits[:], rows(valid[:].rearrange("p (t o) -> p t o", o=1)),
                            ALU.mult).then_inc(s.chosen, 1)
            v.tensor_tensor(best[:, :, 2:3], best[:, :, 1:2], best[:, :, 0:1], ALU.subtract).then_inc(s.gap, 1)
            v.wait_ge(s.gap_exp, 1)
            vstep(v, v.tensor_scalar(gate[:, :, 1:2], best[:, :, 3:4], 1.0, None, ALU.add))
            vstep(v, v.reciprocal(gate[:, :, 0:1], gate[:, :, 1:2]))
            v.tensor_tensor(gate[:, :, 1:2], best[:, :, 3:4], gate[:, :, 0:1], ALU.mult)
            v.wait_ge(s.counted, 1)
            vstep(v, v.tensor_copy(per_expert[:, 0, :], psum[:, 5, 0:E]))
            vstep(v, v.tensor_tensor(step_gt[:], per_expert[:, 0, :].rearrange("p (e o) -> p e o", o=1)
                                     .to_broadcast([P, E, TILES]), steps128[:], ALU.is_gt))
            vstep(v, v.tensor_reduce(per_expert[:, 1, :], step_gt[:], AX.X, ALU.add))
            vstep(v, v.tensor_tensor(lt_prod[:], expert_lt[:], per_expert[:, 1:2, :].to_broadcast([P, E, E]), ALU.mult))
            vstep(v, v.tensor_reduce(per_expert[:, 2, :], lt_prod[:], AX.X, ALU.add))
            vstep(v, v.tensor_tensor(per_expert[:, 3, :], per_expert[:, 2, :], per_expert[:, 1, :], ALU.add))
            vstep(v, v.tensor_tensor(slot_ge[:], slot_iota[:], per_expert[:, 3:4, :].to_broadcast([P, SLOTS, E]),
                                     ALU.is_ge))
            vstep(v, v.tensor_reduce(slot_f[:], slot_ge[:], AX.X, ALU.add))
            vstep(v, v.tensor_scalar(slot_expert[:], slot_f[:], E - 1.0, None, ALU.min))
            vstep(v, v.scalar_tensor_tensor(rest[:], per_expert[:, 2:3, :].to_broadcast([P, TILES, E]), float(P),
                                            psum[:, 4, 0:TILES * E].rearrange("p (t e) -> p t e", e=E),
                                            ALU.mult, ALU.add))
            for which, hot in enumerate((first, second)):
                vstep(v, v.tensor_tensor(eq[:], rest[:], hot[:], ALU.mult))
                vstep(v, v.tensor_reduce(pos[:, which, :], eq[:], AX.X, ALU.add))
            slot_, in_slot = split_pos[:, 0], split_pos[:, 1]
            vstep(v, v.tensor_scalar(slot_, pos[:], 1.0 / P, 0.5 / P - 0.5, ALU.mult, ALU.add))
            vstep(v, v.tensor_scalar(slot_, slot_, ROUND, ROUND, ALU.add, ALU.subtract))
            vstep(v, v.scalar_tensor_tensor(in_slot, slot_, -float(P), pos[:], ALU.mult, ALU.add))

            def each(ap, width):
                return ap.rearrange("p w (t o) -> p (w t) o", o=1).to_broadcast([P, 2 * TILES, width])

            def const(ap, width):
                return ap[:].rearrange("p (o j) -> p o j", o=1).to_broadcast([P, 2 * TILES, width])

            v.tensor_tensor(place_hot[:], const(place_row, P), each(in_slot, P), ALU.is_equal)
            vstep(v, v.tensor_tensor(slot_hot[:], const(place_slot, SLOTS), each(slot_, SLOTS), ALU.is_equal))
            for c in range(2):
                ins = v.tensor_tensor(slot_vals[:, :, c, :], slot_hot[:], each(tile_p[:, c], SLOTS), ALU.mult)
            ins.then_inc(s.hot_ready, 1)
            v.wait_ge(s.mapped, 1)
            vstep(v, v.tensor_copy(mapped[:], psum[:, 6, 0:2 * SLOTS].rearrange("p (c k) -> p c k", c=2)))
            v.scalar_tensor_tensor(map_base[:], mapped[:, 0, :], float(P), mapped[:, 1, :], ALU.mult, ALU.add)
            v.scalar_tensor_tensor(spare_f[:], mapped[:, 0, :], 0.0, spare_row[:], ALU.is_equal, ALU.mult)
            vstep(v, v.tensor_scalar(source_f[:], mapped[:, 0, :], TILES + 0.5, -float(NP), ALU.is_gt, ALU.mult))
            vstep(v, v.tensor_tensor(source_f[:], source_f[:], map_base[:], ALU.add))
            v.tensor_scalar(source_row[:], source_f[:], -float(P), 0.0, ALU.add, ALU.max).then_inc(s.sources_ready, 1)
            vstep(v, v.tensor_tensor(target_f[:], spare_f[:], map_base[:], ALU.add))
            v.tensor_scalar(target_row[:], target_f[:], -float(P), None, ALU.add).then_inc(s.placed, 1)

            def keep_h(k, parity, early=False):
                v.wait_ge(s.h_ready, k * 2 + 2)
                if not early:
                    v.wait_ge(s.h_turned, k * 2 - 2 if x == "L1_ffn" else k - 1)
                bank = psum[:, 2 * parity + 1, :]
                if x == "L1_ffn":
                    v.tensor_scalar(slot_h[:, parity, BANK:2 * BANK], bank, 0.0, None, ALU.max).then_inc(s.h_kept_v, 1)
                else:
                    v.wait_ge(s.h_kept_s, k + 1)
                    v.tensor_tensor(slot_h[:, parity, 0:BANK], bank, slot_silu[:], ALU.mult).then_inc(s.h_kept_v, 1)

            def keep_ht(k):
                if x == "L1_ffn":
                    v.wait_ge(s.h_turned, k * 2 + 2)
                    if not isinstance(k, int) or k > 0:
                        v.wait_ge(s.y_ready, k)
                    v.tensor_copy(slot_ht[:, BANK:2 * BANK], psum[:, 5, :]).then_inc(s.ht_ready_v, 1)

            def keep_y(k, parity, half):
                v.wait_ge(s.y_ready, k + 1)
                if not isinstance(k, int) or k > 1:
                    v.wait_ge(s.y_stored[parity], half * 16)
                v.tensor_copy(slot_y[:, parity, :], psum[:, 7, 0:D]).then_inc(s.y_kept, 1)

            def step(k, parity, half, early=False):
                keep_ht(k - 1)
                keep_h(k, parity, early)
                keep_y(k - 1, 1 - parity, half)

            keep_h(0, 0, early=True)
            step(1, 1, 0, early=True)
            step(2, 0, 0)
            with v.Fori(0, (SLOTS - 5) // 2) as j:
                step(j * 2 + 3, 1, j + 1)
                step(j * 2 + 4, 0, j + 1)
            step(SLOTS - 2, 1, (SLOTS - 3) // 2)
            step(SLOTS - 1, 0, (SLOTS - 3) // 2)
            keep_ht(SLOTS - 1)
            keep_y(SLOTS - 1, 0, (SLOTS - 1) // 2)
            for c, (t0, w_) in enumerate(GROUPS):
                v.wait_ge(y_loaded[c], y_loads[c] * (inst + 1))
                for which in range(2):
                    for t in range(t0, t0 + w_):
                        r_ = LAST if t == TILES - 1 else P
                        ins = v.scalar_tensor_tensor(resid[0:r_, t, :], gathered[0:r_, t, which, :],
                                                     gate[0:r_, t, which:which + 1], resid[0:r_, t, :],
                                                     ALU.mult, ALU.add)
                    vstep(v, ins)
                for t in range(t0, t0 + w_):
                    row_stats(v, t)

        def moe_pool(p, x):
            s = ml[x]

            def load(k, parity):
                p.indirect_dma_start(slot_x[:, parity, :], None, x_rows,
                                     bass.IndirectOffsetOnAxis(source_row[:, k:k + 1], 0)).then_inc(s.x_loaded[parity], 16)

            def store(k, parity):
                p.indirect_dma_start(y_rows, bass.IndirectOffsetOnAxis(target_row[:, k:k + 1], 0),
                                     slot_y[:, parity, :], None).then_inc(s.y_stored[parity], 16)

            place_biases(p, x)
            p.wait_ge(s.rows_stored, 16)
            p.wait_ge(s.sources_ready, 1)
            load(0, 0)
            load(1, 1)
            p.wait_ge(s.placed, 1)
            for k in range(SLOTS):
                if k == 0:
                    p.wait_ge(s.x_turned, 1)
                    load(2, 0)
                if k + 3 < SLOTS:
                    p.wait_ge(s.x_turned, k + 2)
                    load(k + 3, (k + 3) % 2)
                p.wait_ge(s.y_kept, k + 1)
                store(k, k % 2)

        def f_items():
            return ([("in", wh, kb, half) for wh in range(2) for kb in range(KD) for half in range(2)] +
                    [("out", e, kp) for e in range(E + 1) for kp in range(2)] + [("gates",)] +
                    logit_items())

        def load_f(q):
            def every(b, width):
                return b.rearrange("(o n) -> o n", o=1).to_broadcast([P, width])

            for dst, src in ((gate_nat[0:2, :], d["L3_ffn_group_gate_w"]), (gate_nat[2:E + 2, :], d["L3_ffn_expert_gate_w"]),
                             (gate_b[:, 0:2], every(d["L3_ffn_group_bias"], 2)),
                             (gate_b[:, 2:E + 2], every(d["L3_ffn_expert_bias"], E)),
                             (ln_rows[:, 0, :], every(d["L3_ffn_ln_scale"], D)),
                             (ln_rows[:, 1, :], every(d["L3_ffn_ln_bias"], D)),
                             (bias9[0:E, :], d["L3_ffn_expert_out_bias"]),
                             (bias9[E:E + 1, :], d["L3_ffn_shared_out_b"].rearrange("(o n) -> o n", o=1))):
                q.dma_start(dst, src).then_inc(fs.loaded, 16)

        def load_f_in(q, wh):
            src = d[("L3_ffn_shared_in_w", "L3_ffn_expert_in_w")[wh]]
            q.dma_start(nat_in[:, wh], src.rearrange("(b p) n -> p b n", p=P)).then_inc(fs.in_loaded[wh], 16)

        def load_f_out(q, e):
            src = d["L3_ffn_expert_out_weight"][e] if e < E else d["L3_ffn_shared_out_w"]
            q.dma_start(nat_out[:, e], src.rearrange("(b p) n -> p b n", p=P)).then_inc(fs.out_loaded, 16)

        def f_source(it, k):
            bank = psum[:, k % RING, :]
            if it[0] == "gates":
                return bank[:, 0:KD * (E + 2)].rearrange("p (k n) -> p k n", k=KD), gate_hi[:], gate_lo[:]
            if it[0] == "in":
                _, wh, kb, half = it
                cols = slice(half * BANK, (half + 1) * BANK)
                return bank, in_hi[:, wh, kb, cols], in_lo[:, wh, kb, cols]
            if it[0] == "out":
                _, e, kp = it
                ix = (slice(None), slice(2 * kp, 2 * kp + 2), slice(e * D, (e + 1) * D))
                return bank.rearrange("p (k n) -> p k n", k=2), out_hi[ix], out_lo[ix]
            src, cols = turn_source(it[1], k)
            return src, f_turned_hi[:, :, cols], f_turned_lo[:, :, cols]

        def f_tensor(pe, rows_base):
            s = fs
            for k, it in enumerate(f_items()):
                ring_free(pe, s.item_done, k)
                if it[0] == "gates":
                    pe.wait_ge(s.loaded, 16 * 8)
                    for kb in range(KD):
                        ins = pe.transpose(psum[:, k % RING, kb * (E + 2):(kb + 1) * (E + 2)],
                                           gate_nat[:, kb * P:(kb + 1) * P], ident[0:E + 2, 0:E + 2])
                elif it[0] == "in":
                    _, wh, kb, half = it
                    pe.wait_ge(s.in_loaded[wh], 16)
                    for j in range(4):
                        ins = pe.transpose(psum[:, k % RING, j * P:(j + 1) * P],
                                           nat_in[:, wh, 4 * half + j, kb * P:(kb + 1) * P], ident[:])
                elif it[0] == "out":
                    _, e, kp = it
                    pe.wait_ge(s.out_loaded, 16 * (E + 1))
                    for j in range(2):
                        for nb in range(2):
                            at = (2 * kp + j) * P
                            ins = pe.transpose(psum[:, k % RING, j * D + nb * P:j * D + (nb + 1) * P],
                                               nat_out[:, e, nb, at:at + P], ident[:])
                elif it[0] == "turn":
                    ins = turn_tensor(pe, it[1], k, rows_base)
                else:
                    ins = logits_tensor(pe, it, f_items(), k, E + 2, pairs(f_turned_hi, f_turned_lo),
                                        pairs(gate_hi, gate_lo), f_logits_t, s.item_done)
                ins.then_inc(s.item_ready, 1)
            pe.wait_ge(s.item_done, len(f_items()))

            def hidden_(t, wh):
                k = 2 * t + wh
                if t >= 1:
                    pe.wait_ge(s.h_kept, k - 1)
                for half in range(2):
                    for kb in range(KD):
                        ins = product(pe, psum[:, 2 * wh + half, :],
                                      pairs(f_turned_hi, f_turned_lo)(slice(None), kb, slice(t * P, (t + 1) * P)),
                                      pairs(in_hi, in_lo)(slice(None), wh, kb, slice(half * BANK, (half + 1) * BANK)),
                                      kb == 0, kb == KD - 1)
                ins.then_inc(s.h_ready, 1)

            def turn(t, wh):
                k = 2 * t + wh
                pe.wait_ge(s.h_kept, k + 1)
                if k >= 1:
                    pe.wait_ge(s.ht_done, k)
                for j in range(4):
                    ins = pe.transpose(psum[:, 4, j * P:(j + 1) * P], act_h[:, wh, j * P:(j + 1) * P], ident[:])
                ins.then_inc(s.h_turned, 1)

            def outputs(t):
                k = 5 * t
                pe.wait_ge(s.ht_done, 2 * t + 1)
                if t >= 1:
                    pe.wait_ge(s.y_used, k - 4)
                if t == 0:
                    pe.wait_ge(s.cnt_kept, NG)
                pe.matmul(psum[:, 5, 0:D], cnt_t[:, t, :], bias9[:], start=True, stop=False)
                for kq in range(4):
                    ins = product(pe, psum[:, 5, 0:D], pairs(act_t_hi, act_t_lo)(slice(None), 0, slice(kq * P, (kq + 1) * P)),
                                  pairs(out_hi, out_lo)(slice(None), kq, slice(E * D, (E + 1) * D)), False, kq == 3)
                ins.then_inc(s.y_ready, 1)
                pe.wait_ge(s.ht_done, 2 * t + 2)
                for q in range(4):
                    n_ = k + 1 + q
                    if q >= 2:
                        pe.wait_ge(s.y_used, n_ - 1)
                    elif t >= 1:
                        pe.wait_ge(s.y_used, n_ - 2)
                    for kq in range(4):
                        ins = product(pe, psum[:, 6 + q % 2, :],
                                      pairs(act_t_hi, act_t_lo)(slice(None), 1, slice(kq * P, (kq + 1) * P)),
                                      pairs(out_hi, out_lo)(slice(None), kq, slice(q * BANK, (q + 1) * BANK)),
                                      kq == 0, kq == 3)
                    ins.then_inc(s.y_ready, 1)

            hidden_(0, 0)
            hidden_(0, 1)
            pe.wait_ge(s.cnt_ready, 1)
            for c, (t0, w_) in enumerate(GROUPS):
                for j in range(w_):
                    ins = pe.transpose(psum[0:E + 1, 5 + c, j * P:(j + 1) * P], cnt[:, t0 + j, :], ident[:])
                ins.then_inc(s.cnt_turned, 1)
            for t in range(TILES):
                turn(t, 0)
                if t + 1 < TILES:
                    hidden_(t + 1, 0)
                turn(t, 1)
                if t + 1 < TILES:
                    hidden_(t + 1, 1)
                outputs(t)

        def f_scalar(a):
            s = fs
            for k, it in enumerate(f_items()[:-1]):
                if it == ("turn", 0):
                    norm_scalar(a, norm_index["L3_ffn"] + 1)
                a.wait_ge(s.item_ready, k + 1)
                if it[0] == "chunk":
                    a_, cols = PCHUNKS[it[1]]
                    a.copy(f_logits_t[:, a_:a_ + cols], psum[0:E + 2, k % RING, 0:cols]).then_inc(s.item_hi, 1)
                else:
                    src, hi_, _ = f_source(it, k)
                    a.copy(hi_, src).then_inc(s.item_hi, 1)
            a.wait_ge(s.exp_in, 1)
            a.activation(esel[:, 1], esel[:, 0], ACT.Exp).then_inc(s.exp_out, 1)

            def silu(t, wh):
                a.wait_ge(s.h_ready, 2 * t + wh + 1)
                if t >= 1:
                    a.wait_ge(s.h_kept, 2 * t + wh - 1)
                a.activation(act_silu[:, wh, :], psum[:, 2 * wh, :], ACT.Silu).then_inc(s.silu, 1)

            def hi(t, wh):
                a.wait_ge(s.h_turned, 2 * t + wh + 1)
                if t >= 1:
                    a.wait_ge(s.y_ready, 5 * t - 4 if wh == 0 else 5 * t)
                a.copy(act_t_hi[:, wh, :], psum[:, 4, :]).then_inc(s.ht_hi, 1)

            silu(0, 0)
            silu(0, 1)
            for c, (t0, w_) in enumerate(GROUPS):
                a.wait_ge(s.cnt_turned, c + 1)
                a.copy(cnt_t[:, t0:t0 + w_, :], psum[0:E + 1, 5 + c, 0:w_ * P].rearrange("p (t n) -> p t n", n=P)).then_inc(
                    s.cnt_kept, 1)
            for t in range(TILES):
                hi(t, 0)
                if t + 1 < TILES:
                    silu(t + 1, 0)
                hi(t, 1)
                if t + 1 < TILES:
                    silu(t + 1, 1)

        def f_norm(v, rows_base, index):
            v.wait_ge(rows_normed, rows_base + TILES)
            v.wait_ge(fs.loaded, 16 * 8)
            for t in range(TILES):
                ins = v.bn_stats(stats[:, t, :], normed[:, t, :])
            vstep(v, ins)
            for t in range(TILES):
                ins = v.bn_aggr(mean_var[:, t, :], stats[:, t, :])
            vstep(v, ins)
            v.tensor_scalar(var_eps[:], mean_var[:, :, 1], EPS, None, ALU.add).then_inc(var_ready, 1)
            v.wait_ge(std_ready, index + 1)
            vstep(v, v.reciprocal(rstd[:], std[:]))
            for t in range(TILES):
                ins = v.tensor_scalar(normed[:, t, :], normed[:, t, :], mean_var[:, t, 0:1], rstd[:, t:t + 1],
                                      ALU.subtract, ALU.mult)
            vstep(v, ins)
            vstep(v, v.tensor_tensor(normed[:], normed[:], ln_rows[:, 0:1, :].to_broadcast([P, TILES, D]), ALU.mult))
            for t in range(TILES):
                v.tensor_tensor(normed[:, t, :], normed[:, t, :], ln_rows[:, 1, :], ALU.add).then_inc(rows_normed, 1)

        def f_vector(v):
            s = fs
            for k, it in enumerate(f_items()[:-1]):
                if it == ("turn", 0):
                    f_norm(v, rows_at["L3_ffn"], norm_index["L3_ffn"] + 1)
                v.wait_ge(s.item_hi, k + 1)
                if it[0] == "chunk":
                    v.engine_nop().then_inc(s.item_done, 1)
                else:
                    src, hi_, lo_ = f_source(it, k)
                    v.tensor_tensor(lo_, src, hi_.bitcast(F32), ALU.subtract).then_inc(s.item_done, 1)
            v.wait_ge(s.item_ready, len(f_items()))
            bank = psum[:, (len(f_items()) - 1) % RING, 0:TILES * (E + 2)].rearrange("p (t e) -> p t e", t=TILES)
            ins = v.tensor_tensor(glog[:], bank, gate_b[:].rearrange("p (o e) -> p o e", o=1)
                                  .to_broadcast([P, TILES, E + 2]), ALU.add)
            ins.then_inc(s.item_done, 1)
            v.wait_ge(s.item_done, len(f_items()))

            def four(ap):
                return ap.to_broadcast([P, TILES, 4])

            def col_(i):
                return psel[:, i:i + 1, :].rearrange("p o t -> p t o")

            vstep(v, v.tensor_tensor(grp[:, :, 1:2], glog[:, :, 1:2], glog[:, :, 0:1], ALU.is_gt))
            vstep(v, v.tensor_scalar(grp[:, :, 0:1], grp[:, :, 1:2], -1.0, 1.0, ALU.mult, ALU.add))
            v.tensor_tensor(esel[:, 1], glog[:, :, 2:6], four(grp[:, :, 0:1]), ALU.mult)
            vstep(v, v.tensor_tensor(esel[:, 2], glog[:, :, 6:10], four(grp[:, :, 1:2]), ALU.mult))
            vstep(v, v.tensor_tensor(esel[:, 0], esel[:, 1], esel[:, 2], ALU.add))
            vstep(v, v.tensor_reduce(psel[:, 0, :], esel[:, 0], AX.X, ALU.max))
            v.tensor_tensor(esel[:, 0], esel[:, 0], four(col_(0)), ALU.subtract).then_inc(s.exp_in, 1)
            v.wait_ge(s.exp_out, 1)
            vstep(v, v.tensor_reduce(psel[:, 1, :], esel[:, 1], AX.X, ALU.add))
            vstep(v, v.reciprocal(psel[:, 1, :], psel[:, 1, :]))
            vstep(v, v.tensor_tensor(esel[:, 2], esel[:, 1], four(col_(1)), ALU.mult))
            probs4, hot1, rest4, hot2 = esel[:, 2], esel[:, 3], esel[:, 4], esel[:, 5]
            for which, (frm, hot) in enumerate(((probs4, hot1), (rest4, hot2))):
                vstep(v, v.tensor_reduce(psel[:, which, :], frm, AX.X, ALU.max))
                vstep(v, v.tensor_tensor(pk[:], frm, four(col_(which)), ALU.is_equal))
                vstep(v, v.tensor_tensor(pk[:], pk[:], rank_down[:, :, 4:8], ALU.mult))
                vstep(v, v.tensor_reduce(psel[:, 2, :], pk[:], AX.X, ALU.max))
                vstep(v, v.tensor_tensor(hot, pk[:], four(col_(2)), ALU.is_equal))
                if which == 0:
                    vstep(v, v.scalar_tensor_tensor(rest4, hot1, -8.0, probs4, ALU.mult, ALU.add))
            vstep(v, v.tensor_tensor(psel[:, 3, :], psel[:, 0, :], psel[:, 1, :], ALU.add))
            vstep(v, v.tensor_scalar(psel[:, 3, :], psel[:, 3, :], 1e-8, None, ALU.add))
            vstep(v, v.reciprocal(psel[:, 3, :], psel[:, 3, :]))
            vstep(v, v.tensor_tensor(esel[:, 0], hot1, hot2, ALU.add))
            vstep(v, v.tensor_tensor(esel[:, 1], esel[:, 0], probs4, ALU.mult))
            vstep(v, v.tensor_tensor(esel[:, 1], esel[:, 1], four(col_(3)), ALU.mult))
            for gi in range(2):
                v.tensor_tensor(comb[:, :, 4 * gi:4 * gi + 4], esel[:, 1], four(grp[:, :, gi:gi + 1]), ALU.mult)
                v.tensor_tensor(cnt[:, :, 4 * gi:4 * gi + 4], esel[:, 0], four(grp[:, :, gi:gi + 1]), ALU.mult)
            vstep(v, v.memset(cnt[:, :, E:E + 1], 1.0))
            v.engine_nop().then_inc(s.cnt_ready, 1)

            def gated(t, wh):
                k = 2 * t + wh
                v.wait_ge(s.silu, k + 1)
                if t >= 1:
                    v.wait_ge(s.h_turned, k - 1)
                v.tensor_tensor(act_h[:, wh, :], psum[:, 2 * wh + 1, :], act_silu[:, wh, :], ALU.mult).then_inc(s.h_kept, 1)

            def lo(t, wh):
                v.wait_ge(s.ht_hi, 2 * t + wh + 1)
                v.tensor_tensor(act_t_lo[:, wh, :], psum[:, 4, :], act_t_hi[:, wh, :].bitcast(F32),
                                ALU.subtract).then_inc(s.ht_done, 1)

            gated(0, 0)
            gated(0, 1)
            for t in range(TILES):
                lo(t, 0)
                if t + 1 < TILES:
                    gated(t + 1, 0)
                lo(t, 1)
                if t + 1 < TILES:
                    gated(t + 1, 1)
                v.wait_ge(s.y_ready, 5 * t + 1)
                ins = v.tensor_tensor(resid[:, t, :], psum[:, 5, 0:D], resid[:, t, :], ALU.add)
                ins.then_inc(s.y_used, 1)
                v.wait_ge(s.y_used, 5 * t + 1)
                for q in range(4):
                    v.wait_ge(s.y_ready, 5 * t + 2 + q)
                    for j in range(2):
                        ins = v.scalar_tensor_tensor(resid[:, t, :], psum[:, 6 + q % 2, j * D:(j + 1) * D],
                                                     comb[:, t, 2 * q + j:2 * q + j + 1], resid[:, t, :],
                                                     ALU.mult, ALU.add)
                        if j == 0:
                            vstep(v, ins)
                    ins.then_inc(s.y_used, 1)
                    v.wait_ge(s.y_used, 5 * t + 2 + q)

        numbers = {}
        rows_at = {}
        count = 1
        rows = 0
        for st in stages:
            if st == "L3_gnn":
                numbers["L3a"], numbers["L3b"] = count, count + 1
                rows_at["L3a"], rows_at["L3b"] = rows, rows + TILES
                rows += 3 * TILES
                count += 2
            else:
                numbers[st] = count
                rows_at[st] = rows
                rows += TILES * (2 if st == "L3_ffn" else 1)
                count += 1
        counts["rows_end_L3b"] = rows_at.get("L3b", 0) + 2 * TILES
        order = [x for st in stages for x in (("L3a", "L3b") if st == "L3_gnn" else (st,))]
        norm_index = {}
        for x in order:
            if x != "L3b":
                norm_index[x] = len(norm_index)

        def loads_ahead(q, x):
            if x == "L1_gnn" and "L1_ffn" in stages:
                return [lambda e=e: load_up(q, "L1_ffn", e) for e in range(up_ahead["L1_ffn"])]
            if x == "L2_gnn" and "L2_ffn" in stages:
                return [lambda e=e: load_up(q, "L2_ffn", e) for e in range(up_ahead["L2_ffn"])]
            if x == "L3b" and "L3_ffn" in stages:
                return ([lambda wh=wh: load_f_in(q, wh) for wh in range(2)] +
                        [lambda e=e: load_f_out(q, e) for e in range(E + 1)])
            return []

        @block.sync
        def _(sp):
            for c, (t0, w_) in enumerate(GROUPS):
                w_ = min(w_, TILES - 1 - t0)
                sp.dma_start(resid[:, t0:t0 + w_, :],
                             d["x"][t0 * P:(t0 + w_) * P, :].rearrange("(t p) n -> p t n", p=P)).then_inc(x_loaded[c], 16)
            sp.wait_ge(padding_zeroed, 1)
            sp.dma_start(resid[0:LAST, TILES - 1, :], d["x"][(TILES - 1) * P:N, :]).then_inc(x_loaded[NG - 1], 16)
            for x in order:
                if numbers[x] > 1:
                    sp.wait_ge(stage_done, 4 * (numbers[x] - 1))
                if x in gb:
                    load_weights(sp, x)
                    load_adjacency(sp, x, loads_ahead(sp, x))
                    if x == "L0_gnn" and "L0_ffn" in numbers:
                        load_nibble_weights(sp)
                elif x == "L0_ffn" and numbers[x] == 1:
                    load_nibble_weights(sp)
                elif x in ml:
                    load_router(sp, x)
                    store_rows(sp, x, rows_at[x])
                    for e in range(up_ahead[x], E):
                        load_up(sp, x, e)
                    for e in range(E):
                        load_down(sp, x, e)
                    load_results(sp, x)
                elif x == "L3_ffn":
                    load_f(sp)
                    if "L3_gnn" not in stages:
                        for wh in range(2):
                            load_f_in(sp, wh)
                        for e in range(E + 1):
                            load_f_out(sp, e)
            sp.wait_ge(stage_done, 4 * (count - 1))
            sp.dma_start(out[0:(TILES - 1) * P, :].rearrange("(t p) n -> p t n", p=P),
                         resid[:, 0:TILES - 1, :]).then_inc(out_stored, 16)
            sp.dma_start(out[(TILES - 1) * P:N, :], resid[0:LAST, TILES - 1, :]).then_inc(out_stored, 16)
            sp.wait_ge(out_stored, 32)

        @block.gpsimd
        def _(p):
            p.memset(resid[:, TILES - 1, :], 0.0).then_inc(padding_zeroed, 1)
            p.memset(ident[:], 0.0)
            p.memset(valid[:], 1.0)
            p.memset(ones3[:], 1.0)
            p.memset(ones_b[:], 1.0)
            p.memset(before[:], 1.0)
            pstep(p, p.memset(ones[:], 1.0))
            p.affine_select(out=ident[:], in_=ident[:], compare_op=ALU.not_equal, fill=1.0, base=0,
                            pattern=[[-1, P]], channel_multiplier=1)
            p.affine_select(out=before[:], in_=before[:], compare_op=ALU.is_gt, fill=0.0, base=0,
                            pattern=[[1, P]], channel_multiplier=-1)
            pstep(p, p.affine_select(out=valid[:], in_=valid[:], compare_op=ALU.is_gt, fill=0.0, base=N,
                                     pattern=[[-P, TILES]], channel_multiplier=-1))
            p.tensor_copy(before_b[:], before[:])
            p.memset(nib_w[:], 0.0).then_inc(ns.w_zeroed, 1)
            for choice in range(2):
                p.iota(tile_p[:, 0, choice, :], pattern=[[1, TILES]], base=1 + choice * TILES, channel_multiplier=0,
                       allow_small_or_imprecise_dtypes=True)
                pstep(p, p.iota(tile_p[:, 1, choice, :], pattern=[[0, TILES]], base=0, channel_multiplier=1,
                                allow_small_or_imprecise_dtypes=True))
                for c in range(2):
                    p.tensor_tensor(tile_p[:, c, choice, :], tile_p[:, c, choice, :], valid[:], ALU.mult)
            p.iota(place_row[:], pattern=[[1, P]], base=0, channel_multiplier=0, allow_small_or_imprecise_dtypes=True)
            p.iota(place_slot[:], pattern=[[1, SLOTS]], base=0, channel_multiplier=0, allow_small_or_imprecise_dtypes=True)
            p.iota(spare_row[:], pattern=[[P, SLOTS]], base=2 * NP + P, channel_multiplier=1,
                   allow_small_or_imprecise_dtypes=True)
            for dst, pattern, start in ((rank_down[:], [[0, TILES], [-1, E]], E), (steps128[:], [[0, E], [P, TILES]], 0),
                                        (slot_iota[:], [[1, SLOTS], [0, E]], 0)):
                p.iota(dst, pattern=pattern, base=start, channel_multiplier=0, allow_small_or_imprecise_dtypes=True)
            pstep(p, p.memset(expert_lt[:], 1.0))
            p.affine_select(out=expert_lt[:], in_=expert_lt[:], compare_op=ALU.is_gt, fill=0.0, base=0,
                            pattern=[[1, E], [-1, E]], channel_multiplier=0)
            p.tensor_scalar(invalid_bias[:], valid[:], -1.0, 1e30, ALU.add, ALU.mult).then_inc(consts_ready, 1)
            for x in order:
                if x in gb:
                    graph_pool(p, x)
                elif x == "L0_ffn":
                    nibble_pool(p)
                elif x in ml:
                    moe_pool(p, x)
                stage_end(p, numbers[x])

        @block.scalar
        def _(a):
            a.wait_ge(consts_ready, 1)
            for x in order:
                if x != "L3b":
                    norm_scalar(a, norm_index[x])
                if x in gb:
                    graph_scalar(a, x)
                elif x == "L0_ffn":
                    nibble_scalar(a)
                elif x in ml:
                    moe_scalar(a, x)
                elif x == "L3_ffn":
                    f_scalar(a)
                stage_end(a, numbers[x])

        @block.vector
        def _(v):
            v.wait_ge(consts_ready, 1)
            for c, (t0, w_) in enumerate(GROUPS):
                v.wait_ge(x_loaded[c], 32 if c == NG - 1 else 16)
                for t in range(t0, t0 + w_):
                    row_stats(v, t)
            for x in order:
                if x != "L3b":
                    norm_vector(v, resid, norm_index[x])
                if x in gb:
                    graph_vector(v, x)
                elif x == "L0_ffn":
                    nibble_vector(v, rows_at[x])
                elif x in ml:
                    moe_vector(v, x, moe_layers.index(x))
                elif x == "L3_ffn":
                    f_vector(v)
                stage_end(v, numbers[x])

        @block.tensor
        def _(pe):
            pe.wait_ge(consts_ready, 1)
            for x in order:
                if x in gb:
                    graph_tensor(pe, x, rows_at[x])
                elif x == "L0_ffn":
                    nibble_tensor(pe)
                elif x in ml:
                    moe_tensor(pe, x, rows_at[x])
                elif x == "L3_ffn":
                    f_tensor(pe, rows_at[x] + TILES)
                stage_end(pe, numbers[x])


_INPUTS = ("x", "adj", "L0_gnn_W", "L0_gnn_b", "L0_ffn_and_w1", "L0_ffn_and_b1", "L0_ffn_and_w2", "L0_ffn_and_b2",
           "L0_ffn_or_w1", "L0_ffn_or_b1", "L0_ffn_or_w2", "L0_ffn_or_b2", "L0_ffn_xor_w1", "L0_ffn_xor_b1",
           "L0_ffn_xor_w2", "L0_ffn_xor_b2", "L1_gnn_weight", "L1_gnn_bias", "L1_gnn_node_w", "L1_gnn_edge_w",
           "L1_ffn_Wr", "L1_ffn_br", "L1_ffn_W1", "L1_ffn_b1", "L1_ffn_W2", "L1_ffn_b2", "L2_gnn_W", "L2_gnn_a_w",
           "L2_gnn_a_b", "L2_gnn_fc_w", "L2_gnn_fc_b", "L2_ffn_Wg", "L2_ffn_Wgu", "L2_ffn_bgu", "L2_ffn_Wd",
           "L2_ffn_bd", "L3_gnn_W_stack", "L3_ffn_ln_scale", "L3_ffn_ln_bias", "L3_ffn_shared_in_w",
           "L3_ffn_shared_out_w", "L3_ffn_shared_out_b", "L3_ffn_expert_in_w", "L3_ffn_expert_out_weight",
           "L3_ffn_expert_out_bias", "L3_ffn_group_gate_w", "L3_ffn_expert_gate_w", "L3_ffn_group_bias",
           "L3_ffn_expert_bias")


def kernel(**inputs):
    import numpy as np
    import concourse.bacc as bacc
    from concourse.bass_utils import run_bass_kernel_spmd

    nc = bacc.Bacc("TRN2", target_bir_lowering=False, num_devices=1)
    arrays, drams = {}, {}
    for name in _INPUTS:
        a = np.ascontiguousarray(inputs[name])
        if name == "L2_gnn_a_b":
            a = a.reshape(1, 1)
        arrays["in_" + name] = a
        drams[name] = nc.dram_tensor("in_" + name, a.shape, mybir.dt.from_np(a.dtype), kind="ExternalInput").ap()
    result = nc.dram_tensor("result", (N, D), F32, kind="ExternalOutput").ap()
    build(nc, drams, result)
    r = run_bass_kernel_spmd(nc, [arrays], core_ids=[0])
    return r.results[0]["result"]
```

```python
from contextlib import ExitStack

import concourse.bass as bass
from concourse import mybir

F32, F32R, BF16 = mybir.dt.float32, mybir.dt.float32r, mybir.dt.bfloat16
I32, U32 = mybir.dt.int32, mybir.dt.uint32
ALU = mybir.AluOpType
ACT = mybir.ActivationFunctionType
AX = mybir.AxisListType

P = 128
N = 1354
D = 256
KD = D // P
TILES = -(-N // P)
LAST = N - (TILES - 1) * P
NP = TILES * P
BANK = 512
CHUNKS = [(a, min(BANK, N - a)) for a in range(0, N, BANK)]
PCHUNKS = [(a, min(BANK, NP - a)) for a in range(0, NP, BANK)]
GROUPS = [(a, min(4, TILES - a)) for a in range(0, TILES, 4)]
NG = len(GROUPS)
EPS = 1e-5
NEG_BIG = -9e15
LOWEST = -3e38
ROUND = 12582912.0
E = 8
SLOTS = (2 * N + E * (P - 1)) // P
LAG = 2
NPROB, NADJ, NPT, RING = 3, 3, 3, 4
GE = 160
STAGES = ("L0_gnn", "L0_ffn", "L1_gnn", "L1_ffn", "L2_gnn", "L2_ffn", "L3_gnn", "L3_ffn")


def build(nc, d, out, stages=STAGES):
    with ExitStack() as ctx:
        def sem(name):
            return ctx.enter_context(nc.semaphore(name))

        base = (nc.sbuf_base + 31) // 32 * 32
        top = nc.sbuf_usable_end

        class Area:

            def __init__(self, at):
                self.at = at

            def __call__(self, name, shape, dt=F32):
                words = 1
                for s in shape[1:]:
                    words *= s
                t = nc.alloc_sbuf_tensor_at(name, list(shape), dt, offset=self.at)
                self.at += (words * (2 if dt == BF16 else 4) + 31) // 32 * 32
                assert self.at <= top, (name, self.at, top)
                return t

        keep = Area(base)
        resid = keep("resid", [P, TILES, D])
        normed_at = keep.at
        normed = keep("normed", [P, TILES, D])
        ident = keep("ident", [P, P])
        ones = keep("ones", [P, P])
        before_b = keep("before_b", [P, P], BF16)
        ones_b = keep("ones_b", [P, P], BF16)
        chosen_b = keep("chosen_b", [P, TILES, E], BF16)
        ones3 = keep("ones3", [3, P], BF16)
        valid = keep("valid", [P, TILES])
        invalid_bias = keep("invalid_bias", [P, TILES])
        stats = keep("stats", [P, TILES, 6])
        mean_var = keep("mean_var", [P, TILES, 2])
        var_eps = keep("var_eps", [P, TILES])
        std = keep("std", [P, TILES])
        rstd = keep("rstd", [P, TILES])
        chunk_max = keep("chunk_max", [P, TILES, NG])
        neg_max = keep("neg_max", [P, TILES])
        row_sum = keep("row_sum", [P, TILES])
        row_scale = keep("row_scale", [P, TILES])
        node_att = keep("node_att", [P, TILES])
        node_logit = keep("node_logit", [P, TILES])
        col = keep("col", [P, 5])
        deg = keep("deg", [P, TILES])
        first = keep("first", [P, TILES, E])
        second = keep("second", [P, TILES, E])
        gate = keep("gate", [P, TILES, 2])
        rank_down = keep("rank_down", [P, TILES, E])
        router_sb = [keep(f"router_sb{i}", [P, TILES, E]) for i in range(3)]
        best = keep("best", [P, TILES, 4])
        pos = keep("pos", [P, 2, TILES])
        steps128 = keep("steps128", [P, E, TILES])
        step_gt = keep("step_gt", [P, E, TILES])
        expert_lt = keep("expert_lt", [P, E, E])
        lt_prod = keep("lt_prod", [P, E, E])
        per_expert = keep("per_expert", [P, 4, E])
        slot_iota = keep("slot_iota", [P, SLOTS, E])
        slot_ge = keep("slot_ge", [P, SLOTS, E])
        slot_f = keep("slot_f", [P, SLOTS])
        slot_expert = keep("slot_expert", [P, SLOTS], I32)
        nib_w = keep("nib_w", [64, 2 * GE + 2])
        place_row = keep("place_row", [P, P], BF16)
        place_slot = keep("place_slot", [P, SLOTS], BF16)
        spare_row = keep("spare_row", [P, SLOTS])
        tile_p = keep("tile_p", [P, 2, 2, TILES])
        split_pos = keep("split_pos", [P, 2, 2, TILES])
        split_pos_b = keep("split_pos_b", [P, 2, 2, TILES], BF16)
        mapped = keep("mapped", [P, 2, SLOTS])
        source_f = keep("source_f", [P, SLOTS])
        target_f = keep("target_f", [P, SLOTS])
        spare_f = keep("spare_f", [P, SLOTS])
        map_base = keep("map_base", [P, SLOTS])
        source_row = keep("source_row", [P, SLOTS], U32)
        target_row = keep("target_row", [P, SLOTS], U32)
        shared_at = keep.at

        g0 = Area(shared_at)
        turned_hi = g0("turned_hi", [P, KD, NP], F32R)
        turned_lo = g0("turned_lo", [P, KD, NP], F32R)
        w_raw = g0("w_raw", [P, KD, 2 * D + 2])
        w_hi = g0("w_hi", [P, KD, 2 * D + 2], F32R)
        w_lo = g0("w_lo", [P, KD, 2 * D + 2], F32R)
        ATTENTION_BYTES = 4 * (TILES * D * 2 + KD * NP * 2 + NPROB * NP + NADJ * N + 2 * NPT * BANK + N + 4 * D) + 512
        g = Area((top - ATTENTION_BYTES) // 32 * 32)
        attention_at = g.at
        made = Area(attention_at + 4 * 2 * TILES * D)
        split_f = made("split_f", [80, 2, 3, P])
        split_b = made("split_b", [80, 2, 3, P], BF16)
        before = made("before", [P, P])
        values_hi = g("values_hi", [P, TILES, D], F32R)
        values_lo = g("values_lo", [P, TILES, D], F32R)
        q_hi = g("q_hi", [P, KD, NP], F32R)
        q_lo = g("q_lo", [P, KD, NP], F32R)
        probs = g("probs", [P, NPROB, NP])
        adj_rows = g("adj_rows", [P, NADJ, N])
        pt_hi = g("pt_hi", [P, NPT, BANK], F32R)
        pt_lo = g("pt_lo", [P, NPT, BANK], F32R)
        mask_bias = g("mask_bias", [P, 2, N], BF16)
        bias_row = g("bias_row", [P, D])
        biased = g("biased", [P, 3, D])
        k_at = (attention_at - 4 * (3 * N + D + 3 * KD * D + 2 * KD * P) - 512) // 32 * 32
        keys_at = attention_at - 4 * 2 * KD * NP
        g1 = Area(keys_at)
        k_hi = g1("k_hi", [P, KD, NP], F32R)
        k_lo = g1("k_lo", [P, KD, NP], F32R)
        g2 = Area(k_at)
        unscaled = g2("unscaled", [P, TILES, D])
        deg_part = g2("deg_part", [P, TILES, 12])
        g3 = Area(k_at)
        s2_row = g3("s2_row", [P, N])
        a_row = g3("a_row", [P, D])
        a_prod = g3("a_prod", [P, 2, KD, D], BF16)
        attn_w = g3("attn_w", [P, 2, KD])
        attn_raw = g3("attn_raw", [P, 2, KD, D])
        rep_hi = g3("rep_hi", [P, KD, P], F32R)
        rep_lo = g3("rep_lo", [P, KD, P], F32R)
        s1 = g3("s1", [P, TILES])
        s1_fifth = g3("s1_fifth", [P, TILES])
        ab = g3("ab", [P, 1])
        leaky = g3("leaky", [P, 2, N])
        assert g0.at <= min(k_at, keys_at) and max(g1.at, g2.at, g3.at) <= attention_at

        n = Area(shared_at)
        bit_w = n("bit_w", [P, TILES, 64])
        bits = n("bits", [P, TILES, 64])
        nib_max = n("nib_max", [P, TILES, 4])
        nib_rev = n("nib_rev", [P, TILES, 4])
        nib = n("nib", [P, TILES, 4])
        opf = n("opf", [P, TILES, 3])
        opn = n("opn", [P, TILES, 2])
        sel = n("sel", [P, TILES, 3])
        active = n("active", [P, TILES, 3])
        feat6 = n("feat6", [P, 2, TILES, 6])
        feats = n("feats", [P, TILES, 64])
        feats_t = n("feats_t", [64, TILES, P])
        hidden = n("hidden", [P, 2, 2, GE])
        nib_prod = n("nib_prod", [P, 2, 2, GE])
        res_b = n("res_b", [P, TILES, 1])
        res = n("res", [P, TILES, 2])
        digit = n("digit", [P, 2 * TILES, 16])
        onehot = n("onehot", [P, 2 * TILES, 16])

        m = Area(shared_at)
        expert_w = m("expert_w", [P, E * 4096])
        bias12 = m("bias12", [12, E, 2, P], BF16)
        bias3 = m("bias3", [3, E, D], BF16)
        block_of = m("block_of", [12, 4, P], BF16)
        m0 = Area(m.at)
        logits_t = m0("logits_t", [E, NP])
        block_of_f = m0("block_of_f", [12, 4, P])
        down_hi = m("down_hi", [P, 4, D], F32R)
        down_lo = m("down_lo", [P, 4, D], F32R)
        m.at = max(m.at, m0.at)
        m_at = m.at
        mturned_hi = m("mturned_hi", [P, KD, NP], F32R)
        mturned_lo = m("mturned_lo", [P, KD, NP], F32R)
        m2 = Area(m_at)
        slot_x = m2("slot_x", [P, 2, D])
        slot_xt = m2("slot_xt", [P, 2, KD, P])
        ht_hi = m2("ht_hi", [P, 2, BANK], F32R)
        ht_lo = m2("ht_lo", [P, 2, BANK], F32R)
        ht_rest = m2("ht_rest", [P, 2, BANK])
        slot_y = m2("slot_y", [P, 2, D])
        slot_w = [m2("slot_w0", [P, KD, 1024]), Area(normed_at)("slot_w1", [P, KD, 1024])]
        slot_silu = Area(shared_at + 4 * E * 3072)("slot_silu", [P, BANK])
        m5 = Area(m_at + 4 * 4 * D)
        place_hot = m5("place_hot", [P, 2 * TILES, P], BF16)
        slot_hot = m5("slot_hot", [P, 2 * TILES, SLOTS], BF16)
        slot_vals = m5("slot_vals", [P, 2 * TILES, 2, SLOTS], BF16)
        m3 = Area(max(m.at, m2.at, m5.at))
        router_raw = m3("router_raw", [P, KD, E])
        router_hi = m3("router_hi", [P, KD, E], F32R)
        router_lo = m3("router_lo", [P, KD, E], F32R)
        router_b = m3("router_b", [P, E])
        m4 = Area(shared_at)
        gathered = m4("gathered", [P, TILES, 2, D])

        f = Area(shared_at)
        nat_in = f("nat_in", [P, 2, 8, D])
        nat_out = f("nat_out", [P, E + 1, KD, BANK])
        assert f.at <= keys_at, (f.at, keys_at)
        f1 = Area(shared_at)
        act_silu = f1("act_silu", [P, 2, BANK])
        act_h = f1("act_h", [P, 2, BANK])
        act_t_hi = f1("act_t_hi", [P, 2, BANK], F32R)
        act_t_lo = f1("act_t_lo", [P, 2, BANK], F32R)
        f_turned_hi = f1("f_turned_hi", [P, KD, NP], F32R)
        f_turned_lo = f1("f_turned_lo", [P, KD, NP], F32R)
        f.at = max(f.at, f1.at)
        in_hi = f("in_hi", [P, 2, KD, 1024], F32R)
        in_lo = f("in_lo", [P, 2, KD, 1024], F32R)
        out_hi = f("out_hi", [P, 4, 9 * D], F32R)
        out_lo = f("out_lo", [P, 4, 9 * D], F32R)
        gate_nat = f("gate_nat", [E + 2, D])
        gate_hi = f("gate_hi", [P, KD, E + 2], F32R)
        gate_lo = f("gate_lo", [P, KD, E + 2], F32R)
        ln_rows = f("ln_rows", [P, 2, D])
        gate_b = f("gate_b", [P, E + 2])
        glog = f("glog", [P, TILES, E + 2])
        grp = f("grp", [P, TILES, 2])
        esel = f("esel", [P, 6, TILES, 4])
        pk = f("pk", [P, TILES, 4])
        comb = f("comb", [P, TILES, E])
        psel = f("psel", [P, 4, TILES])
        cnt = f("cnt", [P, TILES, E + 1])
        f_logits_t = Area(f.at)("f_logits_t", [E + 2, NP])
        cnt_t = f("cnt_t", [E + 1, TILES, P])
        bias9 = f("bias9", [E + 1, D])

        psum = ctx.enter_context(nc.psum_tensor("psum", [P, 8, BANK], F32))

        x_rows = nc.dram_tensor("x_rows", [NP, D], F32).ap()
        y_rows = nc.dram_tensor("y_rows", [2 * NP + SLOTS * P, D], F32).ap()
        bias_scratch = nc.dram_tensor("bias_scratch", [2, 3, E * 10, P], BF16).ap()

        stage_done = sem("stage_done")
        vector_step = sem("vector_step")
        scalar_step = sem("scalar_step")
        pool_step = sem("pool_step")
        consts_ready = sem("consts_ready")
        x_loaded = [sem(f"x_loaded{i}") for i in range(NG)]
        padding_zeroed = sem("padding_zeroed")
        out_stored = sem("out_stored")
        var_ready = sem("var_ready")
        std_ready = sem("std_ready")
        rows_normed = sem("rows_normed")
        block = ctx.enter_context(nc.Block())

        counts = {"v": 0, "s": 0, "p": 0, "norms": 0}

        def vstep(v, ins):
            counts["v"] += 1
            ins.then_inc(vector_step, 1)
            v.wait_ge(vector_step, counts["v"])

        def sstep(a, ins):
            counts["s"] += 1
            ins.then_inc(scalar_step, 1)
            a.wait_ge(scalar_step, counts["s"])

        def pstep(p, ins):
            counts["p"] += 1
            ins.then_inc(pool_step, 1)
            p.wait_ge(pool_step, counts["p"])

        def stage_end(eng, number):
            eng.drain().then_inc(stage_done, 1)
            eng.wait_ge(stage_done, 4 * number)

        def graph_items(layer):
            items = [("turn", i) for i in range(0, TILES, 2)]
            items.insert(2, ("weights",))
            if layer in ("L1_gnn", "L3a", "L3b"):
                items += [("features", "q", mb, c) for c in range(3) for mb in range(KD)]
            if layer in ("L3a", "L3b"):
                items += [("features", "k", mb, c) for c in range(3) for mb in range(KD)]
            items += [("values", t) for t in range(TILES)]
            if layer == "L2_gnn":
                items += [("s2", c) for c in range(3)]
            return items

        graph_layers = [s for s in stages if s.endswith("gnn")]
        graph_layers = [x for s in graph_layers for x in (("L3a", "L3b") if s == "L3_gnn" else (s,))]
        moe_layers = [s for s in stages if s in ("L1_ffn", "L2_ffn")]
        w_cols = {"L0_gnn": D, "L1_gnn": 2 * D + 2, "L2_gnn": D + 2, "L3a": 2 * D, "L3b": 2 * D}
        v_col = {"L0_gnn": 0, "L1_gnn": D, "L2_gnn": 0, "L3a": 0, "L3b": 0}

        class gs:
            w_loaded = sem("w_loaded")
            adj_loaded = [sem(f"adj_loaded{i}") for i in range(NADJ)]
            cleared = sem("cleared")
            item_ready = sem("item_ready")
            item_hi = sem("item_hi")
            item_done = sem("item_done")
            scores_ready = sem("scores_ready")
            scores_free = sem("scores_free")
            max_ready = sem("max_ready")
            exp_done = sem("exp_done")
            probs_ready = sem("probs_ready")
            adj_used = sem("adj_used")
            turned = sem("turned")
            pt_hi_ready = sem("pt_hi_ready")
            pt_ready = sem("pt_ready")
            pt_used = sem("pt_used")
            mixed_taken = sem("mixed_taken")
            node_max = sem("node_max")
            node_exp = sem("node_exp")
            node_sum = sem("node_sum")
            attn_split = sem("attn_split")
            biased_ready = sem("biased_ready")
            leaky_used = sem("leaky_used")
        w_dmas = {"L0_gnn": 2, "L1_gnn": 4, "L2_gnn": 5, "L3a": 1, "L3b": 1}

        def graph_counts(x):
            scored, items = x in ("L1_gnn", "L3a", "L3b"), len(graph_items(x))
            return dict(
                w_loaded=16 * w_dmas[x], cleared=1, item_ready=items - 1, item_hi=items, item_done=items,
                scores_ready=NG * TILES if scored else TILES if x == "L2_gnn" else 0,
                scores_free=NG * TILES if scored else 0, max_ready=TILES if x != "L0_gnn" else 0,
                exp_done=TILES if scored else 0, probs_ready=TILES, adj_used=TILES if x == "L2_gnn" else 0,
                turned=NG * TILES, pt_hi_ready=NG * TILES, pt_ready=NG * TILES, pt_used=NG * TILES,
                mixed_taken=TILES, node_max=2 if x == "L1_gnn" else 0, node_exp=1 if x == "L1_gnn" else 0,
                node_sum=1 if x == "L1_gnn" else 0, attn_split=KD if x == "L2_gnn" else 0,
                biased_ready=TILES + (x == "L2_gnn") if x in ("L0_gnn", "L2_gnn") else 0, leaky_used=TILES if x == "L2_gnn" else 0)

        gb = {}
        so_far, adj_so_far = {name: 0 for name in graph_counts("L0_gnn")}, [0] * NADJ
        for x in graph_layers:
            gb[x] = dict(adj_loaded=list(adj_so_far), **so_far)
            so_far = {name: so_far[name] + n_ for name, n_ in graph_counts(x).items()}
            adj_so_far = [adj_so_far[i] + 16 * len(range(i, TILES, NADJ)) for i in range(NADJ)]
        ml = {}
        for x in moe_layers:
            class sems:
                w_loaded = sem(f"{x}_w_loaded")
                r_loaded = sem(f"{x}_r_loaded")
                b_spread = sem(f"{x}_b_spread")
                item_ready = sem(f"{x}_item_ready")
                item_hi = sem(f"{x}_item_hi")
                item_done = sem(f"{x}_item_done")
                logits = sem(f"{x}_logits")
                gap = sem(f"{x}_gap")
                gap_exp = sem(f"{x}_gap_exp")
                chosen = sem(f"{x}_chosen")
                counted = sem(f"{x}_counted")
                placed = sem(f"{x}_placed")
                rows_stored = sem(f"{x}_rows_stored")
                hot_ready = sem(f"{x}_hot_ready")
                mapped = sem(f"{x}_mapped")
                sources_ready = sem(f"{x}_sources_ready")
                x_loaded = [sem(f"{x}_x_loaded{i}") for i in range(2)]
                x_turned = sem(f"{x}_x_turned")
                w_kept_s = sem(f"{x}_w_kept_s")
                w_kept_v = sem(f"{x}_w_kept_v")
                xt_ready = sem(f"{x}_xt_ready")
                h_ready = sem(f"{x}_h_ready")
                silu_kept = sem(f"{x}_silu_kept")
                h_hi = sem(f"{x}_h_hi")
                h_lo = sem(f"{x}_h_lo")
                down_hi_kept = sem(f"{x}_down_hi_kept")
                down_lo_kept = sem(f"{x}_down_lo_kept")
                h_kept_v = sem(f"{x}_h_kept_v")
                y_ready = sem(f"{x}_y_ready")
                y_kept = sem(f"{x}_y_kept")
                y_stored = [sem(f"{x}_y_stored{i}") for i in range(2)]
            ml[x] = sems
        if moe_layers:
            y_loaded = [sem(f"y_loaded{i}") for i in range(NG)]
            b_loaded = sem("b_loaded")
            b_split = sem("b_split")
            b_placed = sem("b_placed")

        class ns:
            w_zeroed = sem("nib_w_zeroed")
            w_loaded = sem("nib_w_loaded")
            feats_ready = sem("nib_feats_ready")
            turned = sem("nib_turned")
            turned_kept = sem("nib_turned_kept")
            hidden = sem("nib_hidden")
            relu = sem("nib_relu")
            used = sem("nib_used")
            iota = sem("nib_iota")
            added = sem("nib_added")
        class fs:
            loaded = sem("f_loaded")
            in_loaded = [sem(f"f_in_loaded{i}") for i in range(2)]
            out_loaded = sem("f_out_loaded")
            item_ready = sem("f_item_ready")
            item_hi = sem("f_item_hi")
            item_done = sem("f_item_done")
            rows_ready = sem("f_rows_ready")
            exp_in = sem("f_exp_in")
            exp_out = sem("f_exp_out")
            cnt_ready = sem("f_cnt_ready")
            cnt_turned = sem("f_cnt_turned")
            cnt_kept = sem("f_cnt_kept")
            h_ready = sem("f_h_ready")
            silu = sem("f_silu")
            h_kept = sem("f_h_kept")
            h_turned = sem("f_h_turned")
            ht_hi = sem("f_ht_hi")
            ht_done = sem("f_ht_done")
            ht_used = sem("f_ht_used")
            y_ready = sem("f_y_ready")
            y_used = sem("f_y_used")

        def pairs(hi, lo):
            return lambda *ix: (hi[ix], lo[ix])

        def product(eng, o, lhs, rhs, start, stop):
            eng.matmul(o, lhs[0], rhs[0], start=start, stop=False)
            eng.matmul(o, lhs[0], rhs[1], start=False, stop=False)
            return eng.matmul(o, lhs[1], rhs[0], start=False, stop=stop)

        def row_stats(v, t):
            v.bn_stats(stats[:, t, :], resid[:, t, :])

        def norm_vector(v, src, index):
            vstep(v, v.engine_nop())
            for t in range(TILES):
                ins = v.bn_aggr(mean_var[:, t, :], stats[:, t, :])
            vstep(v, ins)
            v.tensor_scalar(var_eps[:], mean_var[:, :, 1], EPS, None, ALU.add).then_inc(var_ready, 1)
            v.wait_ge(std_ready, index + 1)
            vstep(v, v.reciprocal(rstd[:], std[:]))
            for t in range(TILES):
                v.tensor_scalar(normed[:, t, :], src[:, t, :], mean_var[:, t, 0:1], rstd[:, t:t + 1],
                                ALU.subtract, ALU.mult).then_inc(rows_normed, 1)

        def sqrt_ahead(a):
            a.activation(col[:, 4:5], ones[:, 0:1], ACT.Sqrt)

        def norm_scalar(a, index):
            a.wait_ge(var_ready, index + 1)
            a.activation(std[:], var_eps[:], ACT.Sqrt).then_inc(std_ready, 1)

        def ring_free(eng, done, k, start=0):
            if k >= RING:
                eng.wait_ge(done, start + k - RING + 1)

        def turn_tensor(pe, i, k, wait_rows):
            for j in range(min(2, TILES - i)):
                pe.wait_ge(rows_normed, wait_rows + i + j + 1)
                for kb in range(KD):
                    ins = pe.transpose(psum[:, k % RING, kb * 256 + j * P:kb * 256 + (j + 1) * P],
                                       normed[:, i + j, kb * P:(kb + 1) * P], ident[:])
            return ins

        def turn_source(i, k):
            w = min(2, TILES - i) * P
            return psum[:, k % RING, :].rearrange("p (k n) -> p k n", k=KD)[:, :, 0:w], slice(i * P, i * P + w)

        def turn_banks(x):
            return 2 if x in ("L1_gnn", "L3a", "L3b") else 6

        def turn_bank(x, n_):
            return 4 + n_ % 2 if turn_banks(x) == 2 else n_ % 6

        def graph_tensor(pe, x, rows_base):
            s, b, items = gs, gb[x], graph_items(x)
            where = {it: k for k, it in enumerate(items)}
            turned, w = pairs(turned_hi, turned_lo), pairs(w_hi, w_lo)
            for k, it in enumerate(items):
                if it[0] == "weights":
                    continue
                ring_free(pe, s.item_done, k, b["item_done"])
                if it[0] == "turn":
                    ins = turn_tensor(pe, it[1], k, rows_base)
                elif it[0] == "features":
                    _, dst, mb, c = it
                    a, width = PCHUNKS[c]
                    last = max(where[("turn", min(4 * c + 2, (TILES - 1) // 2 * 2))], where[("weights",)])
                    pe.wait_ge(s.item_done, b["item_done"] + last + 1)
                    off = (D if dst == "k" else 0) + mb * P
                    for kb in range(KD):
                        ins = product(pe, psum[:, k % RING, 0:width], w(slice(None), kb, slice(off, off + P)),
                                      turned(slice(None), kb, slice(a, a + width)), kb == 0, kb == KD - 1)
                elif it[0] == "values":
                    t = it[1]
                    last = max(where[("turn", t // 2 * 2)], where[("weights",)])
                    pe.wait_ge(s.item_done, b["item_done"] + last + 1)
                    width = D + 2 if x in ("L1_gnn", "L2_gnn") else D
                    for kb in range(KD):
                        ins = product(pe, psum[:, k % RING, 0:width], turned(slice(None), kb, slice(t * P, t * P + P)),
                                      w(slice(None), kb, slice(v_col[x], v_col[x] + width)), kb == 0, kb == KD - 1)
                elif it[0] == "s2":
                    a, width = CHUNKS[it[1]]
                    pe.wait_ge(s.attn_split, b["attn_split"] + KD)
                    for kb in range(KD):
                        ins = product(pe, psum[:, k % RING, 0:width], pairs(rep_hi, rep_lo)(slice(None), kb, slice(None)),
                                      turned(slice(None), kb, slice(a, a + width)), kb == 0, kb == KD - 1)
                ins.then_inc(s.item_ready, 1)
            pe.wait_ge(s.item_done, b["item_done"] + len(items))

            q = pairs(q_hi, q_lo)
            keys = pairs(k_hi, k_lo) if x in ("L3a", "L3b") else q
            scored = x in ("L1_gnn", "L3a", "L3b")
            pt, vals = pairs(pt_hi, pt_lo), pairs(values_hi, values_lo)

            def scores(r):
                for c, (a, width) in enumerate(CHUNKS):
                    n_ = r * NG + c
                    if n_ >= RING:
                        pe.wait_ge(s.scores_free, b["scores_free"] + n_ - RING + 1)
                    for kb in range(KD):
                        ins = product(pe, psum[:, n_ % RING, 0:width], q(slice(None), kb, slice(r * P, r * P + P)),
                                      keys(slice(None), kb, slice(a, a + width)), kb == 0, kb == KD - 1)
                    ins.then_inc(s.scores_ready, 1)

            def turn(r, c):
                n_ = r * NG + c
                if n_ >= turn_banks(x):
                    pe.wait_ge(s.pt_ready, b["pt_ready"] + n_ - turn_banks(x) + 1)
                a, w_ = GROUPS[c]
                for j in range(w_):
                    ins = pe.transpose(psum[:, turn_bank(x, n_), j * P:(j + 1) * P],
                                       probs[:, r % NPROB, (a + j) * P:(a + j + 1) * P], ident[:])
                ins.then_inc(s.turned, 1)

            def mix(r, c):
                n_ = r * NG + c
                pe.wait_ge(s.pt_ready, b["pt_ready"] + n_ + 1)
                a, w_ = GROUPS[c]
                o = psum[:, 6 + r % 2, 0:D]
                for j in range(w_):
                    l = pt(slice(None), n_ % NPT, slice(j * P, (j + 1) * P))
                    rr = vals(slice(None), a + j, slice(None))
                    st, sp = c == 0 and j == 0, c == NG - 1 and j == w_ - 1
                    if x == "L0_gnn":
                        pe.matmul(o, l[0], rr[0], start=st, stop=False)
                        ins = pe.matmul(o, l[0], rr[1], start=False, stop=sp)
                    else:
                        ins = product(pe, o, l, rr, st, sp)
                ins.then_inc(s.pt_used, 1)

            pe.wait_ge(s.cleared, b["cleared"] + 1)
            for r in range(0 if scored else TILES + 1):
                if r < TILES:
                    pe.wait_ge(s.probs_ready, b["probs_ready"] + r + 1)
                    for c in range(NG):
                        turn(r, c)
                if r >= 1:
                    if r >= 3:
                        pe.wait_ge(s.mixed_taken, b["mixed_taken"] + r - 2)
                    for c in range(NG):
                        mix(r - 1, c)
            for i in range(TILES + LAG if scored else 0):
                r = i - LAG
                if r >= 0:
                    pe.wait_ge(s.probs_ready, b["probs_ready"] + r + 1)
                    turn(r, 0)
                    turn(r, 1)
                if i < TILES and scored:
                    scores(i)
                if r >= 0:
                    if r >= 2:
                        pe.wait_ge(s.mixed_taken, b["mixed_taken"] + r - 1)
                    mix(r, 0)
                    turn(r, 2)
                    mix(r, 1)
                    mix(r, 2)

        def graph_scalar(a, x):
            s, b, items = gs, gb[x], graph_items(x)
            n_pe = 0
            for k, it in enumerate(items):
                if it[0] == "weights":
                    a.wait_ge(s.w_loaded, b["w_loaded"] + 16 * w_dmas[x])
                    a.wait_ge(s.cleared, b["cleared"] + 1)
                    if x == "L2_gnn":
                        a.wait_ge(s.attn_split, b["attn_split"] + KD)
                    a.copy(w_hi[:, :, 0:w_cols[x]], w_raw[:, :, 0:w_cols[x]]).then_inc(s.item_hi, 1)
                    continue
                n_pe += 1
                a.wait_ge(s.item_ready, b["item_ready"] + n_pe)
                bank = psum[:, k % RING, :]
                if it[0] == "turn":
                    src, cols = turn_source(it[1], k)
                    ins = a.copy(turned_hi[:, :, cols], src)
                elif it[0] == "features":
                    _, dst, mb, c = it
                    at, width = PCHUNKS[c]
                    ins = a.copy((q_hi if dst == "q" else k_hi)[:, mb, at:at + width], bank[:, 0:width])
                elif it[0] == "values":
                    if x in ("L0_gnn", "L2_gnn"):
                        a.wait_ge(s.biased_ready, b["biased_ready"] + it[1] + 1)
                        ins = a.copy(values_hi[:, it[1], :], biased[:, it[1] % 3, :])
                    else:
                        ins = a.copy(values_hi[:, it[1], :], bank[:, 0:D])
                else:
                    at, width = CHUNKS[it[1]]
                    ins = a.copy(s2_row[:, at:at + width], bank[:, 0:width])
                ins.then_inc(s.item_hi, 1)
            if x == "L1_gnn":
                a.wait_ge(s.node_max, b["node_max"] + 2)
                a.activation(node_att[:], node_logit[:], ACT.Exp, bias=col[:, 1:2],
                             accum_out=col[:, 2:3]).then_inc(s.node_exp, 1)
            if x == "L2_gnn":
                a.wait_ge(s.item_done, b["item_done"] + len(items))
                a.wait_ge(s.biased_ready, b["biased_ready"] + TILES + 1)

            def slope(r):
                if r >= 2:
                    a.wait_ge(s.leaky_used, b["leaky_used"] + r - 1)
                a.activation(leaky[:, r % 2, :], s2_row[:], ACT.Identity, bias=s1_fifth[:, r:r + 1],
                             scale=0.2).then_inc(s.scores_ready, 1)

            def exp(r):
                a.wait_ge(s.max_ready, b["max_ready"] + r + 1)
                a.activation(probs[:, r % NPROB, 0:N], probs[:, r % NPROB, 0:N], ACT.Exp, bias=neg_max[:, r:r + 1],
                             accum_out=row_sum[:, r:r + 1]).then_inc(s.exp_done if x != "L2_gnn" else s.probs_ready, 1)

            def hi(r, c):
                n_ = r * NG + c
                a.wait_ge(s.turned, b["turned"] + n_ + 1)
                if n_ >= NPT:
                    a.wait_ge(s.pt_used, b["pt_used"] + n_ - NPT + 1)
                w_ = GROUPS[c][1] * P
                a.copy(pt_hi[:, n_ % NPT, 0:w_], psum[:, turn_bank(x, n_), 0:w_]).then_inc(s.pt_hi_ready, 1)

            for i in range(TILES + LAG):
                if x == "L2_gnn" and i < TILES:
                    slope(i)
                if i >= LAG:
                    hi(i - LAG, 0)
                    hi(i - LAG, 1)
                if x != "L0_gnn" and 1 <= i <= TILES:
                    exp(i - 1)
                if i >= LAG:
                    hi(i - LAG, 2)

        def graph_vector(v, x):
            s, b, items = gs, gb[x], graph_items(x)
            masked = x == "L1_gnn"
            if x == "L2_gnn":
                v.wait_ge(s.w_loaded, b["w_loaded"] + 16 * w_dmas[x])
                v.wait_ge(s.cleared, b["cleared"] + 1)
                for half in range(2):
                    for kb in range(KD):
                        to = w_raw[:, kb, D:D + 1] if half == 0 else attn_w[:, 1, kb:kb + 1]
                        ins = v.tensor_tensor_reduce(a_prod[:, half, kb, :], attn_raw[:, half, kb, :], a_row[:], 1.0, 0.0,
                                                     ALU.mult, ALU.add, to)
                vstep(v, ins)
                for kb in range(KD):
                    vstep(v, v.tensor_scalar(rep_hi[:, kb, :], ones[:], attn_w[:, 1, kb:kb + 1], None, ALU.mult))
                    v.scalar_tensor_tensor(rep_lo[:, kb, :], ones[:], attn_w[:, 1, kb:kb + 1],
                                           rep_hi[:, kb, :].bitcast(F32), ALU.mult, ALU.subtract).then_inc(s.attn_split, 1)
            n_pe = 0

            def add_bias(t, k, nth):
                bank = psum[:, k % RING, :]
                v.wait_ge(s.w_loaded, b["w_loaded"] + 16 * w_dmas[x])
                v.wait_ge(s.item_ready, b["item_ready"] + nth)
                if x == "L2_gnn":
                    v.tensor_scalar(s1[:, t:t + 1], bank[:, D:D + 1], ab[:, 0:1], None, ALU.add)
                v.tensor_tensor(biased[:, t % 3, :], bank[:, 0:D], bias_row[:], ALU.add).then_inc(s.biased_ready, 1)

            for k, it in enumerate(items):
                bank = psum[:, k % RING, :]
                n_pe += it[0] != "weights"
                if it[0] == "values" and x in ("L0_gnn", "L2_gnn"):
                    t = it[1]
                    if t == 0:
                        add_bias(0, k, n_pe)
                    if t + 1 < TILES:
                        if t >= 2:
                            v.wait_ge(s.item_done, b["item_done"] + k - 1)
                        add_bias(t + 1, k + 1, n_pe + 1)
                    v.wait_ge(s.item_hi, b["item_hi"] + k + 1)
                    v.tensor_tensor(values_lo[:, t, :], biased[:, t % 3, :], values_hi[:, t, :].bitcast(F32),
                                    ALU.subtract).then_inc(s.item_done, 1)
                    continue
                v.wait_ge(s.item_hi, b["item_hi"] + k + 1)
                if it[0] == "weights":
                    ins = v.tensor_tensor(w_lo[:, :, 0:w_cols[x]], w_raw[:, :, 0:w_cols[x]],
                                          w_hi[:, :, 0:w_cols[x]].bitcast(F32), ALU.subtract)
                elif it[0] == "turn":
                    src, cols = turn_source(it[1], k)
                    ins = v.tensor_tensor(turned_lo[:, :, cols], src, turned_hi[:, :, cols].bitcast(F32), ALU.subtract)
                elif it[0] == "features":
                    _, dst, mb, c = it
                    at, width = PCHUNKS[c]
                    h_, l_ = (q_hi, q_lo) if dst == "q" else (k_hi, k_lo)
                    ins = v.tensor_tensor(l_[:, mb, at:at + width], bank[:, 0:width],
                                          h_[:, mb, at:at + width].bitcast(F32), ALU.subtract)
                elif it[0] == "values":
                    t = it[1]
                    if x == "L1_gnn":
                        v.tensor_copy(node_logit[:, t:t + 1], bank[:, D:D + 1])
                    ins = v.tensor_tensor(values_lo[:, t, :], bank[:, 0:D], values_hi[:, t, :].bitcast(F32), ALU.subtract)
                else:
                    ins = v.engine_nop()
                ins.then_inc(s.item_done, 1)
            if x == "L2_gnn":
                v.tensor_scalar(s1_fifth[:], s1[:], 0.2, None, ALU.mult).then_inc(s.biased_ready, 1)
            v.wait_ge(s.item_done, b["item_done"] + len(items))
            if x == "L1_gnn":
                vstep(v, v.tensor_tensor(node_logit[:], node_logit[:], valid[:], ALU.mult))
                vstep(v, v.tensor_tensor(node_logit[:], node_logit[:], invalid_bias[:], ALU.add))
                v.tensor_reduce(col[:, 0:1], node_logit[:], AX.X, ALU.max).then_inc(s.node_max, 1)

            def leaky_scores(r):
                pr = probs[:, r % NPROB, 0:N]
                if r >= NPROB:
                    v.wait_ge(s.turned, b["turned"] + (r - NPROB + 1) * NG)
                v.wait_ge(s.scores_ready, b["scores_ready"] + r + 1)
                v.scalar_tensor_tensor(pr, s2_row[:], s1[:, r:r + 1], leaky[:, r % 2, :],
                                       ALU.add, ALU.max).then_inc(s.leaky_used, 1)

            def masked_max(r):
                pr, mb = probs[:, r % NPROB, 0:N], mask_bias[:, r % 2, :]
                v.wait_ge(s.leaky_used, b["leaky_used"] + r + 1)
                v.wait_ge(s.adj_used, b["adj_used"] + r + 1)
                vstep(v, v.tensor_tensor_reduce(pr, pr, mb, 1.0, LOWEST, ALU.add, ALU.max, chunk_max[:, r, 0:1]))
                v.tensor_scalar(neg_max[:, r:r + 1], chunk_max[:, r, 0:1], -1.0, None, ALU.mult).then_inc(s.max_ready, 1)

            def front(r):
                pr, ad = probs[:, r % NPROB, 0:N], adj_rows[:, r % NADJ, :]
                if r >= NPROB:
                    v.wait_ge(s.turned, b["turned"] + (r - NPROB + 1) * NG)
                if x == "L0_gnn":
                    v.wait_ge(s.adj_loaded[r % NADJ], b["adj_loaded"][r % NADJ] + 16 * (r // NADJ + 1))
                    v.tensor_scalar(pr, ad, 0.0, None, ALU.not_equal).then_inc(s.probs_ready, 1)
                    return
                mb = mask_bias[:, r % 2, :]
                if x == "L1_gnn":
                    v.wait_ge(s.adj_loaded[r % NADJ], b["adj_loaded"][r % NADJ] + 16 * (r // NADJ + 1))
                    vstep(v, v.tensor_scalar(mb, ad, 0.0, NEG_BIG, ALU.is_le, ALU.mult))
                for c, (at, width) in enumerate(CHUNKS):
                    n_ = r * NG + c
                    v.wait_ge(s.scores_ready, b["scores_ready"] + n_ + 1)
                    bank = psum[:, n_ % RING, 0:width]
                    if masked:
                        ins = v.tensor_tensor_reduce(pr[:, at:at + width], bank, mb[:, at:at + width], 1.0, LOWEST,
                                                     ALU.add, ALU.max, chunk_max[:, r, c:c + 1])
                    else:
                        ins = v.tensor_scalar(pr[:, at:at + width], bank, 1.0, None, ALU.mult, ALU.max,
                                              accum_out=chunk_max[:, r, c:c + 1])
                    ins.then_inc(s.scores_free, 1)
                v.wait_ge(s.scores_free, b["scores_free"] + (r + 1) * NG)
                v.tensor_reduce(neg_max[:, r:r + 1], chunk_max[:, r, :], AX.X, ALU.max, negate=True).then_inc(s.max_ready, 1)

            def lo(r, c):
                n_ = r * NG + c
                v.wait_ge(s.pt_hi_ready, b["pt_hi_ready"] + n_ + 1)
                a_, w_ = GROUPS[c]
                if x == "L0_gnn":
                    rows = LAST if r == TILES - 1 else P
                    v.tensor_reduce(deg_part[:, r, a_:a_ + w_],
                                    psum[:, turn_bank(x, n_), 0:w_ * P].rearrange("p (b n) -> p b n", n=P)[:, :, 0:rows],
                                    AX.X, ALU.add).then_inc(s.pt_ready, 1)
                else:
                    v.tensor_tensor(pt_lo[:, n_ % NPT, 0:w_ * P], psum[:, turn_bank(x, n_), 0:w_ * P],
                                    pt_hi[:, n_ % NPT, 0:w_ * P].bitcast(F32), ALU.subtract).then_inc(s.pt_ready, 1)

            def back(r):
                v.wait_ge(s.pt_used, b["pt_used"] + (r + 1) * NG)
                o = psum[:, 6 + r % 2, 0:D]
                if x == "L0_gnn":
                    v.tensor_copy(unscaled[:, r, :], o).then_inc(s.mixed_taken, 1)
                    return
                vstep(v, v.reciprocal(row_scale[:, r:r + 1], row_sum[:, r:r + 1]))
                if x == "L1_gnn":
                    vstep(v, v.tensor_tensor(row_scale[:, r:r + 1], row_scale[:, r:r + 1], node_att[:, r:r + 1], ALU.mult))
                if x in ("L1_gnn", "L2_gnn"):
                    v.scalar_tensor_tensor(resid[:, r, :], o, row_scale[:, r:r + 1], resid[:, r, :],
                                           ALU.mult, ALU.add).then_inc(s.mixed_taken, 1)
                else:
                    ins = v.scalar_tensor_tensor(normed[:, r, :], o, row_scale[:, r:r + 1], normed[:, r, :],
                                                 ALU.mult, ALU.add)
                    ins.then_inc(s.mixed_taken, 1)
                    v.wait_ge(s.mixed_taken, b["mixed_taken"] + r + 1)
                    v.scalar_tensor_tensor(normed[:, r, :], normed[:, r, :], 0.01, normed[:, r, :],
                                           ALU.mult, ALU.max).then_inc(rows_normed, 1)
                    if x == "L3b":
                        v.wait_ge(rows_normed, counts["rows_end_" + x] - TILES + r + 1)
                        vstep(v, v.tensor_tensor(resid[:, r, :], resid[:, r, :], normed[:, r, :], ALU.add))
                        row_stats(v, r)

            for i in range(TILES + LAG + 1):
                if LAG <= i < TILES + LAG:
                    lo(i - LAG, 0)
                    lo(i - LAG, 1)
                if x == "L2_gnn" and i < TILES:
                    leaky_scores(i)
                if LAG <= i < TILES + LAG:
                    lo(i - LAG, 2)
                if i > LAG:
                    back(i - LAG - 1)
                if x == "L2_gnn" and i < TILES:
                    masked_max(i)
                elif i < TILES:
                    front(i)
                if x == "L1_gnn" and i == 1:
                    v.wait_ge(s.node_sum, b["node_sum"] + 1)
                    vstep(v, v.reciprocal(col[:, 3:4], col[:, 3:4]))
                    vstep(v, v.tensor_scalar(node_att[:], node_att[:], col[:, 3:4], None, ALU.mult))
                if i > LAG + 1 and x in ("L1_gnn", "L2_gnn"):
                    v.wait_ge(s.mixed_taken, b["mixed_taken"] + i - LAG - 1)
                    row_stats(v, i - LAG - 2)
            if x in ("L1_gnn", "L2_gnn"):
                v.wait_ge(s.mixed_taken, b["mixed_taken"] + TILES)
                row_stats(v, TILES - 1)
            if x == "L0_gnn":
                v.wait_ge(s.pt_ready, b["pt_ready"] + TILES * NG)
                vstep(v, v.tensor_reduce(deg[:], deg_part[:, :, 0:TILES].rearrange("p r b -> p b r"), AX.X, ALU.add))
                vstep(v, v.scalar_tensor_tensor(deg[:], valid[:], -1.0, deg[:], ALU.mult, ALU.add))
                vstep(v, v.tensor_scalar(deg[:], deg[:], 1.0, None, ALU.add))
                vstep(v, v.reciprocal(row_scale[:], deg[:]))
                v.wait_ge(s.mixed_taken, b["mixed_taken"] + TILES)
                for t in range(TILES):
                    ins = v.scalar_tensor_tensor(resid[:, t, :], unscaled[:, t, :], row_scale[:, t:t + 1],
                                                 resid[:, t, :], ALU.mult, ALU.add)
                vstep(v, ins)
                for t in range(TILES):
                    row_stats(v, t)

        def graph_pool(p, x):
            s, b = gs, gb[x]
            p.memset({"L1_gnn": w_raw[:, :, 2 * D + 1:2 * D + 2], "L2_gnn": w_raw[:, :, D:D + 2]}.get(
                x, w_raw[:, :, 2 * D:2 * D + 2]), 0.0)
            p.memset(probs[:, :, N:NP], 0.0).then_inc(s.cleared, 1)
            if x == "L1_gnn":
                p.wait_ge(s.node_max, b["node_max"] + 1)
                pstep(p, p.partition_all_reduce(col[:, 1:2], col[:, 0:1], P, bass.bass_isa.ReduceOp.max))
                p.tensor_scalar(col[:, 1:2], col[:, 1:2], -1.0, 0.0, ALU.mult, ALU.add).then_inc(s.node_max, 1)
                p.wait_ge(s.w_loaded, b["w_loaded"] + 16 * w_dmas[x])
                for t in range(TILES):
                    ins = p.tensor_tensor(resid[:, t, :], resid[:, t, :], bias_row[:], ALU.add)
                p.wait_ge(s.node_exp, b["node_exp"] + 1)
                p.partition_all_reduce(col[:, 3:4], col[:, 2:3], P, bass.bass_isa.ReduceOp.add).then_inc(s.node_sum, 1)
            if x == "L2_gnn":
                for r in range(TILES):
                    p.wait_ge(s.adj_loaded[r % NADJ], b["adj_loaded"][r % NADJ] + 16 * (r // NADJ + 1))
                    if r >= 2:
                        p.wait_ge(s.max_ready, b["max_ready"] + r - 1)
                    p.tensor_scalar(mask_bias[:, r % 2, :], adj_rows[:, r % NADJ, :], 0.0, NEG_BIG,
                                    ALU.is_le, ALU.mult).then_inc(s.adj_used, 1)
            if x in ("L1_gnn", "L3a", "L3b"):
                for r in range(TILES):
                    p.wait_ge(s.exp_done, b["exp_done"] + r + 1)
                    p.wait_ge(s.adj_loaded[r % NADJ], b["adj_loaded"][r % NADJ] + 16 * (r // NADJ + 1))
                    ins = p.tensor_tensor(probs[:, r % NPROB, 0:N], probs[:, r % NPROB, 0:N], adj_rows[:, r % NADJ, :],
                                          ALU.mult)
                    ins.then_inc(s.probs_ready, 1)

        def load_weights(q, x):
            s, b = gs, gb[x]

            def put(dst, src):
                q.dma_start(dst, src).then_inc(s.w_loaded, 16)

            def rows(w):
                return w.rearrange("(k p) n -> p k n", p=P)

            def every(b):
                return b.rearrange("(o n) -> o n", o=1).to_broadcast([P, D])

            if x == "L0_gnn":
                put(w_raw[:, :, 0:D], rows(d["L0_gnn_W"]))
                put(bias_row[:], every(d["L0_gnn_b"]))
            elif x == "L1_gnn":
                put(w_raw[:, :, 0:D], rows(d["L1_gnn_edge_w"]))
                put(w_raw[:, :, D:2 * D], rows(d["L1_gnn_weight"]))
                with nc.allow_non_contiguous_dma(reason="one column of 256 numbers"):
                    put(w_raw[:, :, 2 * D:2 * D + 1], rows(d["L1_gnn_node_w"]))
                put(bias_row[:], every(d["L1_gnn_bias"]))
            elif x == "L2_gnn":
                put(w_raw[:, :, 0:D], rows(d["L2_gnn_fc_w"]))
                put(attn_raw[:], d["L2_gnn_W"].rearrange("(h k p) n -> p h k n", h=2, p=P))
                put(bias_row[:], every(d["L2_gnn_fc_b"]))
                put(a_row[:], every(d["L2_gnn_a_w"]))
                put(ab[:], d["L2_gnn_a_b"].to_broadcast([P, 1]))
            else:
                put(w_raw[:, :, 0:2 * D], rows(d["L3_gnn_W_stack"][0 if x == "L3a" else 1]))

        def load_adjacency(q, x, ahead):
            s, b = gs, gb[x]
            for r in range(TILES):
                if r >= NADJ:
                    if x == "L2_gnn":
                        q.wait_ge(s.adj_used, b["adj_used"] + r - NADJ + 1)
                    else:
                        q.wait_ge(s.probs_ready, b["probs_ready"] + r - NADJ + 1)
                rows = LAST if r == TILES - 1 else P
                q.dma_start(adj_rows[0:rows, r % NADJ, :], d["adj"][r * P:r * P + rows, :]).then_inc(
                    s.adj_loaded[r % NADJ], 16)
                if r == NADJ:
                    q.wait_ge(s.item_done, b["item_done"] + len(graph_items(x)))
                if r >= NADJ:
                    for load in ahead[(r - NADJ) * 2:(r - NADJ) * 2 + 2]:
                        load()

        def load_nibble_weights(q):
            q.wait_ge(ns.w_zeroed, 1)
            for o, op in enumerate(("and", "or", "xor")):
                w1, b1 = d[f"L0_ffn_{op}_w1"], d[f"L0_ffn_{op}_b1"]
                w2, b2 = d[f"L0_ffn_{op}_w2"], d[f"L0_ffn_{op}_b2"]
                r = 6 * o
                with nc.allow_non_contiguous_dma(reason="one column of the second layer"):
                    for dst, src in ((nib_w[r:r + 2, 0:GE], w1[0:2, :]), (nib_w[r + 2:r + 5, 0:GE], w1[44:47, :]),
                                     (nib_w[r + 5:r + 6, 0:GE], b1.rearrange("(o n) -> o n", o=1)),
                                     (nib_w[r + 5:r + 6, GE:2 * GE], w2[:, 64:65].rearrange("n o -> o n")),
                                     (nib_w[r + 5:r + 6, 2 * GE:2 * GE + 1], b2.rearrange("(o n) -> o n", o=1)[:, 64:65])):
                        q.dma_start(dst, src).then_inc(ns.w_loaded, 16)
            q.wait_ge(ns.w_loaded, 16 * 15)
            q.dma_start(nib_w[32:50, :], nib_w[0:18, :]).then_inc(ns.w_loaded, 16)

        NIB_BANKS = 2

        def nibble_pool(p, rows_base):
            p.iota(bit_w[:].rearrange("p t (k j) -> p t k j", j=16), pattern=[[0, TILES], [0, 4], [-1, 16]], base=16,
                   channel_multiplier=0, allow_small_or_imprecise_dtypes=True)
            p.iota(digit[:], pattern=[[0, 2 * TILES], [1, 16]], base=0, channel_multiplier=0,
                   allow_small_or_imprecise_dtypes=True)
            p.memset(feats[:], 0.0).then_inc(ns.iota, 1)
            p.wait_ge(rows_normed, rows_base + TILES)
            p.tensor_tensor(resid[:], resid[:], normed[:], ALU.add).then_inc(ns.added, 1)

        def nibble_vector(v, rows_base):
            v.wait_ge(ns.iota, 1)
            v.wait_ge(rows_normed, rows_base + TILES)
            vstep(v, v.scalar_tensor_tensor(bits[:], normed[:, :, 16:80], 0.5, bit_w[:], ALU.is_gt, ALU.mult))
            vstep(v, v.tensor_reduce(nib_max[:].rearrange("p t k -> p (t k)"),
                                     bits[:].rearrange("p t (k j) -> p (t k) j", j=16), AX.X, ALU.max))
            vstep(v, v.tensor_scalar(nib_rev[:], nib_max[:], -1.0, 16.0, ALU.mult, ALU.add))
            v.scalar_tensor_tensor(nib[:], nib_max[:], 0.0, nib_rev[:], ALU.is_gt, ALU.mult)
            vstep(v, v.tensor_scalar(opf[:], normed[:, :, 1:4], 0.5, None, ALU.is_gt))
            vstep(v, v.tensor_scalar(opn[:], opf[:, :, 0:2], -1.0, 1.0, ALU.mult, ALU.add))
            v.tensor_copy(sel[:, :, 0:1], opf[:, :, 0:1])
            v.tensor_tensor(sel[:, :, 1:2], opf[:, :, 1:2], opn[:, :, 0:1], ALU.mult)
            v.tensor_tensor(sel[:, :, 2:3], opn[:, :, 0:1], opn[:, :, 1:2], ALU.mult)
            vstep(v, v.tensor_tensor(active[:, :, 0:1], opf[:, :, 0:1], opf[:, :, 1:2], ALU.max))
            vstep(v, v.tensor_tensor(active[:, :, 1:2], active[:, :, 0:1], opf[:, :, 2:3], ALU.max))
            vstep(v, v.scalar_tensor_tensor(active[:, :, 2:3], normed[:, :, 0:1], 0.5, active[:, :, 1:2],
                                            ALU.is_ge, ALU.mult))
            vstep(v, v.tensor_scalar(active[:, :, 0:1], active[:, :, 2:3], 2.0, None, ALU.mult))
            for row in range(2):
                v.tensor_copy(feat6[:, row, :, 0:1], nib[:, :, row:row + 1])
                v.tensor_copy(feat6[:, row, :, 1:2], nib[:, :, 2 + row:3 + row])
                v.tensor_copy(feat6[:, row, :, 2:4], normed[:, :, 2:4])
                v.tensor_copy(feat6[:, row, :, 4:5], normed[:, :, 1:2])
                ins = v.memset(feat6[:, row, :, 5:6], 1.0)
            vstep(v, ins)
            for row in range(2):
                for o in range(3):
                    at = 32 * row + 6 * o
                    ins = v.tensor_tensor(feats[:, :, at:at + 6], feat6[:, row, :, :],
                                          sel[:, :, o:o + 1].to_broadcast([P, TILES, 6]), ALU.mult)
            ins.then_inc(ns.feats_ready, 1)
            for t in range(TILES):
                bank = psum[:, 4 + t % NIB_BANKS, :]
                v.wait_ge(ns.relu, t + 1)
                for row in range(2):
                    v.tensor_tensor_reduce(nib_prod[:, t % 2, row, :], hidden[:, t % 2, row, :], bank[:, GE:2 * GE], 1.0, 0.0,
                                           ALU.mult, ALU.add, res[:, t, row:row + 1])
                v.tensor_copy(res_b[:, t, :], bank[:, 2 * GE:2 * GE + 1]).then_inc(ns.used, 1)
            v.wait_ge(ns.used, TILES)
            vstep(v, v.tensor_tensor(res[:], res[:], res_b[:].to_broadcast([P, TILES, 2]), ALU.add))
            vstep(v, v.tensor_scalar(res[:], res[:], 0.0, 15.0, ALU.max, ALU.min))
            vstep(v, v.tensor_scalar(res[:], res[:], ROUND, ROUND, ALU.add, ALU.subtract))
            vstep(v, v.tensor_tensor(onehot[:], digit[:], res[:].rearrange("p t (r o) -> p (t r) o", o=1)
                                     .to_broadcast([P, 2 * TILES, 16]), ALU.is_equal))
            both = onehot[:].rearrange("p (t r) j -> p t (r j)", r=2)
            vstep(v, v.tensor_tensor(both, both, active[:, :, 0:1].to_broadcast([P, TILES, 32]), ALU.mult))
            v.wait_ge(ns.added, 1)
            vstep(v, v.tensor_tensor(resid[:, :, 80:112], resid[:, :, 80:112], both, ALU.add))
            for t in range(TILES):
                row_stats(v, t)

        def nibble_scalar(a):
            for c, (t0, w_) in enumerate(GROUPS):
                a.wait_ge(ns.turned, c + 1)
                a.copy(feats_t[:, t0:t0 + w_, :], psum[0:64, c, 0:w_ * P].rearrange("p (t n) -> p t n", n=P)).then_inc(
                    ns.turned_kept, 1)
            for t in range(TILES):
                a.wait_ge(ns.hidden, t + 1)
                if t >= 2:
                    a.wait_ge(ns.used, t - 1)
                a.activation(hidden[:, t % 2, 0, :], psum[:, 4 + t % NIB_BANKS, 0:GE], ACT.Relu)
                a.activation(hidden[:, t % 2, 1, :], psum[:, 6 + t % NIB_BANKS, 0:GE],
                             ACT.Relu).then_inc(ns.relu, 1)

        def nibble_tensor(pe):
            pe.wait_ge(ns.feats_ready, 1)
            for c, (t0, w_) in enumerate(GROUPS):
                for j in range(w_):
                    ins = pe.transpose(psum[0:64, c, j * P:(j + 1) * P], feats[:, t0 + j, :], ident[:])
                ins.then_inc(ns.turned, 1)
            pe.wait_ge(ns.w_loaded, 16 * 16)
            for t in range(TILES):
                pe.wait_ge(ns.turned_kept, t // 4 + 1)
                if t >= NIB_BANKS:
                    pe.wait_ge(ns.used, t - NIB_BANKS + 1)
                pe.matmul(psum[:, 4 + t % NIB_BANKS, 0:2 * GE + 1], feats_t[0:18, t, :], nib_w[0:18, 0:2 * GE + 1], start=True, stop=True)
                pe.matmul(psum[:, 6 + t % NIB_BANKS, 0:GE], feats_t[32:50, t, :], nib_w[32:50, 0:GE],
                          start=True, stop=True).then_inc(ns.hidden, 1)

        MOE = {"L1_ffn": ("L1_ffn_W1", "L1_ffn_b1", "L1_ffn_W2", "L1_ffn_b2", "L1_ffn_Wr"),
               "L2_ffn": ("L2_ffn_Wgu", "L2_ffn_bgu", "L2_ffn_Wd", "L2_ffn_bd", "L2_ffn_Wg")}
        UP = KD * 1024
        up_w = expert_w[:, 0:E * UP].rearrange("p (e k n) -> p e k n", e=E, k=KD)
        down = {x: expert_w[:, E * UP:E * (UP + kh * D)].rearrange("p (e k n) -> p e k n", e=E, k=kh)
                for x, kh in (("L1_ffn", 8), ("L2_ffn", 4))}

        y_loads = [32, 32, 64]

        def logit_items():
            turns = [("turn", i) for i in range(0, TILES, 2)]
            return (turns[0:3] + [("chunk", 0)] + turns[3:5] + [("chunk", 1)] + turns[5:] + [("chunk", 2), ("logits",)])

        def moe_items():
            return [("weights",)] + logit_items()

        def logits_tensor(pe, it, items, k, width, turned, w, logits_t, done):
            if it[0] == "chunk":
                a_, cols = PCHUNKS[it[1]]
                pe.wait_ge(done, items.index(("turn", min(4 * it[1] + 2, (TILES - 1) // 2 * 2))) + 1)
                for kb in range(KD):
                    ins = product(pe, psum[0:width, k % RING, 0:cols], w(slice(None), kb, slice(None)),
                                  turned(slice(None), kb, slice(a_, a_ + cols)), kb == 0, kb == KD - 1)
            else:
                pe.wait_ge(done, k)
                for t in range(TILES):
                    ins = pe.transpose(psum[:, k % RING, t * width:(t + 1) * width], logits_t[:, t * P:(t + 1) * P],
                                       ident[0:width, 0:width])
            return ins

        def load_router(q, x):
            s = ml[x]
            q.dma_start(router_raw[:], d[MOE[x][4]].rearrange("(k p) e -> p k e", p=P)).then_inc(s.r_loaded, 16)
            if x == "L1_ffn":
                q.dma_start(router_b[:], d["L1_ffn_br"].rearrange("(o n) -> o n", o=1).to_broadcast([P, E])).then_inc(
                    s.r_loaded, 16)

        def load_biases(q):
            for l, x in enumerate(moe_layers):
                q.dma_start(split_f[0:64, l, 0, :], d[MOE[x][1]].rearrange("e (j n) -> (e j) n", n=P)).then_inc(b_loaded, 16)
                q.dma_start(split_f[64:80, l, 0, :], d[MOE[x][3]].rearrange("e (j n) -> (e j) n", n=P)).then_inc(b_loaded, 16)

        def split_biases(v):
            v.wait_ge(b_loaded, 32 * len(moe_layers))
            f_, b_, ls = split_f, split_b, slice(0, len(moe_layers))
            vstep(v, v.tensor_copy(b_[:, ls, 0, :], f_[:, ls, 0, :]))
            vstep(v, v.tensor_tensor(f_[:, ls, 1, :], f_[:, ls, 0, :], b_[:, ls, 0, :], ALU.subtract))
            vstep(v, v.tensor_copy(b_[:, ls, 1, :], f_[:, ls, 1, :]))
            vstep(v, v.tensor_tensor(f_[:, ls, 2, :], f_[:, ls, 1, :], b_[:, ls, 1, :], ALU.subtract))
            v.tensor_copy(b_[:, ls, 2, :], f_[:, ls, 2, :]).then_inc(b_split, 1)

        def place_biases(q):
            q.wait_ge(b_split, 1)
            for l in range(len(moe_layers)):
                for i in range(3):
                    q.dma_start(bias_scratch[l, i], split_b[:, l, i, :]).then_inc(b_placed, 16)
            q.wait_ge(b_placed, 48 * len(moe_layers))

        def load_up(q, x, e):
            q.dma_start(up_w[:, e], d[MOE[x][0]][e].rearrange("(k p) n -> p k n", p=P)).then_inc(ml[x].w_loaded, 16)

        def load_down(q, x, e):
            q.dma_start(down[x][:, e], d[MOE[x][2]][e].rearrange("(k p) n -> p k n", p=P)).then_inc(ml[x].w_loaded, 16)

        up_ahead = {"L1_ffn": min(E, (attention_at - shared_at) // (4 * UP)) if "L1_gnn" in stages else 0,
                    "L2_ffn": min(E, (k_at - shared_at) // (4 * UP)) if "L2_gnn" in stages else 0}

        def spread_biases(q, x):
            q.wait_ge(b_placed, 48 * len(moe_layers))
            s, scratch = ml[x], bias_scratch[moe_layers.index(x)]
            blocks = scratch[:, 0:E * 8, :].rearrange("i (e b) n -> i e b n", b=4)
            for b in range(4):
                q.dma_start(bias12[3 * b:3 * b + 3].rearrange("i e c n -> i (e c) n"), blocks[:, :, b, :]).then_inc(
                    s.b_spread, 16)
            q.dma_start(bias3[:].rearrange("i e (b n) -> i (e b) n", n=P), scratch[:, E * 8:E * 10, :]).then_inc(
                s.b_spread, 16)

        def store_rows(q, x, rows_base):
            q.wait_ge(rows_normed, rows_base + TILES)
            q.dma_start(x_rows.rearrange("(t p) n -> p t n", p=P), normed[:]).then_inc(ml[x].rows_stored, 16)

        def load_results(q, x):
            q.wait_ge(ml[x].y_stored[0], 16 * ((SLOTS + 1) // 2))
            q.wait_ge(ml[x].y_stored[1], 16 * (SLOTS // 2))
            for c, (t0, w_) in enumerate(GROUPS):
                for which in range(2):
                    base_ = which * NP
                    whole = w_ if t0 + w_ < TILES else w_ - 1
                    q.dma_start(gathered[:, t0:t0 + whole, which, :], y_rows[base_ + t0 * P:base_ + (t0 + whole) * P, :]
                                .rearrange("(t p) n -> p t n", p=P)).then_inc(y_loaded[c], 16)
                    if whole < w_:
                        q.dma_start(gathered[0:LAST, TILES - 1, which, :],
                                    y_rows[base_ + (TILES - 1) * P:base_ + N, :]).then_inc(y_loaded[c], 16)

        def moe_tensor(pe, x, rows_base):
            s = ml[x]
            turned, w = pairs(mturned_hi, mturned_lo), pairs(router_hi, router_lo)
            for k, it in enumerate(moe_items()):
                if it[0] == "weights":
                    continue
                ring_free(pe, s.item_done, k)
                if it[0] == "turn":
                    ins = turn_tensor(pe, it[1], k, rows_base)
                else:
                    ins = logits_tensor(pe, it, moe_items(), k, E, turned, w, logits_t, s.item_done)
                ins.then_inc(s.item_ready, 1)
            pe.wait_ge(s.chosen, 1)
            both = chosen_b
            flat = psum[:, 4, 0:TILES * E]
            pe.matmul(flat, before_b[:], both[:].rearrange("p t e -> p (t e)"), start=True, stop=False)
            for t in range(TILES - 1):
                rest = TILES - 1 - t
                pe.matmul(psum[:, 4, (t + 1) * E:TILES * E].rearrange("p (t e) -> p t e", e=E), ones_b[:],
                          both[:, t:t + 1, :].to_broadcast([P, rest, E]), start=False, stop=t == TILES - 2)
            for t in range(TILES):
                ins = pe.matmul(psum[:, 5, 0:E], ones_b[:], both[:, t, :], start=t == 0, stop=t == TILES - 1)
            ins.then_inc(s.counted, 1)

            for i in range(2 * TILES):
                pe.wait_ge(s.hot_ready, 1 + i // TILES)
                ins = pe.matmul(psum[:, 6, 0:2 * SLOTS], place_hot[:, i, :],
                                slot_vals[:, i, :, :].rearrange("p c k -> p (c k)"), start=i == 0, stop=i == 2 * TILES - 1)
            ins.then_inc(s.mapped, 1)

            HB = 8 if x == "L1_ffn" else 4
            pe.wait_ge(s.placed, 1)

            def expert(k):
                return bass.ds(pe.value_load(slot_expert[0:1, bass.ds(k, 1)], min_val=0, max_val=E - 1), 1)

            def one(ap):
                return ap.rearrange("p o n -> p (o n)")

            def turn_x(k, parity, half):
                pe.wait_ge(s.x_loaded[parity], (half + 1) * 16)
                for kb in range(KD):
                    ins = pe.transpose(psum[:, 6, kb * P:(kb + 1) * P], slot_x[:, parity, kb * P:(kb + 1) * P], ident[:])
                ins.then_inc(s.x_turned, 1)

            def up(k, parity, early=False):
                e = expert(k)
                pe.wait_ge(s.xt_ready, k + 1)
                pe.wait_ge(s.w_kept_s, k + 1)
                pe.wait_ge(s.w_kept_v, k + 1)
                if not early:
                    pe.wait_ge(s.h_lo, k - 1)
                    pe.wait_ge(s.h_kept_v, k - 1)
                for c in range(2):
                    pe.matmul(psum[:, 2 * parity + c, :], one(bias12[:, e, c, :]),
                              block_of[:].rearrange("p b n -> p (b n)"), start=True, stop=False)
                    for b in range(4):
                        o = psum[:, 2 * parity + c, b * P:(b + 1) * P]
                        at = (4 * c + b) * P
                        for kb in range(KD):
                            ins = pe.matmul(o, slot_w[parity][:, kb, at:at + P], slot_xt[:, parity, kb, :],
                                            start=False, stop=b == 3 and kb == KD - 1)
                    ins.then_inc(s.h_ready, 1)

            def down_(k, parity):
                e = expert(k)
                pe.wait_ge(s.h_lo, k + 1)
                pe.wait_ge(s.h_kept_v, k + 1)
                pe.wait_ge(s.down_lo_kept, k + 1)
                if not isinstance(k, int) or k > 0:
                    pe.wait_ge(s.y_kept, k)
                o = psum[:, 7, 0:D]
                pe.matmul(o, ones3[:], one(bias3[:, e, :]), start=True, stop=False)
                for b in range(4):
                    ins = product(pe, o, pairs(ht_hi, ht_lo)(slice(None), parity, slice(b * P, (b + 1) * P)),
                                  pairs(down_hi, down_lo)(slice(None), b, slice(None)), False, b == HB - 1)
                for b in range(4, HB):
                    ins = pe.matmul(o, ht_rest[:, parity, (b - 4) * P:(b - 3) * P], one(down[x][:, e, b, :]),
                                    start=False, stop=b == HB - 1)
                ins.then_inc(s.y_ready, 1)

            def step(k, parity, half, early=False, last=False):
                up(k, parity, early)
                if not last:
                    turn_x(k + 1, 1 - parity, half + parity)
                down_(k - 1, 1 - parity)

            pe.wait_ge(s.b_spread, 16 * 5)
            turn_x(0, 0, 0)
            up(0, 0, early=True)
            turn_x(1, 1, 0)
            step(1, 1, 0, early=True)
            step(2, 0, 1)
            with pe.Fori(0, (SLOTS - 5) // 2) as j:
                step(j * 2 + 3, 1, j + 1)
                step(j * 2 + 4, 0, j + 2)
            step(SLOTS - 2, 1, (SLOTS - 2) // 2)
            step(SLOTS - 1, 0, (SLOTS - 1) // 2, last=True)
            down_(SLOTS - 1, 0)

        def moe_scalar(a, x):
            s = ml[x]
            n_pe = 0
            for k, it in enumerate(moe_items()):
                if it[0] == "weights":
                    a.wait_ge(s.r_loaded, 32 if x == "L1_ffn" else 16)
                    a.copy(router_hi[:], router_raw[:]).then_inc(s.item_hi, 1)
                elif it[0] == "turn":
                    n_pe += 1
                    a.wait_ge(s.item_ready, n_pe)
                    src, cols = turn_source(it[1], k)
                    a.copy(mturned_hi[:, :, cols], src).then_inc(s.item_hi, 1)
                elif it[0] == "chunk":
                    n_pe += 1
                    a.wait_ge(s.item_ready, n_pe)
                    a_, cols = PCHUNKS[it[1]]
                    a.copy(logits_t[:, a_:a_ + cols], psum[0:E, k % RING, 0:cols]).then_inc(s.item_hi, 1)
            a.wait_ge(s.gap, 1)
            a.activation(best[:, :, 3], best[:, :, 2], ACT.Exp).then_inc(s.gap_exp, 1)

            def keep_xt(k, parity, early=False):
                a.wait_ge(s.x_turned, k + 1)
                if not early:
                    a.wait_ge(s.h_ready, k * 2 - 2)
                a.copy(slot_xt[:, parity, :, :], psum[:, 6, 0:D].rearrange("p (k n) -> p k n", k=KD)).then_inc(
                    s.xt_ready, 1)

            def keep_w(k, parity, early=False):
                e = bass.ds(a.value_load(slot_expert[0:1, bass.ds(k, 1)], min_val=0, max_val=E - 1), 1)
                if not early:
                    a.wait_ge(s.h_ready, k * 2 - 2)
                a.copy(slot_w[parity][:, 0, :], up_w[:, e, 0, :].rearrange("p o n -> p (o n)")).then_inc(s.w_kept_s, 1)

            def keep_down(k, early=False):
                e = bass.ds(a.value_load(slot_expert[0:1, bass.ds(k, 1)], min_val=0, max_val=E - 1), 1)
                if not early:
                    a.wait_ge(s.y_ready, k)
                a.copy(down_hi[:], down[x][:, e, 0:4, :].rearrange("p o b n -> p (o b) n")).then_inc(s.down_hi_kept, 1)

            def keep_h(k, parity, early=False):
                a.wait_ge(s.h_ready, k * 2 + 1)
                if x == "L1_ffn":
                    if not early:
                        a.wait_ge(s.y_ready, k - 1)
                    a.activation(ht_hi[:, parity, :], psum[:, 2 * parity, :], ACT.Relu).then_inc(s.h_hi, 1)
                else:
                    if not isinstance(k, int) or k > 0:
                        a.wait_ge(s.h_kept_v, k)
                    a.activation(slot_silu[:], psum[:, 2 * parity, :], ACT.Silu).then_inc(s.silu_kept, 1)

            def keep_hi(k, parity, early=False):
                if x == "L2_ffn":
                    a.wait_ge(s.h_kept_v, k + 1)
                    if not early:
                        a.wait_ge(s.y_ready, k - 1)
                    a.copy(ht_hi[:, parity, :], ht_rest[:, parity, :]).then_inc(s.h_hi, 1)

            def step(k, parity, early=False, last=False):
                keep_down(k - 1, early=isinstance(k, int) and k == 1)
                if not last:
                    keep_w(k + 1, 1 - parity)
                keep_h(k, parity, early)
                if not last:
                    keep_xt(k + 1, 1 - parity)
                keep_hi(k, parity, early)

            a.wait_ge(s.placed, 1)
            a.wait_ge(s.rows_stored, 16)
            a.wait_ge(s.w_loaded, 16 * 2 * E)
            keep_w(0, 0, early=True)
            keep_w(1, 1, early=True)
            keep_xt(0, 0, early=True)
            keep_h(0, 0, early=True)
            keep_xt(1, 1, early=True)
            keep_hi(0, 0, early=True)
            step(1, 1, early=True)
            step(2, 0)
            with a.Fori(0, (SLOTS - 5) // 2) as j:
                step(j * 2 + 3, 1)
                step(j * 2 + 4, 0)
            step(SLOTS - 2, 1)
            step(SLOTS - 1, 0, last=True)
            keep_down(SLOTS - 1)

        def moe_vector(v, x, inst):
            s = ml[x]
            if x == "L2_ffn":
                vstep(v, v.memset(router_b[:], 0.0))
            for k, it in enumerate(moe_items()):
                if it[0] == "logits":
                    continue
                v.wait_ge(s.item_hi, k + 1)
                if it[0] == "weights":
                    ins = v.tensor_tensor(router_lo[:], router_raw[:], router_hi[:].bitcast(F32), ALU.subtract)
                elif it[0] == "chunk":
                    ins = v.engine_nop()
                else:
                    src, cols = turn_source(it[1], k)
                    ins = v.tensor_tensor(mturned_lo[:, :, cols], src, mturned_hi[:, :, cols].bitcast(F32), ALU.subtract)
                ins.then_inc(s.item_done, 1)
            logits, eq, rest = router_sb

            def rows(ap, width=E):
                return ap.to_broadcast([P, TILES, width])

            v.wait_ge(s.item_ready, len(moe_items()) - 1)
            src = psum[:, (len(moe_items()) - 1) % RING, 0:TILES * E].rearrange("p (t e) -> p t e", e=E)
            ins = v.tensor_tensor(logits[:], src, router_b[:].rearrange("p (o e) -> p o e", o=1)
                                  .to_broadcast([P, TILES, E]), ALU.add)
            ins.then_inc(s.logits, 1)
            v.wait_ge(s.logits, 1)
            for which, (frm, hot) in enumerate(((logits, first), (rest, second))):
                vstep(v, v.tensor_reduce(best[:, :, which], frm[:], AX.X, ALU.max))
                vstep(v, v.tensor_tensor(eq[:], frm[:], rows(best[:, :, which:which + 1]), ALU.is_equal))
                vstep(v, v.tensor_tensor(eq[:], eq[:], rank_down[:], ALU.mult))
                vstep(v, v.tensor_reduce(best[:, :, 2], eq[:], AX.X, ALU.max))
                vstep(v, v.tensor_tensor(hot[:], eq[:], rows(best[:, :, 2:3]), ALU.is_equal))
                if which == 0:
                    vstep(v, v.scalar_tensor_tensor(rest[:], first[:], LOWEST, logits[:], ALU.mult, ALU.add))
            vstep(v, v.tensor_tensor(logits[:], first[:], second[:], ALU.add))
            v.tensor_tensor(chosen_b[:], logits[:], rows(valid[:].rearrange("p (t o) -> p t o", o=1)),
                            ALU.mult).then_inc(s.chosen, 1)
            v.tensor_tensor(best[:, :, 2:3], best[:, :, 1:2], best[:, :, 0:1], ALU.subtract).then_inc(s.gap, 1)
            v.wait_ge(s.gap_exp, 1)
            vstep(v, v.tensor_scalar(gate[:, :, 1:2], best[:, :, 3:4], 1.0, None, ALU.add))
            vstep(v, v.reciprocal(gate[:, :, 0:1], gate[:, :, 1:2]))
            v.tensor_tensor(gate[:, :, 1:2], best[:, :, 3:4], gate[:, :, 0:1], ALU.mult)
            v.wait_ge(s.counted, 1)
            vstep(v, v.tensor_copy(per_expert[:, 0, :], psum[:, 5, 0:E]))
            vstep(v, v.tensor_tensor(step_gt[:], per_expert[:, 0, :].rearrange("p (e o) -> p e o", o=1)
                                     .to_broadcast([P, E, TILES]), steps128[:], ALU.is_gt))
            vstep(v, v.tensor_reduce(per_expert[:, 1, :], step_gt[:], AX.X, ALU.add))
            vstep(v, v.tensor_tensor(lt_prod[:], expert_lt[:], per_expert[:, 1:2, :].to_broadcast([P, E, E]), ALU.mult))
            vstep(v, v.tensor_reduce(per_expert[:, 2, :], lt_prod[:], AX.X, ALU.add))
            vstep(v, v.tensor_tensor(per_expert[:, 3, :], per_expert[:, 2, :], per_expert[:, 1, :], ALU.add))
            vstep(v, v.tensor_tensor(slot_ge[:], slot_iota[:], per_expert[:, 3:4, :].to_broadcast([P, SLOTS, E]),
                                     ALU.is_ge))
            vstep(v, v.tensor_reduce(slot_f[:], slot_ge[:], AX.X, ALU.add))
            vstep(v, v.tensor_scalar(slot_expert[:], slot_f[:], E - 1.0, None, ALU.min))
            vstep(v, v.scalar_tensor_tensor(rest[:], per_expert[:, 2:3, :].to_broadcast([P, TILES, E]), float(P),
                                            psum[:, 4, 0:TILES * E].rearrange("p (t e) -> p t e", e=E),
                                            ALU.mult, ALU.add))
            for which, hot in enumerate((first, second)):
                vstep(v, v.tensor_tensor(eq[:], rest[:], hot[:], ALU.mult))
                vstep(v, v.tensor_reduce(pos[:, which, :], eq[:], AX.X, ALU.add))
            slot_, in_slot = split_pos[:, 0], split_pos[:, 1]
            vstep(v, v.tensor_scalar(slot_, pos[:], 1.0 / P, 0.5 / P - 0.5, ALU.mult, ALU.add))
            vstep(v, v.tensor_scalar(slot_, slot_, ROUND, ROUND, ALU.add, ALU.subtract))
            vstep(v, v.scalar_tensor_tensor(in_slot, slot_, -float(P), pos[:], ALU.mult, ALU.add))

            def each(ap, width):
                return ap.rearrange("p w (t o) -> p (w t) o", o=1).to_broadcast([P, 2 * TILES, width])

            def const(ap, width):
                return ap[:].rearrange("p (o j) -> p o j", o=1).to_broadcast([P, 2 * TILES, width])

            vstep(v, v.tensor_copy(split_pos_b[:], split_pos[:]))
            vstep(v, v.tensor_tensor(slot_hot[:], const(place_slot, SLOTS), each(split_pos_b[:, 0], SLOTS), ALU.is_equal))
            for c in range(2):
                v.tensor_tensor(slot_vals[:, :, c, :], slot_hot[:], each(tile_p[:, c], SLOTS), ALU.mult)
            for c in range(2):
                half = slice(c * TILES, (c + 1) * TILES)
                v.tensor_tensor(place_hot[:, half, :], const(place_row, P)[:, half, :], each(split_pos_b[:, 1], P)[:, half, :],
                                ALU.is_equal).then_inc(s.hot_ready, 1)
            v.wait_ge(s.mapped, 1)
            vstep(v, v.tensor_copy(mapped[:], psum[:, 6, 0:2 * SLOTS].rearrange("p (c k) -> p c k", c=2)))
            v.scalar_tensor_tensor(map_base[:], mapped[:, 0, :], float(P), mapped[:, 1, :], ALU.mult, ALU.add)
            v.scalar_tensor_tensor(spare_f[:], mapped[:, 0, :], 0.0, spare_row[:], ALU.is_equal, ALU.mult)
            vstep(v, v.tensor_scalar(source_f[:], mapped[:, 0, :], TILES + 0.5, -float(NP), ALU.is_gt, ALU.mult))
            vstep(v, v.tensor_tensor(source_f[:], source_f[:], map_base[:], ALU.add))
            v.tensor_scalar(source_row[:], source_f[:], -float(P), 0.0, ALU.add, ALU.max).then_inc(s.sources_ready, 1)
            vstep(v, v.tensor_tensor(target_f[:], spare_f[:], map_base[:], ALU.add))
            v.tensor_scalar(target_row[:], target_f[:], -float(P), None, ALU.add).then_inc(s.placed, 1)

            def keep_w(k, parity, early=False):
                e = bass.ds(v.value_load(slot_expert[0:1, bass.ds(k, 1)], min_val=0, max_val=E - 1), 1)
                if not early:
                    v.wait_ge(s.h_ready, k * 2 - 2)
                v.tensor_copy(slot_w[parity][:, 1, :], up_w[:, e, 1, :].rearrange("p o n -> p (o n)")).then_inc(
                    s.w_kept_v, 1)

            def keep_down(k):
                e = bass.ds(v.value_load(slot_expert[0:1, bass.ds(k, 1)], min_val=0, max_val=E - 1), 1)
                v.wait_ge(s.down_hi_kept, k + 1)
                v.tensor_tensor(down_lo[:], down[x][:, e, 0:4, :].rearrange("p o b n -> p (o b) n"),
                                down_hi[:].bitcast(F32), ALU.subtract).then_inc(s.down_lo_kept, 1)

            def keep_h(k, parity, early=False):
                if x == "L1_ffn":
                    v.wait_ge(s.h_hi, k + 1)
                    v.scalar_tensor_tensor(ht_lo[:, parity, :], psum[:, 2 * parity, :], 0.0,
                                           ht_hi[:, parity, :].bitcast(F32), ALU.max, ALU.subtract).then_inc(s.h_lo, 1)
                v.wait_ge(s.h_ready, k * 2 + 2)
                if not early:
                    v.wait_ge(s.y_ready, k - 1)
                bank = psum[:, 2 * parity + 1, :]
                if x == "L1_ffn":
                    v.tensor_scalar(ht_rest[:, parity, :], bank, 0.0, None, ALU.max).then_inc(s.h_kept_v, 1)
                else:
                    v.wait_ge(s.silu_kept, k + 1)
                    v.tensor_tensor(ht_rest[:, parity, :], bank, slot_silu[:], ALU.mult).then_inc(s.h_kept_v, 1)
                    v.wait_ge(s.h_hi, k + 1)
                    v.tensor_tensor(ht_lo[:, parity, :], ht_rest[:, parity, :], ht_hi[:, parity, :].bitcast(F32),
                                    ALU.subtract).then_inc(s.h_lo, 1)

            def keep_y(k, parity, half):
                v.wait_ge(s.y_ready, k + 1)
                if not isinstance(k, int) or k > 1:
                    v.wait_ge(s.y_stored[parity], half * 16)
                v.tensor_copy(slot_y[:, parity, :], psum[:, 7, 0:D]).then_inc(s.y_kept, 1)

            def step(k, parity, half, early=False, last=False):
                keep_down(k - 1)
                if not last:
                    keep_w(k + 1, 1 - parity)
                keep_h(k, parity, early)
                keep_y(k - 1, 1 - parity, half)

            v.wait_ge(s.placed, 1)
            v.wait_ge(s.rows_stored, 16)
            v.wait_ge(s.w_loaded, 16 * 2 * E)
            keep_w(0, 0, early=True)
            keep_w(1, 1, early=True)
            keep_h(0, 0, early=True)
            step(1, 1, 0, early=True)
            step(2, 0, 0)
            with v.Fori(0, (SLOTS - 5) // 2) as j:
                step(j * 2 + 3, 1, j + 1)
                step(j * 2 + 4, 0, j + 1)
            step(SLOTS - 2, 1, (SLOTS - 3) // 2)
            step(SLOTS - 1, 0, (SLOTS - 3) // 2, last=True)
            keep_down(SLOTS - 1)
            keep_y(SLOTS - 1, 0, (SLOTS - 1) // 2)
            for c, (t0, w_) in enumerate(GROUPS):
                v.wait_ge(y_loaded[c], y_loads[c] * (inst + 1))
                for which in range(2):
                    for t in range(t0, t0 + w_):
                        r_ = LAST if t == TILES - 1 else P
                        ins = v.scalar_tensor_tensor(resid[0:r_, t, :], gathered[0:r_, t, which, :],
                                                     gate[0:r_, t, which:which + 1], resid[0:r_, t, :],
                                                     ALU.mult, ALU.add)
                    vstep(v, ins)
                for t in range(t0, t0 + w_):
                    row_stats(v, t)

        def moe_pool(p, x):
            s = ml[x]

            def load(k, parity):
                p.indirect_dma_start(slot_x[:, parity, :], None, x_rows,
                                     bass.IndirectOffsetOnAxis(source_row[:, k:k + 1], 0)).then_inc(s.x_loaded[parity], 16)

            def store(k, parity):
                p.indirect_dma_start(y_rows, bass.IndirectOffsetOnAxis(target_row[:, k:k + 1], 0),
                                     slot_y[:, parity, :], None).then_inc(s.y_stored[parity], 16)

            pstep(p, p.memset(block_of_f[:], 1.0))
            pstep(p, p.affine_select(out=block_of_f[:], in_=block_of_f[:], compare_op=ALU.is_ge, fill=0.0, base=0,
                                     pattern=[[-3, 4], [0, P]], channel_multiplier=1))
            pstep(p, p.affine_select(out=block_of_f[:], in_=block_of_f[:], compare_op=ALU.is_ge, fill=0.0, base=2,
                                     pattern=[[3, 4], [0, P]], channel_multiplier=-1))
            pstep(p, p.tensor_copy(block_of[:], block_of_f[:]))
            p.wait_ge(s.rows_stored, 16)
            p.wait_ge(s.sources_ready, 1)
            load(0, 0)
            load(1, 1)
            p.wait_ge(s.placed, 1)
            for k in range(SLOTS):
                if k == 0:
                    p.wait_ge(s.x_turned, 1)
                    load(2, 0)
                if k + 3 < SLOTS:
                    p.wait_ge(s.x_turned, k + 2)
                    load(k + 3, (k + 3) % 2)
                p.wait_ge(s.y_kept, k + 1)
                store(k, k % 2)

        def f_items():
            return ([("in", wh, kb, half) for wh in range(2) for kb in range(KD) for half in range(2)] +
                    [("out", e, kp) for e in range(E + 1) for kp in range(2)] + [("gates",)] +
                    logit_items())

        def load_f(q):
            def every(b, width):
                return b.rearrange("(o n) -> o n", o=1).to_broadcast([P, width])

            for dst, src in ((gate_nat[0:2, :], d["L3_ffn_group_gate_w"]), (gate_nat[2:E + 2, :], d["L3_ffn_expert_gate_w"]),
                             (gate_b[:, 0:2], every(d["L3_ffn_group_bias"], 2)),
                             (gate_b[:, 2:E + 2], every(d["L3_ffn_expert_bias"], E)),
                             (ln_rows[:, 0, :], every(d["L3_ffn_ln_scale"], D)),
                             (ln_rows[:, 1, :], every(d["L3_ffn_ln_bias"], D)),
                             (bias9[0:E, :], d["L3_ffn_expert_out_bias"]),
                             (bias9[E:E + 1, :], d["L3_ffn_shared_out_b"].rearrange("(o n) -> o n", o=1))):
                q.dma_start(dst, src).then_inc(fs.loaded, 16)

        def load_f_in(q, wh):
            src = d[("L3_ffn_shared_in_w", "L3_ffn_expert_in_w")[wh]]
            q.dma_start(nat_in[:, wh], src.rearrange("(b p) n -> p b n", p=P)).then_inc(fs.in_loaded[wh], 16)

        def load_f_out(q, e):
            src = d["L3_ffn_expert_out_weight"][e] if e < E else d["L3_ffn_shared_out_w"]
            q.dma_start(nat_out[:, e], src.rearrange("(b p) n -> p b n", p=P)).then_inc(fs.out_loaded, 16)

        def f_source(it, k):
            bank = psum[:, k % RING, :]
            if it[0] == "gates":
                return bank[:, 0:KD * (E + 2)].rearrange("p (k n) -> p k n", k=KD), gate_hi[:], gate_lo[:]
            if it[0] == "in":
                _, wh, kb, half = it
                cols = slice(half * BANK, (half + 1) * BANK)
                return bank, in_hi[:, wh, kb, cols], in_lo[:, wh, kb, cols]
            if it[0] == "out":
                _, e, kp = it
                ix = (slice(None), slice(2 * kp, 2 * kp + 2), slice(e * D, (e + 1) * D))
                return bank.rearrange("p (k n) -> p k n", k=2), out_hi[ix], out_lo[ix]
            src, cols = turn_source(it[1], k)
            return src, f_turned_hi[:, :, cols], f_turned_lo[:, :, cols]

        def f_tensor(pe, rows_base):
            s = fs
            for k, it in enumerate(f_items()):
                ring_free(pe, s.item_done, k)
                if it[0] == "gates":
                    pe.wait_ge(s.loaded, 16 * 8)
                    for kb in range(KD):
                        ins = pe.transpose(psum[:, k % RING, kb * (E + 2):(kb + 1) * (E + 2)],
                                           gate_nat[:, kb * P:(kb + 1) * P], ident[0:E + 2, 0:E + 2])
                elif it[0] == "in":
                    _, wh, kb, half = it
                    pe.wait_ge(s.in_loaded[wh], 16)
                    for j in range(4):
                        ins = pe.transpose(psum[:, k % RING, j * P:(j + 1) * P],
                                           nat_in[:, wh, 4 * half + j, kb * P:(kb + 1) * P], ident[:])
                elif it[0] == "out":
                    _, e, kp = it
                    pe.wait_ge(s.out_loaded, 16 * (E + 1))
                    for j in range(2):
                        for nb in range(2):
                            at = (2 * kp + j) * P
                            ins = pe.transpose(psum[:, k % RING, j * D + nb * P:j * D + (nb + 1) * P],
                                               nat_out[:, e, nb, at:at + P], ident[:])
                elif it[0] == "turn":
                    ins = turn_tensor(pe, it[1], k, rows_base)
                else:
                    ins = logits_tensor(pe, it, f_items(), k, E + 2, pairs(f_turned_hi, f_turned_lo),
                                        pairs(gate_hi, gate_lo), f_logits_t, s.item_done)
                ins.then_inc(s.item_ready, 1)
            pe.wait_ge(s.item_done, len(f_items()))

            def hidden_(t, wh):
                k = 2 * t + wh
                if t >= 1:
                    pe.wait_ge(s.h_kept, k - 1)
                for half in range(2):
                    for kb in range(KD):
                        ins = product(pe, psum[:, 2 * wh + half, :],
                                      pairs(f_turned_hi, f_turned_lo)(slice(None), kb, slice(t * P, (t + 1) * P)),
                                      pairs(in_hi, in_lo)(slice(None), wh, kb, slice(half * BANK, (half + 1) * BANK)),
                                      kb == 0, kb == KD - 1)
                ins.then_inc(s.h_ready, 1)

            def turn(t, wh):
                k = 2 * t + wh
                pe.wait_ge(s.h_kept, k + 1)
                if k >= 1:
                    pe.wait_ge(s.ht_done, k)
                for j in range(4):
                    ins = pe.transpose(psum[:, 4, j * P:(j + 1) * P], act_h[:, wh, j * P:(j + 1) * P], ident[:])
                ins.then_inc(s.h_turned, 1)

            def outputs(t):
                k = 5 * t
                pe.wait_ge(s.ht_done, 2 * t + 1)
                if t >= 1:
                    pe.wait_ge(s.y_used, k - 4)
                if t == 0:
                    pe.wait_ge(s.cnt_kept, NG)
                pe.matmul(psum[:, 5, 0:D], cnt_t[:, t, :], bias9[:], start=True, stop=False)
                for kq in range(4):
                    ins = product(pe, psum[:, 5, 0:D], pairs(act_t_hi, act_t_lo)(slice(None), 0, slice(kq * P, (kq + 1) * P)),
                                  pairs(out_hi, out_lo)(slice(None), kq, slice(E * D, (E + 1) * D)), False, kq == 3)
                ins.then_inc(s.y_ready, 1)
                pe.wait_ge(s.ht_done, 2 * t + 2)
                for q in range(4):
                    n_ = k + 1 + q
                    if q >= 2:
                        pe.wait_ge(s.y_used, n_ - 1)
                    elif t >= 1:
                        pe.wait_ge(s.y_used, n_ - 2)
                    for kq in range(4):
                        ins = product(pe, psum[:, 6 + q % 2, :],
                                      pairs(act_t_hi, act_t_lo)(slice(None), 1, slice(kq * P, (kq + 1) * P)),
                                      pairs(out_hi, out_lo)(slice(None), kq, slice(q * BANK, (q + 1) * BANK)),
                                      kq == 0, kq == 3)
                    ins.then_inc(s.y_ready, 1)

            hidden_(0, 0)
            hidden_(0, 1)
            for t in range(TILES):
                turn(t, 0)
                if t + 1 < TILES:
                    hidden_(t + 1, 0)
                turn(t, 1)
                if t + 1 < TILES:
                    hidden_(t + 1, 1)
                if t == 0:
                    pe.wait_ge(s.cnt_ready, 1)
                    for c, (t0, w_) in enumerate(GROUPS):
                        for j in range(w_):
                            ins = pe.transpose(psum[0:E + 1, 5 + c, j * P:(j + 1) * P], cnt[:, t0 + j, :], ident[:])
                        ins.then_inc(s.cnt_turned, 1)
                outputs(t)

        def f_scalar(a):
            s = fs
            norm_scalar(a, norm_index["L3_ffn"] + 1)
            for k, it in enumerate(f_items()[:-1]):
                a.wait_ge(s.item_ready, k + 1)
                if it[0] == "chunk":
                    a_, cols = PCHUNKS[it[1]]
                    a.copy(f_logits_t[:, a_:a_ + cols], psum[0:E + 2, k % RING, 0:cols]).then_inc(s.item_hi, 1)
                else:
                    src, hi_, _ = f_source(it, k)
                    a.copy(hi_, src).then_inc(s.item_hi, 1)
            a.wait_ge(s.exp_in, 1)
            a.activation(esel[:, 1], esel[:, 0], ACT.Exp).then_inc(s.exp_out, 1)

            def silu(t, wh):
                a.wait_ge(s.h_ready, 2 * t + wh + 1)
                if t >= 1:
                    a.wait_ge(s.h_kept, 2 * t + wh - 1)
                a.activation(act_silu[:, wh, :], psum[:, 2 * wh, :], ACT.Silu).then_inc(s.silu, 1)

            def hi(t, wh):
                a.wait_ge(s.h_turned, 2 * t + wh + 1)
                if t >= 1:
                    a.wait_ge(s.y_ready, 5 * t - 4 if wh == 0 else 5 * t)
                a.copy(act_t_hi[:, wh, :], psum[:, 4, :]).then_inc(s.ht_hi, 1)

            silu(0, 0)
            silu(0, 1)
            for t in range(TILES):
                hi(t, 0)
                if t + 1 < TILES:
                    silu(t + 1, 0)
                hi(t, 1)
                if t + 1 < TILES:
                    silu(t + 1, 1)
                if t == 0:
                    for c, (t0, w_) in enumerate(GROUPS):
                        a.wait_ge(s.cnt_turned, c + 1)
                        a.copy(cnt_t[:, t0:t0 + w_, :],
                               psum[0:E + 1, 5 + c, 0:w_ * P].rearrange("p (t n) -> p t n", n=P)).then_inc(s.cnt_kept, 1)

        def f_norm(v, rows_base, index):
            v.wait_ge(rows_normed, rows_base + TILES)
            for t in range(TILES):
                ins = v.bn_stats(stats[:, t, :], normed[:, t, :])
            vstep(v, ins)
            for t in range(TILES):
                ins = v.bn_aggr(mean_var[:, t, :], stats[:, t, :])
            vstep(v, ins)
            v.tensor_scalar(var_eps[:], mean_var[:, :, 1], EPS, None, ALU.add).then_inc(var_ready, 1)
            v.wait_ge(std_ready, index + 1)
            vstep(v, v.reciprocal(rstd[:], std[:]))
            for t in range(TILES):
                v.tensor_scalar(normed[:, t, :], normed[:, t, :], mean_var[:, t, 0:1], rstd[:, t:t + 1],
                                ALU.subtract, ALU.mult).then_inc(fs.rows_ready, 1)

        def f_scale(p):
            p.wait_ge(fs.loaded, 16 * 8)
            for t in range(TILES):
                p.wait_ge(fs.rows_ready, t + 1)
                pstep(p, p.tensor_tensor(normed[:, t, :], normed[:, t, :], ln_rows[:, 0, :], ALU.mult))
                p.tensor_tensor(normed[:, t, :], normed[:, t, :], ln_rows[:, 1, :], ALU.add).then_inc(rows_normed, 1)

        probs4, hot1, rest4, hot2 = esel[:, 2], esel[:, 3], esel[:, 4], esel[:, 5]

        def four(ap):
            return ap.to_broadcast([P, TILES, 4])

        def col_(i):
            return psel[:, i:i + 1, :].rearrange("p o t -> p t o")

        def f_group(v):
            s = fs
            vstep(v, v.tensor_tensor(grp[:, :, 1:2], glog[:, :, 1:2], glog[:, :, 0:1], ALU.is_gt))
            vstep(v, v.tensor_scalar(grp[:, :, 0:1], grp[:, :, 1:2], -1.0, 1.0, ALU.mult, ALU.add))
            v.tensor_tensor(esel[:, 1], glog[:, :, 2:6], four(grp[:, :, 0:1]), ALU.mult)
            vstep(v, v.tensor_tensor(esel[:, 2], glog[:, :, 6:10], four(grp[:, :, 1:2]), ALU.mult))
            vstep(v, v.tensor_tensor(esel[:, 0], esel[:, 1], esel[:, 2], ALU.add))
            vstep(v, v.tensor_reduce(psel[:, 0, :], esel[:, 0], AX.X, ALU.max))
            v.tensor_tensor(esel[:, 0], esel[:, 0], four(col_(0)), ALU.subtract).then_inc(s.exp_in, 1)
            v.wait_ge(s.exp_out, 1)
            vstep(v, v.tensor_reduce(psel[:, 1, :], esel[:, 1], AX.X, ALU.add))
            vstep(v, v.reciprocal(psel[:, 1, :], psel[:, 1, :]))
            vstep(v, v.tensor_tensor(probs4, esel[:, 1], four(col_(1)), ALU.mult))

        def f_choose(v, which):
            frm, hot = ((probs4, hot1), (rest4, hot2))[which]
            vstep(v, v.tensor_reduce(psel[:, which, :], frm, AX.X, ALU.max))
            vstep(v, v.tensor_tensor(pk[:], frm, four(col_(which)), ALU.is_equal))
            vstep(v, v.tensor_tensor(pk[:], pk[:], rank_down[:, :, 4:8], ALU.mult))
            vstep(v, v.tensor_reduce(psel[:, 2, :], pk[:], AX.X, ALU.max))
            vstep(v, v.tensor_tensor(hot, pk[:], four(col_(2)), ALU.is_equal))
            if which == 0:
                vstep(v, v.scalar_tensor_tensor(rest4, hot1, -8.0, probs4, ALU.mult, ALU.add))

        def f_weights(v):
            s = fs
            vstep(v, v.tensor_tensor(psel[:, 3, :], psel[:, 0, :], psel[:, 1, :], ALU.add))
            vstep(v, v.tensor_scalar(psel[:, 3, :], psel[:, 3, :], 1e-8, None, ALU.add))
            vstep(v, v.reciprocal(psel[:, 3, :], psel[:, 3, :]))
            vstep(v, v.tensor_tensor(esel[:, 0], hot1, hot2, ALU.add))
            vstep(v, v.tensor_tensor(esel[:, 1], esel[:, 0], probs4, ALU.mult))
            vstep(v, v.tensor_tensor(esel[:, 1], esel[:, 1], four(col_(3)), ALU.mult))
            for gi in range(2):
                v.tensor_tensor(comb[:, :, 4 * gi:4 * gi + 4], esel[:, 1], four(grp[:, :, gi:gi + 1]), ALU.mult)
                v.tensor_tensor(cnt[:, :, 4 * gi:4 * gi + 4], esel[:, 0], four(grp[:, :, gi:gi + 1]), ALU.mult)
            vstep(v, v.memset(cnt[:, :, E:E + 1], 1.0))
            v.engine_nop().then_inc(s.cnt_ready, 1)

        def f_vector(v):
            s = fs
            f_norm(v, rows_at["L3_ffn"], norm_index["L3_ffn"] + 1)
            for k, it in enumerate(f_items()[:-1]):
                v.wait_ge(s.item_hi, k + 1)
                if it[0] == "chunk":
                    v.engine_nop().then_inc(s.item_done, 1)
                else:
                    src, hi_, lo_ = f_source(it, k)
                    v.tensor_tensor(lo_, src, hi_.bitcast(F32), ALU.subtract).then_inc(s.item_done, 1)
            v.wait_ge(s.item_ready, len(f_items()))
            bank = psum[:, (len(f_items()) - 1) % RING, 0:TILES * (E + 2)].rearrange("p (t e) -> p t e", t=TILES)
            ins = v.tensor_tensor(glog[:], bank, gate_b[:].rearrange("p (o e) -> p o e", o=1)
                                  .to_broadcast([P, TILES, E + 2]), ALU.add)
            ins.then_inc(s.item_done, 1)
            v.wait_ge(s.item_done, len(f_items()))
            f_group(v)
            f_choose(v, 0)

            def gated(t, wh):
                k = 2 * t + wh
                v.wait_ge(s.silu, k + 1)
                if t >= 1:
                    v.wait_ge(s.h_turned, k - 1)
                v.tensor_tensor(act_h[:, wh, :], psum[:, 2 * wh + 1, :], act_silu[:, wh, :], ALU.mult).then_inc(s.h_kept, 1)

            def lo(t, wh):
                v.wait_ge(s.ht_hi, 2 * t + wh + 1)
                v.tensor_tensor(act_t_lo[:, wh, :], psum[:, 4, :], act_t_hi[:, wh, :].bitcast(F32),
                                ALU.subtract).then_inc(s.ht_done, 1)

            gated(0, 0)
            f_choose(v, 1)
            gated(0, 1)
            for t in range(TILES):
                lo(t, 0)
                if t + 1 < TILES:
                    gated(t + 1, 0)
                lo(t, 1)
                if t + 1 < TILES:
                    gated(t + 1, 1)
                if t == 0:
                    f_weights(v)
                v.wait_ge(s.y_ready, 5 * t + 1)
                ins = v.tensor_tensor(resid[:, t, :], psum[:, 5, 0:D], resid[:, t, :], ALU.add)
                ins.then_inc(s.y_used, 1)
                v.wait_ge(s.y_used, 5 * t + 1)
                for q in range(4):
                    v.wait_ge(s.y_ready, 5 * t + 2 + q)
                    for j in range(2):
                        ins = v.scalar_tensor_tensor(resid[:, t, :], psum[:, 6 + q % 2, j * D:(j + 1) * D],
                                                     comb[:, t, 2 * q + j:2 * q + j + 1], resid[:, t, :],
                                                     ALU.mult, ALU.add)
                        if j == 0:
                            vstep(v, ins)
                    ins.then_inc(s.y_used, 1)
                    v.wait_ge(s.y_used, 5 * t + 2 + q)

        numbers = {}
        rows_at = {}
        count = 1
        rows = 0
        for st in stages:
            if st == "L3_gnn":
                numbers["L3a"], numbers["L3b"] = count, count + 1
                rows_at["L3a"], rows_at["L3b"] = rows, rows + TILES
                rows += 3 * TILES
                count += 2
            else:
                numbers[st] = count
                rows_at[st] = rows
                rows += TILES * (2 if st == "L3_ffn" else 1)
                count += 1
        counts["rows_end_L3b"] = rows_at.get("L3b", 0) + 2 * TILES
        order = [x for st in stages for x in (("L3a", "L3b") if st == "L3_gnn" else (st,))]
        norm_index = {}
        for x in order:
            if x != "L3b":
                norm_index[x] = len(norm_index)

        def loads_ahead(q, x):
            if x == "L1_gnn" and "L1_ffn" in stages:
                return [lambda e=e: load_up(q, "L1_ffn", e) for e in range(up_ahead["L1_ffn"])]
            if x == "L2_gnn" and "L2_ffn" in stages:
                return [lambda e=e: load_up(q, "L2_ffn", e) for e in range(up_ahead["L2_ffn"])]
            if x == "L3b" and "L3_ffn" in stages:
                return ([lambda wh=wh: load_f_in(q, wh) for wh in range(2)] +
                        [lambda e=e: load_f_out(q, e) for e in range(E + 1)])
            return []

        @block.sync
        def _(sp):
            for c, (t0, w_) in enumerate(GROUPS):
                w_ = min(w_, TILES - 1 - t0)
                sp.dma_start(resid[:, t0:t0 + w_, :],
                             d["x"][t0 * P:(t0 + w_) * P, :].rearrange("(t p) n -> p t n", p=P)).then_inc(x_loaded[c], 16)
            if moe_layers:
                load_biases(sp)
            sp.wait_ge(padding_zeroed, 1)
            sp.dma_start(resid[0:LAST, TILES - 1, :], d["x"][(TILES - 1) * P:N, :]).then_inc(x_loaded[NG - 1], 16)
            for x in order:
                if numbers[x] > 1:
                    sp.wait_ge(stage_done, 4 * (numbers[x] - 1))
                if x in gb:
                    load_weights(sp, x)
                    load_adjacency(sp, x, loads_ahead(sp, x))
                    if x == "L0_gnn" and "L0_ffn" in numbers:
                        load_nibble_weights(sp)
                elif x == "L0_ffn" and numbers[x] == 1:
                    load_nibble_weights(sp)
                elif x in ml:
                    load_router(sp, x)
                    spread_biases(sp, x)
                    store_rows(sp, x, rows_at[x])
                    for e in range(up_ahead[x], E):
                        load_up(sp, x, e)
                    for e in range(E):
                        load_down(sp, x, e)
                    load_results(sp, x)
                elif x == "L3_ffn":
                    load_f(sp)
                    if "L3_gnn" not in stages:
                        for wh in range(2):
                            load_f_in(sp, wh)
                        for e in range(E + 1):
                            load_f_out(sp, e)
            sp.wait_ge(stage_done, 4 * (count - 1))
            sp.dma_start(out[0:(TILES - 1) * P, :].rearrange("(t p) n -> p t n", p=P),
                         resid[:, 0:TILES - 1, :]).then_inc(out_stored, 16)
            sp.dma_start(out[(TILES - 1) * P:N, :], resid[0:LAST, TILES - 1, :]).then_inc(out_stored, 16)
            sp.wait_ge(out_stored, 32)

        @block.gpsimd
        def _(p):
            p.memset(resid[:, TILES - 1, :], 0.0).then_inc(padding_zeroed, 1)
            p.memset(ident[:], 0.0)
            p.memset(valid[:], 1.0)
            p.memset(ones3[:], 1.0)
            p.memset(ones_b[:], 1.0)
            p.memset(before[:], 1.0)
            pstep(p, p.memset(ones[:], 1.0))
            p.affine_select(out=ident[:], in_=ident[:], compare_op=ALU.not_equal, fill=1.0, base=0,
                            pattern=[[-1, P]], channel_multiplier=1)
            p.affine_select(out=before[:], in_=before[:], compare_op=ALU.is_gt, fill=0.0, base=0,
                            pattern=[[1, P]], channel_multiplier=-1)
            pstep(p, p.affine_select(out=valid[:], in_=valid[:], compare_op=ALU.is_gt, fill=0.0, base=N,
                                     pattern=[[-P, TILES]], channel_multiplier=-1))
            p.tensor_copy(before_b[:], before[:])
            p.memset(nib_w[:], 0.0).then_inc(ns.w_zeroed, 1)
            for choice in range(2):
                p.iota(tile_p[:, 0, choice, :], pattern=[[1, TILES]], base=1 + choice * TILES, channel_multiplier=0,
                       allow_small_or_imprecise_dtypes=True)
                pstep(p, p.iota(tile_p[:, 1, choice, :], pattern=[[0, TILES]], base=0, channel_multiplier=1,
                                allow_small_or_imprecise_dtypes=True))
                for c in range(2):
                    p.tensor_tensor(tile_p[:, c, choice, :], tile_p[:, c, choice, :], valid[:], ALU.mult)
            p.iota(place_row[:], pattern=[[1, P]], base=0, channel_multiplier=0, allow_small_or_imprecise_dtypes=True)
            p.iota(place_slot[:], pattern=[[1, SLOTS]], base=0, channel_multiplier=0, allow_small_or_imprecise_dtypes=True)
            p.iota(spare_row[:], pattern=[[P, SLOTS]], base=2 * NP + P, channel_multiplier=1,
                   allow_small_or_imprecise_dtypes=True)
            for dst, pattern, start in ((rank_down[:], [[0, TILES], [-1, E]], E), (steps128[:], [[0, E], [P, TILES]], 0),
                                        (slot_iota[:], [[1, SLOTS], [0, E]], 0)):
                p.iota(dst, pattern=pattern, base=start, channel_multiplier=0, allow_small_or_imprecise_dtypes=True)
            pstep(p, p.memset(expert_lt[:], 1.0))
            p.affine_select(out=expert_lt[:], in_=expert_lt[:], compare_op=ALU.is_gt, fill=0.0, base=0,
                            pattern=[[1, E], [-1, E]], channel_multiplier=0)
            p.tensor_scalar(invalid_bias[:], valid[:], -1.0, 1e30, ALU.add, ALU.mult).then_inc(consts_ready, 1)
            for x in order:
                if x in gb:
                    graph_pool(p, x)
                if x == order[0] and moe_layers:
                    place_biases(p)
                if x == "L0_ffn":
                    nibble_pool(p, rows_at[x])
                elif x in ml:
                    moe_pool(p, x)
                elif x == "L3_ffn":
                    f_scale(p)
                stage_end(p, numbers[x])

        @block.scalar
        def _(a):
            a.wait_ge(consts_ready, 1)
            for x in order:
                if x != "L3b":
                    norm_scalar(a, norm_index[x])
                if x in gb:
                    graph_scalar(a, x)
                elif x == "L0_ffn":
                    nibble_scalar(a)
                elif x in ml:
                    moe_scalar(a, x)
                elif x == "L3_ffn":
                    f_scalar(a)
                if x in order[:-1] and x != "L3a":
                    sqrt_ahead(a)
                stage_end(a, numbers[x])

        @block.vector
        def _(v):
            v.wait_ge(consts_ready, 1)
            for c, (t0, w_) in enumerate(GROUPS):
                v.wait_ge(x_loaded[c], 32 if c == NG - 1 else 16)
                for t in range(t0, t0 + w_):
                    row_stats(v, t)
            for x in order:
                if x != "L3b":
                    norm_vector(v, resid, norm_index[x])
                if x == order[0] and moe_layers:
                    split_biases(v)
                if x in gb:
                    graph_vector(v, x)
                elif x == "L0_ffn":
                    nibble_vector(v, rows_at[x])
                elif x in ml:
                    moe_vector(v, x, moe_layers.index(x))
                elif x == "L3_ffn":
                    f_vector(v)
                stage_end(v, numbers[x])

        @block.tensor
        def _(pe):
            pe.wait_ge(consts_ready, 1)
            for x in order:
                if x in gb:
                    graph_tensor(pe, x, rows_at[x])
                elif x == "L0_ffn":
                    nibble_tensor(pe)
                elif x in ml:
                    moe_tensor(pe, x, rows_at[x])
                elif x == "L3_ffn":
                    f_tensor(pe, rows_at[x] + TILES)
                stage_end(pe, numbers[x])


_INPUTS = ("x", "adj", "L0_gnn_W", "L0_gnn_b", "L0_ffn_and_w1", "L0_ffn_and_b1", "L0_ffn_and_w2", "L0_ffn_and_b2",
           "L0_ffn_or_w1", "L0_ffn_or_b1", "L0_ffn_or_w2", "L0_ffn_or_b2", "L0_ffn_xor_w1", "L0_ffn_xor_b1",
           "L0_ffn_xor_w2", "L0_ffn_xor_b2", "L1_gnn_weight", "L1_gnn_bias", "L1_gnn_node_w", "L1_gnn_edge_w",
           "L1_ffn_Wr", "L1_ffn_br", "L1_ffn_W1", "L1_ffn_b1", "L1_ffn_W2", "L1_ffn_b2", "L2_gnn_W", "L2_gnn_a_w",
           "L2_gnn_a_b", "L2_gnn_fc_w", "L2_gnn_fc_b", "L2_ffn_Wg", "L2_ffn_Wgu", "L2_ffn_bgu", "L2_ffn_Wd",
           "L2_ffn_bd", "L3_gnn_W_stack", "L3_ffn_ln_scale", "L3_ffn_ln_bias", "L3_ffn_shared_in_w",
           "L3_ffn_shared_out_w", "L3_ffn_shared_out_b", "L3_ffn_expert_in_w", "L3_ffn_expert_out_weight",
           "L3_ffn_expert_out_bias", "L3_ffn_group_gate_w", "L3_ffn_expert_gate_w", "L3_ffn_group_bias",
           "L3_ffn_expert_bias")


def kernel(**inputs):
    import numpy as np
    import concourse.bacc as bacc
    from concourse.bass_utils import run_bass_kernel_spmd

    nc = bacc.Bacc("TRN2", target_bir_lowering=False, num_devices=1)
    arrays, drams = {}, {}
    for name in _INPUTS:
        a = np.ascontiguousarray(inputs[name])
        if name == "L2_gnn_a_b":
            a = a.reshape(1, 1)
        arrays["in_" + name] = a
        drams[name] = nc.dram_tensor("in_" + name, a.shape, mybir.dt.from_np(a.dtype), kind="ExternalInput").ap()
    result = nc.dram_tensor("result", (N, D), F32, kind="ExternalOutput").ap()
    build(nc, drams, result)
    r = run_bass_kernel_spmd(nc, [arrays], core_ids=[0])
    return r.results[0]["result"]
```
